# Optimizing a Trainium2 kernel written in Bass

```python
import numpy as np
import jax
import jax.numpy as jnp

def _softmax(x, axis=-1):
    return jax.nn.softmax(x, axis=axis)

def _gelu(x):
    return jax.nn.gelu(x, approximate=True)

def _silu(x):
    return jax.nn.silu(x)

def _sigmoid(x):
    return jax.nn.sigmoid(x)

def _layernorm(x, axis=-1, eps=1e-05):
    m = jnp.mean(x, axis=axis, keepdims=True)
    v = jnp.var(x, axis=axis, keepdims=True)
    return (x - m) / jnp.sqrt(v + eps)

def _scatter_add(tgt, idx, src, axis=0):
    return tgt.at[idx].add(src)

def _segment_sum(src, seg, n):
    return jax.ops.segment_sum(src, seg, n)
kernel_name = 'mk_macaron_d2_jaxref_r8_055f7f'

def setup_inputs(seed: int=0):
    np.random.seed(seed)
    _w = jnp.asarray

    def _L0_attn_setup():
        import jax, jax.numpy as jnp
        import numpy as np
        B, N, DIM = (2, 256, 128)
        H = 16
        HD = DIM // H
        key = jax.random.key(seed)
        ks = jax.random.split(key, 4)
        x = jax.random.normal(ks[0], (B, N, DIM), dtype=jnp.float32)
        w_qkv = jax.random.normal(ks[1], (DIM, 3 * DIM), dtype=jnp.float32) / np.sqrt(DIM)
        w_proj = jax.random.normal(ks[2], (DIM, DIM), dtype=jnp.float32) / np.sqrt(DIM)
        b_proj = jax.random.normal(ks[3], (DIM,), dtype=jnp.float32) * 0.01
        return {'x': x, 'w_qkv': w_qkv, 'w_proj': w_proj, 'b_proj': b_proj}
    _L0_attn_in = _L0_attn_setup()

    def _L0_ffn_setup():
        import jax, jax.numpy as jnp
        import numpy as np
        EMB = 128
        HEADS = 16
        SEQ = 256
        LATENT = 64
        N_EXP = 8
        TOP_K = 2
        EXP_DIM = 256
        BATCH = 2
        EPS = 1e-06

        def _rmsnorm(x, g):
            return x * jax.lax.rsqrt(jnp.mean(x * x, axis=-1, keepdims=True) + EPS) * g

        def _mla(h, Wq, Wdkv, Wuk, Wuv, Wo):
            B, S, D = h.shape
            hd = D // HEADS
            q = (h @ Wq).reshape(B, S, HEADS, hd)
            c = h @ Wdkv
            k = (c @ Wuk).reshape(B, S, HEADS, hd)
            v = (c @ Wuv).reshape(B, S, HEADS, hd)
            scores = jnp.einsum('bqhd,bkhd->bhqk', q, k) / jnp.sqrt(jnp.asarray(hd, h.dtype))
            causal = jnp.tril(jnp.ones((S, S), bool))
            scores = jnp.where(causal, scores, jnp.asarray(-1000000000.0, h.dtype))
            a = jax.nn.softmax(scores, axis=-1)
            out = jnp.einsum('bhqk,bkhd->bqhd', a, v).reshape(B, S, D)
            return out @ Wo

        def _moe(h, gate_w, w1, w2):
            B, S, D = h.shape
            t = h.reshape(B * S, D)
            logits = t @ gate_w
            top_v, top_i = jax.lax.top_k(logits, TOP_K)
            gates = jax.nn.softmax(top_v, axis=-1)
            T = t.shape[0]
            combine = jnp.zeros((T, N_EXP), t.dtype).at[jnp.arange(T)[:, None], top_i].add(gates)
            hid = jax.nn.silu(jnp.einsum('td,edh->teh', t, w1))
            ye = jnp.einsum('teh,ehd->ted', hid, w2)
            out = jnp.einsum('te,ted->td', combine, ye)
            return out.reshape(B, S, D)
        key = jax.random.key(seed)
        ks = jax.random.split(key, 12)
        s = 0.02
        return {'x': jax.random.normal(ks[0], (BATCH, SEQ, EMB), jnp.float32), 'g1': jnp.ones((EMB,), jnp.float32), 'Wq': jax.random.normal(ks[1], (EMB, EMB), jnp.float32) * s, 'Wdkv': jax.random.normal(ks[2], (EMB, LATENT), jnp.float32) * s, 'Wuk': jax.random.normal(ks[3], (LATENT, EMB), jnp.float32) * s, 'Wuv': jax.random.normal(ks[4], (LATENT, EMB), jnp.float32) * s, 'Wo': jax.random.normal(ks[5], (EMB, EMB), jnp.float32) * s, 'g2': jnp.ones((EMB,), jnp.float32), 'gate_w': jax.random.normal(ks[6], (EMB, N_EXP), jnp.float32) * s, 'w1': jax.random.normal(ks[7], (N_EXP, EMB, EXP_DIM), jnp.float32) * s, 'w2': jax.random.normal(ks[8], (N_EXP, EXP_DIM, EMB), jnp.float32) * s}
    _L0_ffn_in = _L0_ffn_setup()

    def _L1_attn_setup():
        import jax, jax.numpy as jnp
        import numpy as np
        DEPTH = 4
        DIM = 128
        TOKEN_DIM = 16
        HEADS = 16
        ADIM = TOKEN_DIM * HEADS
        HID = int(DIM * 4.0)
        SCALE = TOKEN_DIM ** (-0.5)
        EPS_LN = 1e-06
        EPS_NRM = 1e-12

        def _l2norm(x, axis):
            n = jnp.sqrt(jnp.sum(x * x, axis=axis, keepdims=True))
            return x / jnp.maximum(n, EPS_NRM)

        def _layernorm(x, g, b):
            mu = jnp.mean(x, axis=-1, keepdims=True)
            var = jnp.mean((x - mu) ** 2, axis=-1, keepdims=True)
            return (x - mu) * jax.lax.rsqrt(var + EPS_LN) * g + b

        def _forward(x, ln1_g, ln1_b, Wq, bq, Wk, bk, w_g, Wp, bp, Wf, bf, ln2_g, ln2_b, W1, b1, W2, b2):
            for i in range(DEPTH):
                h = _layernorm(x, ln1_g[i], ln1_b[i])
                q = h @ Wq[i] + bq[i]
                k = h @ Wk[i] + bk[i]
                q = _l2norm(q, -1)
                k = _l2norm(k, -1)
                A = q @ w_g[i] * SCALE
                A = _l2norm(A, 1)
                G = jnp.sum(A * q, axis=1)
                out = G[:, None, :] * k @ Wp[i] + bp[i] + q
                attn_out = out @ Wf[i] + bf[i]
                x = x + attn_out
                h2 = _layernorm(x, ln2_g[i], ln2_b[i])
                x = x + jax.nn.gelu(h2 @ W1[i] + b1[i], approximate=False) @ W2[i] + b2[i]
            return x
        key = jax.random.key(seed)
        ks = jax.random.split(key, 20)
        s = 0.02
        inp = {'x_in': jax.random.normal(ks[0], (4, 512, DIM), dtype=jnp.float32), 'ln1_g': jnp.ones((DEPTH, DIM), jnp.float32), 'ln1_b': jnp.zeros((DEPTH, DIM), jnp.float32), 'Wq': jax.random.normal(ks[1], (DEPTH, DIM, ADIM), jnp.float32) * s, 'bq': jnp.zeros((DEPTH, ADIM), jnp.float32), 'Wk': jax.random.normal(ks[2], (DEPTH, DIM, ADIM), jnp.float32) * s, 'bk': jnp.zeros((DEPTH, ADIM), jnp.float32), 'w_g': jax.random.normal(ks[3], (DEPTH, ADIM, 1), jnp.float32), 'Wp': jax.random.normal(ks[4], (DEPTH, ADIM, ADIM), jnp.float32) * s, 'bp': jnp.zeros((DEPTH, ADIM), jnp.float32), 'Wf': jax.random.normal(ks[5], (DEPTH, ADIM, DIM), jnp.float32) * s, 'bf': jnp.zeros((DEPTH, DIM), jnp.float32), 'ln2_g': jnp.ones((DEPTH, DIM), jnp.float32), 'ln2_b': jnp.zeros((DEPTH, DIM), jnp.float32), 'W1': jax.random.normal(ks[6], (DEPTH, DIM, HID), jnp.float32) * s, 'b1': jnp.zeros((DEPTH, HID), jnp.float32), 'W2': jax.random.normal(ks[7], (DEPTH, HID, DIM), jnp.float32) * s, 'b2': jnp.zeros((DEPTH, DIM), jnp.float32)}
        return inp
    _L1_attn_in = _L1_attn_setup()

    def _L1_ffn_setup():
        import math
        import jax, jax.numpy as jnp
        import numpy as np
        E = 8
        H = 128
        HP = 128
        SPARSITY = 8
        N_ROTATE = 64
        ROPE_BASE = 10000.0

        def _rope(x, pos):
            half = N_ROTATE // 2
            inv_freq = 1.0 / ROPE_BASE ** (jnp.arange(half, dtype=jnp.float32) * 2.0 / N_ROTATE)
            ang = pos.astype(jnp.float32)[..., None] * inv_freq
            sin, cos = (jnp.sin(ang), jnp.cos(ang))
            x1, x2 = (x[..., :half], x[..., half:])
            return jnp.concatenate([x1 * cos - x2 * sin, x2 * cos + x1 * sin], axis=-1)
        key = jax.random.key(seed)
        k1, k2, k3, k4 = jax.random.split(key, 4)
        B, T = (4, 1024)
        X = jax.random.normal(k1, (B, T, H), dtype=jnp.float32)
        Wr = jax.random.uniform(k2, (E, H), minval=-1 / math.sqrt(H), maxval=1 / math.sqrt(H), dtype=jnp.float32)
        bq = 1 / math.sqrt(3 * HP)
        Wqkv = jax.random.uniform(k3, (E, H, 3 * HP), minval=-bq, maxval=bq, dtype=jnp.float32)
        bo = 1 / math.sqrt(H * E)
        Wo = jax.random.uniform(k4, (E, HP, H), minval=-bo, maxval=bo, dtype=jnp.float32)
        return {'X': X, 'Wr': Wr, 'Wqkv': Wqkv, 'Wo': Wo}
    _L1_ffn_in = _L1_ffn_setup()
    _d = {'L0_attn_x': _L0_attn_in['x'], 'L0_attn_w_qkv': _L0_attn_in['w_qkv'], 'L0_attn_w_proj': _L0_attn_in['w_proj'], 'L0_attn_b_proj': _L0_attn_in['b_proj'], 'L0_ffn_g1': _L0_ffn_in['g1'], 'L0_ffn_Wq': _L0_ffn_in['Wq'], 'L0_ffn_Wdkv': _L0_ffn_in['Wdkv'], 'L0_ffn_Wuk': _L0_ffn_in['Wuk'], 'L0_ffn_Wuv': _L0_ffn_in['Wuv'], 'L0_ffn_Wo': _L0_ffn_in['Wo'], 'L0_ffn_g2': _L0_ffn_in['g2'], 'L0_ffn_gate_w': _L0_ffn_in['gate_w'], 'L0_ffn_w1': _L0_ffn_in['w1'], 'L0_ffn_w2': _L0_ffn_in['w2'], 'L1_attn_ln1_g': _L1_attn_in['ln1_g'], 'L1_attn_ln1_b': _L1_attn_in['ln1_b'], 'L1_attn_Wq': _L1_attn_in['Wq'], 'L1_attn_bq': _L1_attn_in['bq'], 'L1_attn_Wk': _L1_attn_in['Wk'], 'L1_attn_bk': _L1_attn_in['bk'], 'L1_attn_w_g': _L1_attn_in['w_g'], 'L1_attn_Wp': _L1_attn_in['Wp'], 'L1_attn_bp': _L1_attn_in['bp'], 'L1_attn_Wf': _L1_attn_in['Wf'], 'L1_attn_bf': _L1_attn_in['bf'], 'L1_attn_ln2_g': _L1_attn_in['ln2_g'], 'L1_attn_ln2_b': _L1_attn_in['ln2_b'], 'L1_attn_W1': _L1_attn_in['W1'], 'L1_attn_b1': _L1_attn_in['b1'], 'L1_attn_W2': _L1_attn_in['W2'], 'L1_attn_b2': _L1_attn_in['b2'], 'L1_ffn_Wr': _L1_ffn_in['Wr'], 'L1_ffn_Wqkv': _L1_ffn_in['Wqkv'], 'L1_ffn_Wo': _L1_ffn_in['Wo']}
    _x0 = _d['L0_attn_x']
    _d['L0_attn_x'] = jax.random.normal(jax.random.fold_in(jax.random.key(seed), 1), (4, 512, 128), dtype=_x0.dtype)
    del _x0
    return _d

def reference(L0_attn_x, L0_attn_w_qkv, L0_attn_w_proj, L0_attn_b_proj, L0_ffn_g1, L0_ffn_Wq, L0_ffn_Wdkv, L0_ffn_Wuk, L0_ffn_Wuv, L0_ffn_Wo, L0_ffn_g2, L0_ffn_gate_w, L0_ffn_w1, L0_ffn_w2, L1_attn_ln1_g, L1_attn_ln1_b, L1_attn_Wq, L1_attn_bq, L1_attn_Wk, L1_attn_bk, L1_attn_w_g, L1_attn_Wp, L1_attn_bp, L1_attn_Wf, L1_attn_bf, L1_attn_ln2_g, L1_attn_ln2_b, L1_attn_W1, L1_attn_b1, L1_attn_W2, L1_attn_b2, L1_ffn_Wr, L1_ffn_Wqkv, L1_ffn_Wo):

    def _L0_attn_ref(x, w_qkv, w_proj, b_proj):
        import jax, jax.numpy as jnp
        import numpy as np
        B, N, DIM = (2, 256, 128)
        H = 16
        HD = DIM // H
        b, n, c = x.shape
        scale = HD ** (-0.5)
        qkv = jnp.einsum('bnc,cd->bnd', x, w_qkv)
        qkv = qkv.reshape(b, n, 3, H, HD).transpose(2, 0, 3, 1, 4)
        q, k, v = (qkv[0], qkv[1], qkv[2])
        q = q * scale
        attn = jnp.einsum('bhnd,bhmd->bhnm', q, k)
        attn = jax.nn.softmax(attn, axis=-1)
        out = jnp.einsum('bhnm,bhmd->bhnd', attn, v)
        out = out.transpose(0, 2, 1, 3).reshape(b, n, c)
        return jnp.einsum('bnc,cd->bnd', out, w_proj) + b_proj

    def _L0_ffn_ref(x, g1, Wq, Wdkv, Wuk, Wuv, Wo, g2, gate_w, w1, w2):
        import jax, jax.numpy as jnp
        import numpy as np
        EMB = 128
        HEADS = 16
        SEQ = 256
        LATENT = 64
        N_EXP = 8
        TOP_K = 2
        EXP_DIM = 256
        BATCH = 2
        EPS = 1e-06

        def _rmsnorm(x, g):
            return x * jax.lax.rsqrt(jnp.mean(x * x, axis=-1, keepdims=True) + EPS) * g

        def _mla(h, Wq, Wdkv, Wuk, Wuv, Wo):
            B, S, D = h.shape
            hd = D // HEADS
            q = (h @ Wq).reshape(B, S, HEADS, hd)
            c = h @ Wdkv
            k = (c @ Wuk).reshape(B, S, HEADS, hd)
            v = (c @ Wuv).reshape(B, S, HEADS, hd)
            scores = jnp.einsum('bqhd,bkhd->bhqk', q, k) / jnp.sqrt(jnp.asarray(hd, h.dtype))
            causal = jnp.tril(jnp.ones((S, S), bool))
            scores = jnp.where(causal, scores, jnp.asarray(-1000000000.0, h.dtype))
            a = jax.nn.softmax(scores, axis=-1)
            out = jnp.einsum('bhqk,bkhd->bqhd', a, v).reshape(B, S, D)
            return out @ Wo

        def _moe(h, gate_w, w1, w2):
            B, S, D = h.shape
            t = h.reshape(B * S, D)
            logits = t @ gate_w
            top_v, top_i = jax.lax.top_k(logits, TOP_K)
            gates = jax.nn.softmax(top_v, axis=-1)
            T = t.shape[0]
            combine = jnp.zeros((T, N_EXP), t.dtype).at[jnp.arange(T)[:, None], top_i].add(gates)
            hid = jax.nn.silu(jnp.einsum('td,edh->teh', t, w1))
            ye = jnp.einsum('teh,ehd->ted', hid, w2)
            out = jnp.einsum('te,ted->td', combine, ye)
            return out.reshape(B, S, D)
        x = x + _mla(_rmsnorm(x, g1), Wq, Wdkv, Wuk, Wuv, Wo)
        x = x + _moe(_rmsnorm(x, g2), gate_w, w1, w2)
        return x

    def _L1_attn_ref(x_in, ln1_g, ln1_b, Wq, bq, Wk, bk, w_g, Wp, bp, Wf, bf, ln2_g, ln2_b, W1, b1, W2, b2):
        import jax, jax.numpy as jnp
        import numpy as np
        DEPTH = 4
        DIM = 128
        TOKEN_DIM = 16
        HEADS = 16
        ADIM = TOKEN_DIM * HEADS
        HID = int(DIM * 4.0)
        SCALE = TOKEN_DIM ** (-0.5)
        EPS_LN = 1e-06
        EPS_NRM = 1e-12

        def _l2norm(x, axis):
            n = jnp.sqrt(jnp.sum(x * x, axis=axis, keepdims=True))
            return x / jnp.maximum(n, EPS_NRM)

        def _layernorm(x, g, b):
            mu = jnp.mean(x, axis=-1, keepdims=True)
            var = jnp.mean((x - mu) ** 2, axis=-1, keepdims=True)
            return (x - mu) * jax.lax.rsqrt(var + EPS_LN) * g + b

        def _forward(x, ln1_g, ln1_b, Wq, bq, Wk, bk, w_g, Wp, bp, Wf, bf, ln2_g, ln2_b, W1, b1, W2, b2):
            for i in range(DEPTH):
                h = _layernorm(x, ln1_g[i], ln1_b[i])
                q = h @ Wq[i] + bq[i]
                k = h @ Wk[i] + bk[i]
                q = _l2norm(q, -1)
                k = _l2norm(k, -1)
                A = q @ w_g[i] * SCALE
                A = _l2norm(A, 1)
                G = jnp.sum(A * q, axis=1)
                out = G[:, None, :] * k @ Wp[i] + bp[i] + q
                attn_out = out @ Wf[i] + bf[i]
                x = x + attn_out
                h2 = _layernorm(x, ln2_g[i], ln2_b[i])
                x = x + jax.nn.gelu(h2 @ W1[i] + b1[i], approximate=False) @ W2[i] + b2[i]
            return x
        return _forward(x_in, ln1_g, ln1_b, Wq, bq, Wk, bk, w_g, Wp, bp, Wf, bf, ln2_g, ln2_b, W1, b1, W2, b2)

    def _L1_ffn_ref(X, Wr, Wqkv, Wo):
        import math
        import jax, jax.numpy as jnp
        import numpy as np
        E = 8
        H = 128
        HP = 128
        SPARSITY = 8
        N_ROTATE = 64
        ROPE_BASE = 10000.0

        def _rope(x, pos):
            half = N_ROTATE // 2
            inv_freq = 1.0 / ROPE_BASE ** (jnp.arange(half, dtype=jnp.float32) * 2.0 / N_ROTATE)
            ang = pos.astype(jnp.float32)[..., None] * inv_freq
            sin, cos = (jnp.sin(ang), jnp.cos(ang))
            x1, x2 = (x[..., :half], x[..., half:])
            return jnp.concatenate([x1 * cos - x2 * sin, x2 * cos + x1 * sin], axis=-1)
        B, T, _ = X.shape
        k = min(max(T // SPARSITY, 2), T)
        logits = jax.nn.sigmoid(jnp.einsum('bth,eh->bte', X, Wr))
        topk_vals, topk_I = jax.lax.top_k(logits.transpose(0, 2, 1), k)
        idx_flat = topk_I.reshape(B, E * k)
        Xg = jnp.take_along_axis(X, idx_flat[:, :, None], axis=1).reshape(B, E, k, H)
        QKV = jnp.einsum('beki,eij->bekj', Xg, Wqkv)
        Q, K, V = jnp.split(QKV, 3, axis=-1)
        Q = jnp.concatenate([_rope(Q[..., :N_ROTATE], topk_I), Q[..., N_ROTATE:]], axis=-1)
        K = jnp.concatenate([_rope(K[..., :N_ROTATE], topk_I), K[..., N_ROTATE:]], axis=-1)
        M = topk_I[..., :, None] >= topk_I[..., None, :]
        scores = jnp.einsum('bekd,bemd->bekm', Q, K) / math.sqrt(HP)
        scores = jnp.where(M, scores, -jnp.inf)
        A = jax.nn.softmax(scores, axis=-1)
        AV = jnp.einsum('bekm,bemd->bekd', A, V)
        AV = AV * topk_vals[..., None]
        Xpre = jnp.einsum('bekj,eji->beki', AV, Wo)
        out = jnp.zeros((B, T, H), dtype=X.dtype)
        out = out.at[jnp.arange(B)[:, None], idx_flat].add(Xpre.reshape(B, E * k, H))
        return out
    x = L0_attn_x
    x = x + 0.5 * _L0_ffn_ref(_layernorm(x, axis=-1), L0_ffn_g1, L0_ffn_Wq, L0_ffn_Wdkv, L0_ffn_Wuk, L0_ffn_Wuv, L0_ffn_Wo, L0_ffn_g2, L0_ffn_gate_w, L0_ffn_w1, L0_ffn_w2)
    x = x + _L0_attn_ref(_layernorm(x, axis=-1), L0_attn_w_qkv, L0_attn_w_proj, L0_attn_b_proj)
    x = x + 0.5 * _L0_ffn_ref(_layernorm(x, axis=-1), L0_ffn_g1, L0_ffn_Wq, L0_ffn_Wdkv, L0_ffn_Wuk, L0_ffn_Wuv, L0_ffn_Wo, L0_ffn_g2, L0_ffn_gate_w, L0_ffn_w1, L0_ffn_w2)
    x = x + 0.5 * _L1_ffn_ref(_layernorm(x, axis=-1), L1_ffn_Wr, L1_ffn_Wqkv, L1_ffn_Wo)
    x = x + _L1_attn_ref(_layernorm(x, axis=-1), L1_attn_ln1_g, L1_attn_ln1_b, L1_attn_Wq, L1_attn_bq, L1_attn_Wk, L1_attn_bk, L1_attn_w_g, L1_attn_Wp, L1_attn_bp, L1_attn_Wf, L1_attn_bf, L1_attn_ln2_g, L1_attn_ln2_b, L1_attn_W1, L1_attn_b1, L1_attn_W2, L1_attn_b2)
    x = x + 0.5 * _L1_ffn_ref(_layernorm(x, axis=-1), L1_ffn_Wr, L1_ffn_Wqkv, L1_ffn_Wo)
    return x

_drawn_inputs = setup_inputs


def setup_inputs(seed=0):
    import zlib

    import numpy as np

    out = dict(_drawn_inputs(seed))
    spreads = {'L0_ffn_g1': (1.0, 0.6),
     'L0_ffn_g2': (1.0, 0.6),
     'L1_attn_ln1_g': (1.0, 0.6),
     'L1_attn_ln1_b': (0.0, 0.8),
     'L1_attn_bq': (0.0, 0.8),
     'L1_attn_bk': (0.0, 0.8),
     'L1_attn_bp': (0.0, 0.373),
     'L1_attn_bf': (0.0, 0.1),
     'L1_attn_ln2_g': (1.0, 0.6),
     'L1_attn_ln2_b': (0.0, 0.8),
     'L1_attn_b1': (0.0, 0.54),
     'L1_attn_b2': (0.0, 0.1)}
    factors = {'L0_attn_b_proj': 8.0,
     'L0_ffn_Wq': 8.0,
     'L0_ffn_Wdkv': 8.0,
     'L0_ffn_Wuk': 8.0,
     'L0_ffn_Wuv': 8.0,
     'L0_ffn_Wo': 8.0,
     'L0_ffn_gate_w': 4.16,
     'L0_ffn_w1': 3.659,
     'L0_ffn_w2': 3.641,
     'L1_attn_Wq': 4.604,
     'L1_attn_Wk': 8.0,
     'L1_attn_w_g': 8.0,
     'L1_attn_Wp': 8.0,
     'L1_ffn_Wr': 8.0,
     'L1_ffn_Wqkv': 8.0,
     'L1_ffn_Wo': 8.0}
    for name, (base, spread) in spreads.items():
        noise = np.random.default_rng([zlib.crc32(name.encode()), seed]).standard_normal(out[name].shape)
        drawn = base * np.exp(spread * noise) if base else spread * noise
        out[name] = jnp.asarray(drawn.astype(out[name].dtype))
    for name, factor in factors.items():
        out[name] = (out[name] * factor).astype(out[name].dtype)
    return out
```

```python
from contextlib import ExitStack

import numpy as np

import concourse.bass as bass
from concourse import mybir

P = 128
B = 4
N = 512
D = 128
NT = N // P
TILES = B * NT
H = 16
HD = D // H
QUADS = H // 4
SLOT = 64
EXPERTS = 8
EXP_DIM = 256
DEPTH = 4
ADIM = 256
HID = 512
MEXP = 8
MK = 64
ROT = 64
NEG = -1.0e30

ALU = mybir.AluOpType
ACT = mybir.ActivationFunctionType
F32 = mybir.dt.float32
BF16 = mybir.dt.bfloat16
I32 = mybir.dt.int32
AX = mybir.AxisListType


class Signal:

    def __init__(self, sem, per):
        self.sem, self.per = sem, per

    def __call__(self, b, k):
        return b * self.per + k


class Chain:

    def __init__(self, eng, sem, per):
        self.eng, self.sem, self.per, self.n, self.b = eng, sem, per, 0, 0

    def start(self, b):
        self.b, self.n = b, 0

    def __call__(self, ins):
        ins.then_inc(self.sem, 1)
        self.n += 1

    def wait(self):
        self.eng.wait_ge(self.sem, self.b * self.per + self.n)

    def wait_apart(self, go):
        self.wait()
        self.eng.sem_inc(go, 1)

    def end(self):
        assert self.n == self.per, (self.sem.name, self.n)


def take_semaphore(nc, ctx, name):
    handle = nc.alloc_semaphore(name)
    ctx.callback(lambda: nc.clear_and_free_semaphores([handle]))
    return handle


def end_module(nc):
    nc.all_engine_barrier()


class Kernel:
    pass


def open_buffers(nc, ctx, k):
    def sb(name, shape, dt=F32):
        return ctx.enter_context(nc.sbuf_tensor(name, shape, dt))

    k.x = sb("x", [P, TILES, D])
    k.y = sb("y", [P, TILES, D])
    k.ident = sb("ident", [P, P])
    k.identb = sb("identb", [P, P], BF16)
    k.mask_qk = sb("mask_qk", [P, P], BF16)
    k.mask_kq = sb("mask_kq", [P, P], BF16)
    k.half = sb("half", [P, TILES])
    k.w_mla = sb("w_mla", [P, 3 * D])
    k.w_mla_out = sb("w_mla_out", [P, D])
    k.w_att = sb("w_att", [P, 3 * D])
    k.w_att_out = sb("w_att_out", [P, D])
    k.b_att = sb("b_att", [P, D])
    k.bank = [ctx.enter_context(nc.psum_tensor(f"bank{i}", [P, 512], F32)) for i in range(8)]


def setup(nc, k, a):
    with ExitStack() as ctx:
        ctx.callback(end_module, nc)

        def sb(name, shape, dt=F32):
            return ctx.enter_context(nc.sbuf_tensor(name, shape, dt))

        def sem(name):
            return take_semaphore(nc, ctx, name)

        wdkv = sb("wdkv", [P, 64])
        wukv = sb("wukv", [64, 2 * D])
        wdkvT = sb("wdkvT", [64, P])
        g1 = sb("g1", [P, 1])
        loaded, weights, consts, ident_ok, step, ps, evac, done = (
            sem(n) for n in ("x_loaded", "weights_loaded", "consts_made", "ident_made", "setup_step",
                             "fold_ps", "fold_sb", "fold_done"))
        with nc.Block() as block:
            @block.sync
            def _(sp):
                sp.dma_start(wdkv[:, :], a["L0_ffn_Wdkv"]).then_inc(weights, 16)
                sp.dma_start(wukv[:, 0:D], a["L0_ffn_Wuk"]).then_inc(weights, 16)
                sp.dma_start(wukv[:, D:2 * D], a["L0_ffn_Wuv"]).then_inc(weights, 16)
                sp.dma_start(g1[:, :], a["L0_ffn_g1"].rearrange("(p o) -> p o", o=1)).then_inc(weights, 16)
                sp.dma_start(k.w_mla[:, 0:D], a["L0_ffn_Wq"]).then_inc(weights, 16)
                sp.dma_start(k.w_mla_out[:, :], a["L0_ffn_Wo"]).then_inc(weights, 16)
                sp.dma_start(k.w_att[:, :], a["L0_attn_w_qkv"]).then_inc(weights, 16)
                sp.dma_start(k.w_att_out[:, :], a["L0_attn_w_proj"]).then_inc(weights, 16)
                sp.dma_start(k.b_att[:, :], a["L0_attn_b_proj"].partition_broadcast(P)).then_inc(weights, 16)
                sp.wait_ge(loaded, 16)
                sp.wait_ge(weights, 16 * 9)

            @block.scalar
            def _(act):
                act.dma_start(k.x[:, :, :], a["L0_attn_x"].rearrange("b (t p) d -> p (b t) d", p=P)).then_inc(loaded, 16)

            @block.gpsimd
            def _(pool):
                pool.memset(k.ident[:, :], 0.0).then_inc(consts, 1)
                pool.memset(k.mask_qk[:, :], 0.0).then_inc(consts, 1)
                pool.memset(k.mask_kq[:, :], 0.0).then_inc(consts, 1)
                pool.memset(k.half[:, :], -0.5).then_inc(consts, 1)
                pool.wait_ge(consts, 4)
                pool.affine_select(out=k.ident[:, :], in_=k.ident[:, :], compare_op=ALU.not_equal, fill=1.0,
                                   base=0, pattern=[[-1, P]], channel_multiplier=1).then_inc(ident_ok, 1)
                pool.affine_select(out=k.mask_qk[:, :], in_=k.mask_qk[:, :], compare_op=ALU.is_ge, fill=NEG,
                                   base=0, pattern=[[-1, P]], channel_multiplier=1).then_inc(ident_ok, 1)
                pool.affine_select(out=k.mask_kq[:, :], in_=k.mask_kq[:, :], compare_op=ALU.is_ge, fill=NEG,
                                   base=0, pattern=[[1, P]], channel_multiplier=-1).then_inc(ident_ok, 1)
                pool.wait_ge(ident_ok, 3)
                pool.tensor_copy(k.identb[:, :], k.ident[:, :]).then_inc(consts, 1)

            @block.tensor
            def _(pe):
                pe.wait_ge(ident_ok, 3)
                pe.wait_ge(weights, 16 * 9)
                pe.transpose(k.bank[0][0:64, 0:P], wdkv[:, :], k.ident[:, :]).then_inc(ps, 1)
                pe.wait_ge(evac, 1)
                pe.matmul(k.bank[1][:, 0:2 * D], wdkvT[:, :], wukv[:, :], start=True, stop=True).then_inc(ps, 1)

            @block.vector
            def _(dve):
                dve.wait_ge(ps, 1)
                dve.tensor_copy(wdkvT[:, :], k.bank[0][0:64, 0:P]).then_inc(evac, 1)
                dve.wait_ge(weights, 16 * 9)
                dve.tensor_scalar(k.w_mla[:, 0:D], k.w_mla[:, 0:D], g1[:, 0:1], HD ** -0.5,
                                  ALU.mult, ALU.mult).then_inc(done, 1)
                dve.tensor_scalar(k.w_att[:, 0:D], k.w_att[:, 0:D], HD ** -0.5, None, ALU.mult).then_inc(done, 1)
                dve.wait_ge(ps, 2)
                dve.tensor_scalar(k.w_mla[:, D:3 * D], k.bank[1][:, 0:2 * D], g1[:, 0:1], None,
                                  ALU.mult).then_inc(done, 1)


def attention(nc, k, name, causal):
    with ExitStack() as ctx:
        ctx.callback(end_module, nc)

        def sb(n, shape, dt=F32):
            return ctx.enter_context(nc.sbuf_tensor(f"{name}_{n}", shape, dt))

        def sem(n):
            return take_semaphore(nc, ctx, f"{name}_{n}")

        def signal(n, per):
            return Signal(sem(n), per)

        w_in, w_out = (k.w_mla, k.w_mla_out) if causal else (k.w_att, k.w_att_out)
        eps = 1e-5
        stats = sb("stats", [P, TILES, 6])
        mv = sb("mv", [P, TILES, 2])
        var = sb("var", [P, TILES])
        rstd = sb("rstd", [P, TILES])
        ms = sb("ms", [P, TILES])
        rms = sb("rms", [P, TILES])
        hscale = sb("hscale", [P, TILES])
        h = sb("h", [P, NT, D])
        hT = sb("hT", [P, N])
        qk32 = sb("qk32", [P, NT, 2, D])
        rest = sb("rest", [P, NT, 2, D])
        hi = sb("hi", [P, NT, 2, D], BF16)
        mid = sb("mid", [P, NT, 2, D], BF16)
        lo = sb("lo", [P, NT, 2, D], BF16)
        q_parts = sb("q_parts", [P, NT, H, SLOT], BF16)
        k_parts = sb("k_parts", [P, NT, H, SLOT], BF16)
        v_ones = sb("v_ones", [P, NT, H, 32])
        qT_max = sb("qT_max", [P, 2, N], BF16)
        qT = sb("qT", [P, 2, 2, N], BF16)
        kT = sb("kT", [P, 2, 4, N], BF16)
        negmax = sb("negmax", [P, H, NT])
        nm_rest = sb("nm_rest", [P, H, NT])
        nm_hi = sb("nm_hi", [P, H, NT], BF16)
        nm_mid = sb("nm_mid", [P, H, NT], BF16)
        probs = sb("probs", [P, 2, 4, NT * N])
        oT = sb("oT", [P, 2, N])
        rsum = sb("rsum", [P, 2, NT, 4])
        o = sb("o", [P, NT, D])
        oTn = sb("oTn", [P, N])

        bank = k.bank
        T = bank[0]
        TQ = bank[0][:, 0:256].bitcast(BF16)
        TK = bank[0][:, 256:512].bitcast(BF16)
        S1 = [bank[1], bank[2]]
        AV = bank[3]

        if causal:
            at = {0: 0, 1: 512, 3: 896, 2: 1024}
            rounds = [[(j, 0, 0, 0), (j, 1, 1, 0), (j, 3, 1, 384)] for j in range(4)]
            rounds.append([(j, 2, j // 2, 256 * (j % 2)) for j in range(4)])
        else:
            at = {kt: 512 * kt for kt in range(NT)}
            rounds = [[(j, 2 * r, 0, 0), (j, 2 * r + 1, 1, 0)] for j in range(4) for r in range(2)]
        R = len(rounds)
        PAIRS = H // 2

        def q_from(kt):
            return P * kt if causal else 0

        def keys(t):
            return P * (t + 1) if causal else N

        s_zero = sem("zeroed")
        s_pool_go = sem("pool_go")
        s_init, s_stat, s_ms, s_scale = sem("init"), sem("stat"), sem("rstd_step"), sem("rstd_done")
        h_ready = signal("h_ready", 1)
        hT_ps = signal("hT_ps", 1)
        hT_sb = signal("hT_sb", 1)
        qkv_ps = signal("qkv_ps", NT)
        qk_sb = signal("qk_sb", NT)
        v_sb = signal("v_sb", NT)
        rest_sb = signal("rest_sb", 2)
        parts_dve = signal("parts_dve", 2)
        parts_pool = signal("parts_pool", 2)
        mid_sb = signal("mid_sb", 1)
        turned_max = signal("turned_max", PAIRS)
        q_max_sb = signal("q_max_sb", PAIRS)
        k_sb = signal("k_sb", PAIRS)
        max_ps = signal("max_ps", PAIRS * 2 * NT)
        max_read = signal("max_read", PAIRS * 2 * NT)
        max_rows = signal("max_rows", PAIRS)
        turned_q = signal("turned_q", PAIRS)
        q_sb = signal("q_sb", PAIRS)
        score_ps = signal("score_ps", QUADS * R)
        probs_sb = signal("probs_sb", QUADS * R)
        av_ps = signal("av_ps", QUADS)
        av_sb = signal("av_sb", QUADS)
        turned_o = signal("turned_o", QUADS)
        o_sb = signal("o_sb", QUADS)
        oT_ps = signal("oT_ps", 1)
        oT_sb = signal("oT_sb", 1)
        proj_ps = signal("proj_ps", 1)
        out_sb = signal("out_sb", 1)

        def fronts(g):
            for p in (2 * g, 2 * g + 1):
                yield ("turn_max", p)
                for t in range(NT):
                    yield ("max", p, t)
                yield ("max_rows", p)

        order = [("h",), ("qkv",), ("parts",)] + list(fronts(0))
        for g in range(QUADS):
            ahead = list(fronts(g + 1)) if g + 1 < QUADS else []
            if g > 0:
                ahead[0:0] = [("av", g - 1)]
                ahead[4:4] = [("o", g - 1)]
            for r in range(R):
                order.append(("score", g, r))
                take = -(-len(ahead) // (R - r))
                order += ahead[:take]
                ahead = ahead[take:]
        order += [("av", QUADS - 1), ("o", QUADS - 1), ("proj",)]
        t_uses = [s for s in order if s[0] in ("h", "turn_max", "max_rows", "o", "proj")]

        def wait_t_free(eng, b, s):
            i = t_uses.index(s)
            if i == 0:
                return
            u = t_uses[i - 1]
            if u[0] == "h":
                eng.wait_ge(hT_sb.sem, hT_sb(b, 1))
            elif u[0] == "turn_max":
                eng.wait_ge(q_max_sb.sem, q_max_sb(b, u[1] + 1))
                eng.wait_ge(k_sb.sem, k_sb(b, u[1] + 1))
            elif u[0] == "max_rows":
                eng.wait_ge(q_sb.sem, q_sb(b, u[1] + 1))
            elif u[0] == "o":
                eng.wait_ge(o_sb.sem, o_sb(b, u[1] + 1))

        with nc.Block() as block:
            @block.sync
            def _(sp):
                sp.nop()

            @block.gpsimd
            def _(pool):
                pool.memset(q_parts[:, :, :, :], 0.0).then_inc(s_init, 1)
                pool.memset(k_parts[:, :, :, :], 0.0).then_inc(s_init, 1)
                pool.memset(v_ones[:, :, :, :], 0.0).then_inc(s_init, 1)
                pool.wait_ge(s_init, 3)
                pool.memset(k_parts[:, :, :, 48:51], 1.0).then_inc(s_init, 1)
                pool.memset(v_ones[:, :, :, HD:HD + 1], 1.0).then_inc(s_init, 1)
                n = 0

                def step(ins):
                    nonlocal n
                    ins.then_inc(s_ms, 1)
                    n += 1
                    pool.wait_ge(s_ms, n)

                pool.wait_ge(s_stat, 1)
                step(pool.tensor_scalar(var[:, :], mv[:, :, 1], eps, None, ALU.add))
                step(pool.tensor_tensor(rstd[:, :], var[:, :], k.half[:, :], ALU.pow))
                if causal:
                    step(pool.tensor_tensor(ms[:, :], rstd[:, :], rstd[:, :], ALU.mult))
                    step(pool.tensor_tensor(ms[:, :], ms[:, :], mv[:, :, 1], ALU.mult))
                    step(pool.tensor_scalar(ms[:, :], ms[:, :], 1e-6, None, ALU.add))
                    step(pool.tensor_tensor(rms[:, :], ms[:, :], k.half[:, :], ALU.pow))
                    pool.tensor_tensor(hscale[:, :], rms[:, :], rstd[:, :], ALU.mult).then_inc(s_scale, 1)
                else:
                    pool.tensor_copy(hscale[:, :], rstd[:, :]).then_inc(s_scale, 1)
                with pool.Fori(0, B) as b:
                    pool.wait_ge(rest_sb.sem, rest_sb(b, 1))
                    pool.sem_inc(s_pool_go, 1)
                    pool.tensor_copy(mid[:, :, :, :], rest[:, :, :, :]).then_inc(mid_sb.sem, 1)
                    pool.wait_ge(mid_sb.sem, mid_sb(b, 1))
                    pool.sem_inc(s_pool_go, 1)
                    for s in (3, 4):
                        ins = pool.tensor_copy(q_parts[:, :, :, 8 * s:8 * s + 8],
                                               mid[:, :, 0, :].rearrange("p t (h e) -> p t h e", e=HD))
                    ins.then_inc(parts_pool.sem, 1)
                    for s in (1, 4):
                        ins = pool.tensor_copy(k_parts[:, :, :, 8 * s:8 * s + 8],
                                               mid[:, :, 1, :].rearrange("p t (h e) -> p t h e", e=HD))
                    ins.then_inc(parts_pool.sem, 1)

            @block.scalar
            def _(act):
                act.wait_ge(s_init, 5)
                act.wait_ge(s_zero, 1)
                with act.Fori(0, B) as b:
                    def h_step():
                        act.wait_ge(hT_ps.sem, hT_ps(b, 1))
                        act.copy(hT[:, :], T[:, :]).then_inc(hT_sb.sem, 1)

                    def qkv_step():
                        for t in range(NT):
                            act.wait_ge(qkv_ps.sem, qkv_ps(b, t + 1))
                            act.copy(qk32[:, t, :, :].rearrange("p s d -> p (s d)"),
                                     bank[4 + t][:, 0:2 * D]).then_inc(qk_sb.sem, 1)
                        for t in range(NT):
                            act.copy(v_ones[:, t, :, 0:HD],
                                     bank[4 + t][:, 2 * D:3 * D].rearrange("p (h e) -> p h e", e=HD)).then_inc(v_sb.sem, 1)

                    def turn_max_step(p):
                        g, i = p // 2, 2 * (p % 2)
                        act.wait_ge(q_max_sb.sem, q_max_sb(b, p + 1))
                        if g >= 2:
                            act.wait_ge(score_ps.sem, score_ps(b, R * (g - 1)))
                        act.copy(kT[0:64, g % 2, i, :], TK[0:64, :])
                        act.copy(kT[64:128, g % 2, i + 1, :], TK[64:128, :]).then_inc(k_sb.sem, 1)

                    def score_step(g, r):
                        n = R * g + r
                        act.wait_ge(score_ps.sem, score_ps(b, n + 1))
                        if g >= 2 and r == 0:
                            act.wait_ge(av_ps.sem, av_ps(b, g - 1))
                        pair = 4 + 2 * (n % 2)
                        if causal and r == R - 1:
                            for i in range(2):
                                ins = act.activation(probs[:, g % 2, 2 * i:2 * i + 2, at[2]:at[2] + 256],
                                                     bank[pair + i][:, :].rearrange("p (j q) -> p j q", j=2), ACT.Exp)
                            ins.then_inc(probs_sb.sem, 1)
                        else:
                            j, kt = rounds[r][0][:2]
                            for i in range(2):
                                ins = act.activation(probs[:, g % 2, j, at[kt] + 512 * i:at[kt] + 512 * i + 512],
                                                     bank[pair + i][:, :], ACT.Exp)
                            ins.then_inc(probs_sb.sem, 1)

                    def av_step(g):
                        act.wait_ge(av_ps.sem, av_ps(b, g + 1))
                        act.copy(oT[:, g % 2, :], AV[:, :]).then_inc(av_sb.sem, 1)

                    def proj_step():
                        act.wait_ge(oT_ps.sem, oT_ps(b, 1))
                        act.copy(oTn[:, :], T[:, :]).then_inc(oT_sb.sem, 1)

                    does = {"h": h_step, "qkv": qkv_step, "turn_max": turn_max_step, "score": score_step,
                            "av": av_step, "proj": proj_step}
                    for s in order:
                        if s[0] in does:
                            does[s[0]](*s[1:])

            @block.vector
            def _(dve):
                own = Chain(dve, sem("dve_step"), NT + 3 * PAIRS + QUADS)
                dve.memset(kT[:, :, :, :], 0.0).then_inc(s_zero, 1)
                for t in range(TILES):
                    dve.bn_stats(stats[:, t, :], k.x[:, t, :]).then_inc(own.sem, 1)
                dve.wait_ge(own.sem, TILES)
                for t in range(TILES):
                    ins = dve.bn_aggr(mv[:, t, :], stats[:, t, :])
                ins.then_inc(s_stat, 1)
                dve.wait_ge(s_init, 5)
                dve.wait_ge(s_scale, 1)
                dve.sem_clear(own.sem)
                with dve.Fori(0, B) as b:
                    own.start(b)

                    def h_step():
                        for t in range(NT):
                            tok = k.x[:, b * NT + t, :]
                            if causal:
                                dve.tensor_scalar(k.y[:, b * NT + t, :], tok, mv[:, b * NT + t, 0:1],
                                                  rstd[:, bass.ds(b * NT + t, 1)], ALU.subtract, ALU.mult)
                            ins = dve.tensor_scalar(h[:, t, :], tok, mv[:, b * NT + t, 0:1],
                                                    hscale[:, bass.ds(b * NT + t, 1)], ALU.subtract, ALU.mult)
                        ins.then_inc(h_ready.sem, 1)

                    def parts_step():
                        for t in range(NT):
                            dve.wait_ge(qk_sb.sem, qk_sb(b, t + 1))
                            own(dve.tensor_copy(hi[:, t, :, :], qk32[:, t, :, :]))
                        own.wait()
                        dve.tensor_tensor(rest[:, :, :, :], qk32[:, :, :, :], hi[:, :, :, :],
                                          ALU.subtract).then_inc(rest_sb.sem, 1)
                        qhi = hi[:, :, 0, :].rearrange("p t (h e) -> p t h e", e=HD)
                        khi = hi[:, :, 1, :].rearrange("p t (h e) -> p t h e", e=HD)
                        for s in (0, 1, 2):
                            dve.tensor_copy(q_parts[:, :, :, 8 * s:8 * s + 8], qhi)
                        for s in (0, 3, 5):
                            ins = dve.tensor_copy(k_parts[:, :, :, 8 * s:8 * s + 8], khi)
                        ins.then_inc(parts_dve.sem, 1)
                        dve.memset(q_parts[:, :, :, 48:51], 0.0)
                        dve.wait_ge(mid_sb.sem, mid_sb(b, 1))
                        dve.wait_ge(rest_sb.sem, rest_sb(b, 1))
                        dve.tensor_tensor(lo[:, :, :, :], rest[:, :, :, :], mid[:, :, :, :],
                                          ALU.subtract).then_inc(rest_sb.sem, 1)
                        dve.wait_ge(rest_sb.sem, rest_sb(b, 2))
                        dve.tensor_copy(q_parts[:, :, :, 40:48], lo[:, :, 0, :].rearrange("p t (h e) -> p t h e", e=HD))
                        dve.tensor_copy(k_parts[:, :, :, 16:24], lo[:, :, 1, :].rearrange("p t (h e) -> p t h e", e=HD)
                                        ).then_inc(parts_dve.sem, 1)

                    def turn_max_step(p):
                        dve.wait_ge(turned_max.sem, turned_max(b, p + 1))
                        if p >= 2:
                            dve.wait_ge(max_ps.sem, max_ps(b, 8 * (p - 1)))
                        dve.tensor_copy(qT_max[:, p % 2, :], TQ[:, :]).then_inc(q_max_sb.sem, 1)

                    def max_step(p, t):
                        for j in range(2):
                            n = 8 * p + 2 * t + j
                            dve.wait_ge(max_ps.sem, max_ps(b, n + 1))
                            dve.tensor_reduce(negmax[:, 2 * p + j, t:t + 1], S1[j][:, 0:keys(t)], AX.X, ALU.max,
                                              negate=True).then_inc(max_read.sem, 1)

                    def max_rows_step(p):
                        hs = slice(2 * p, 2 * p + 2)

                        def rows(i):
                            return q_parts[:, :, hs, 48 + i].rearrange("p t h -> p h t")

                        dve.wait_ge(max_read.sem, max_read(b, 8 * (p + 1)))
                        own(dve.tensor_copy(nm_hi[:, hs, :], negmax[:, hs, :]))
                        own.wait()
                        dve.tensor_copy(rows(0), nm_hi[:, hs, :])
                        own(dve.tensor_tensor(nm_rest[:, hs, :], negmax[:, hs, :], nm_hi[:, hs, :], ALU.subtract))
                        own.wait()
                        own(dve.tensor_copy(nm_mid[:, hs, :], nm_rest[:, hs, :]))
                        own.wait()
                        dve.tensor_copy(rows(1), nm_mid[:, hs, :])
                        dve.tensor_tensor(rows(2), nm_rest[:, hs, :], nm_mid[:, hs, :],
                                          ALU.subtract).then_inc(max_rows.sem, 1)
                        dve.wait_ge(turned_q.sem, turned_q(b, p + 1))
                        if p >= 4:
                            dve.wait_ge(score_ps.sem, score_ps(b, R * (p // 2 - 1)))
                        dve.tensor_copy(qT[:, (p // 2) % 2, p % 2, :], TQ[:, :]).then_inc(q_sb.sem, 1)

                    def o_step(g):
                        dve.wait_ge(turned_o.sem, turned_o(b, g + 1))
                        To = T[:, :].rearrange("p (t j e) -> p t j e", t=NT, j=4)
                        own(dve.reciprocal(rsum[:, g % 2, :, :], To[:, :, :, HD]))
                        own.wait()
                        oo = o[:, :, :].rearrange("p t (g j e) -> p t g j e", g=QUADS, j=4)
                        for t in range(NT):
                            ins = dve.tensor_tensor(oo[:, t, g, :, :], To[:, t, :, 0:HD],
                                                    rsum[:, g % 2, t, :].unsqueeze(2).to_broadcast([P, 4, HD]), ALU.mult)
                        ins.then_inc(o_sb.sem, 1)

                    def proj_step():
                        dve.wait_ge(proj_ps.sem, proj_ps(b, 1))
                        dst = k.y if causal else k.x
                        pr = AV[:, :].rearrange("p (t d) -> p t d", t=NT)
                        for t in range(NT):
                            tok = dst[:, b * NT + t, :]
                            ins = dve.tensor_tensor(tok, pr[:, t, :], tok, ALU.add)
                        ins.then_inc(out_sb.sem, 1)
                        dve.wait_ge(out_sb.sem, out_sb(b, 1))
                        if not causal:
                            for t in range(NT):
                                tok = dst[:, b * NT + t, :]
                                dve.tensor_tensor(tok, k.b_att[:, :], tok, ALU.add)

                    does = {"h": h_step, "parts": parts_step, "turn_max": turn_max_step, "max": max_step,
                            "max_rows": max_rows_step, "o": o_step, "proj": proj_step}
                    for s in order:
                        if s[0] in does:
                            does[s[0]](*s[1:])
                    own.end()

            @block.tensor
            def _(pe):
                pe.wait_ge(s_init, 5)
                pe.wait_ge(s_zero, 1)
                with pe.Fori(0, B) as b:
                    def h_step():
                        pe.wait_ge(h_ready.sem, h_ready(b, 1))
                        for t in range(NT):
                            ins = pe.transpose(T[:, P * t:P * t + P], h[:, t, :], k.ident[:, :])
                        ins.then_inc(hT_ps.sem, 1)

                    def qkv_step():
                        pe.wait_ge(hT_sb.sem, hT_sb(b, 1))
                        for t in range(NT):
                            pe.matmul(bank[4 + t][:, 0:3 * D], hT[:, P * t:P * t + P], w_in[:, :],
                                      start=True, stop=True).then_inc(qkv_ps.sem, 1)

                    def turn(dst, parts, p):
                        for t in range(NT):
                            ins = pe.transpose(dst[:, P * t:P * t + P],
                                               parts[:, t, 2 * p:2 * p + 2, :].rearrange("p h s -> p (h s)"),
                                               k.identb[:, :])
                        return ins

                    def turn_max_step(p):
                        if p == 0:
                            pe.wait_ge(parts_dve.sem, parts_dve(b, 2))
                            pe.wait_ge(parts_pool.sem, parts_pool(b, 2))
                        wait_t_free(pe, b, ("turn_max", p))
                        turn(TQ, q_parts, p)
                        turn(TK, k_parts, p).then_inc(turned_max.sem, 1)

                    def max_step(p, t):
                        if t == 0:
                            pe.wait_ge(q_max_sb.sem, q_max_sb(b, p + 1))
                            pe.wait_ge(k_sb.sem, k_sb(b, p + 1))
                        for j in range(2):
                            n = 8 * p + 2 * t + j
                            if n >= 2:
                                pe.wait_ge(max_read.sem, max_read(b, n - 1))
                            kt = kT[:, (p // 2) % 2, 2 * (p % 2) + j, 0:keys(t)]
                            ins = pe.matmul(S1[j][:, 0:keys(t)], qT_max[:, p % 2, P * t:P * t + P], kt,
                                            start=True, stop=not causal)
                            if causal:
                                ins = pe.matmul(S1[j][:, P * t:P * t + P], k.identb[:, :], k.mask_qk[:, :],
                                                start=False, stop=True)
                            ins.then_inc(max_ps.sem, 1)

                    def max_rows_step(p):
                        pe.wait_ge(max_rows.sem, max_rows(b, p + 1))
                        wait_t_free(pe, b, ("max_rows", p))
                        turn(TQ, q_parts, p).then_inc(turned_q.sem, 1)

                    def score_step(g, r):
                        n = R * g + r
                        if r == 0:
                            pe.wait_ge(q_sb.sem, q_sb(b, 2 * g + 2))
                            if g == 0:
                                pe.wait_ge(v_sb.sem, v_sb(b, NT))
                        if n >= 2:
                            pe.wait_ge(probs_sb.sem, probs_sb(b, n - 1))
                        for i, (j, kt, bk, col) in enumerate(rounds[r]):
                            out = bank[4 + 2 * (n % 2) + bk]
                            w = N - q_from(kt)
                            last = not causal
                            ins = pe.matmul(out[:, col:col + w], kT[:, g % 2, j, P * kt:P * kt + P],
                                            qT[:, g % 2, j // 2, q_from(kt):N], start=True, stop=last)
                            if causal:
                                ins = pe.matmul(out[:, col:col + P], k.identb[:, :], k.mask_kq[:, :],
                                                start=False, stop=True)
                        ins.then_inc(score_ps.sem, 1)

                    def av_step(g):
                        pe.wait_ge(probs_sb.sem, probs_sb(b, R * (g + 1)))
                        if g >= 1:
                            pe.wait_ge(av_sb.sem, av_sb(b, g))
                        for kt in range(NT):
                            for j in range(4):
                                w = N - q_from(kt)
                                ins = pe.matmul(AV[32 * j:32 * j + 32, q_from(kt):N], v_ones[:, kt, 4 * g + j, :],
                                                probs[:, g % 2, j, at[kt]:at[kt] + w], start=kt == 0, stop=kt == NT - 1)
                        ins.then_inc(av_ps.sem, 1)

                    def o_step(g):
                        pe.wait_ge(av_sb.sem, av_sb(b, g + 1))
                        wait_t_free(pe, b, ("o", g))
                        for t in range(NT):
                            ins = pe.transpose(T[:, P * t:P * t + P], oT[:, g % 2, P * t:P * t + P], k.ident[:, :])
                        ins.then_inc(turned_o.sem, 1)

                    def proj_step():
                        pe.wait_ge(o_sb.sem, o_sb(b, QUADS))
                        for t in range(NT):
                            ins = pe.transpose(T[:, P * t:P * t + P], o[:, t, :], k.ident[:, :])
                        ins.then_inc(oT_ps.sem, 1)
                        pe.wait_ge(oT_sb.sem, oT_sb(b, 1))
                        for t in range(NT):
                            ins = pe.matmul(AV[:, P * t:P * t + P], oTn[:, P * t:P * t + P], w_out[:, :],
                                            start=True, stop=True)
                        ins.then_inc(proj_ps.sem, 1)

                    does = {"h": h_step, "qkv": qkv_step, "turn_max": turn_max_step, "max": max_step,
                            "max_rows": max_rows_step, "score": score_step, "av": av_step, "o": o_step,
                            "proj": proj_step}
                    for s in order:
                        if s[0] in does:
                            does[s[0]](*s[1:])


def experts(nc, k, a, name):
    with ExitStack() as ctx:
        ctx.callback(end_module, nc)

        def sb(n, shape, dt=F32):
            return ctx.enter_context(nc.sbuf_tensor(f"{name}_{n}", shape, dt))

        def sem(n):
            return take_semaphore(nc, ctx, f"{name}_{n}")

        def signal(n, per):
            return Signal(sem(n), per)

        CH = EXP_DIM // P
        FAR = -3.0e38
        TAKEN = 3.0e38
        w1 = sb("w1", [P, EXPERTS, EXP_DIM])
        w2 = sb("w2", [P, EXPERTS, CH, D])
        gate_w = sb("gate_w", [P, EXPERTS])
        g2 = sb("g2", [P, 1])
        squares = sb("squares", [P, D])
        ms = sb("ms", [P, TILES])
        rms = sb("rms", [P, TILES])
        h = sb("h", [P, NT, D])
        hT = sb("hT", [P, N])
        logits = sb("logits", [P, NT, 16])
        left = sb("left", [P, NT, 16])
        best = sb("best", [P, NT, 8])
        drop = sb("drop", [P, NT, 8])
        taken = sb("taken", [P, NT, EXPERTS])
        away = sb("away", [P, NT, EXPERTS])
        share = sb("share", [P, NT, EXPERTS])
        total = sb("total", [P, NT])
        gates = sb("gates", [P, NT, EXPERTS])
        hidden = sb("hidden", [P, 2, CH, N])
        bank = k.bank
        T, G = bank[0], bank[1]

        s_weighed, s_go = sem("weighed"), sem("go")
        s_w, s_init, s_ms, s_rms, s_sq = sem("weights"), sem("init"), sem("rms_step"), sem("rms_done"), sem("squares_done")
        h_ready = signal("h_ready", 1)
        hT_ps = signal("hT_ps", 1)
        hT_sb = signal("hT_sb", 1)
        gate_ps = signal("gate_ps", 1)
        away_sb = signal("away_sb", 1)
        share_sb = signal("share_sb", 1)
        hid_ps = signal("hid_ps", EXPERTS)
        hid_sb = signal("hid_sb", EXPERTS)
        out_ps = signal("out_ps", EXPERTS)

        with nc.Block() as block:
            @block.sync
            def _(sp):
                sp.dma_start(gate_w[:, :], a["L0_ffn_gate_w"]).then_inc(s_w, 16)
                sp.dma_start(g2[:, :], a["L0_ffn_g2"].rearrange("(p o) -> p o", o=1)).then_inc(s_w, 16)
                sp.dma_start(w1[:, :, :], a["L0_ffn_w1"].rearrange("e d h -> d e h")).then_inc(s_w, 16)
                sp.dma_start(w2[:, :, :, :], a["L0_ffn_w2"].rearrange("e (c p) d -> p e c d", p=P)).then_inc(s_w, 16)
                sp.wait_ge(s_w, 64)

            @block.gpsimd
            def _(pool):
                pool.memset(drop[:, :, :], FAR).then_inc(s_init, 1)
                pool.memset(logits[:, :, :], FAR).then_inc(s_init, 1)
                pool.wait_ge(s_sq, 1)
                pool.tensor_scalar(rms[:, :], ms[:, :], 1.0 / D, 1e-6, ALU.mult, ALU.add).then_inc(s_ms, 1)
                pool.wait_ge(s_ms, 1)
                pool.tensor_tensor(ms[:, :], rms[:, :], k.half[:, :], ALU.pow).then_inc(s_rms, 1)

            @block.scalar
            def _(act):
                act.wait_ge(s_w, 64)
                with act.Fori(0, B) as b:
                    act.wait_ge(hT_ps.sem, hT_ps(b, 1))
                    act.mul(hT[:, :], T[:, :], g2[:, 0:1]).then_inc(hT_sb.sem, 1)
                    act.wait_ge(away_sb.sem, away_sb(b, 1))
                    act.activation(share[:, :, :], away[:, :, :], ACT.Exp).then_inc(share_sb.sem, 1)
                    for e in range(EXPERTS):
                        act.wait_ge(hid_ps.sem, hid_ps(b, e + 1))
                        if e >= 2:
                            act.wait_ge(out_ps.sem, out_ps(b, e - 1))
                        for c in range(CH):
                            ins = act.activation(hidden[:, e % 2, c, :], bank[4 + 2 * (e % 2) + c][:, :], ACT.Silu)
                        ins.then_inc(hid_sb.sem, 1)

            @block.vector
            def _(dve):
                own = Chain(dve, sem("dve_step"), 9)
                weighed = Chain(dve, s_weighed, EXPERTS)
                for t in range(TILES):
                    ins = dve.tensor_tensor_reduce(squares[:, :], k.y[:, t, :], k.y[:, t, :], 1.0, 0.0,
                                                   ALU.mult, ALU.add, ms[:, t:t + 1])
                    if t < TILES - 1:
                        ins.then_inc(own.sem, 1)
                        dve.wait_ge(own.sem, t + 1)
                ins.then_inc(s_sq, 1)
                dve.sem_clear(own.sem)
                dve.wait_ge(s_rms, 1)
                dve.wait_ge(s_init, 2)
                with dve.Fori(0, B) as b:
                    own.start(b)
                    weighed.start(b)
                    for t in range(NT):
                        ins = dve.tensor_scalar(h[:, t, :], k.y[:, b * NT + t, :], ms[:, bass.ds(b * NT + t, 1)],
                                                None, ALU.mult)
                    ins.then_inc(h_ready.sem, 1)
                    dve.wait_ge(gate_ps.sem, gate_ps(b, 1))
                    own(dve.tensor_copy(logits[:, :, 0:EXPERTS],
                                        G[:, 0:NT * EXPERTS].rearrange("p (t e) -> p t e", t=NT)))
                    own.wait_apart(s_go)
                    for t in range(NT):
                        ins = dve.max(best[:, t, :], logits[:, t, 0:EXPERTS])
                    own(ins)
                    own.wait()
                    own(dve.tensor_copy(drop[:, :, 0:2], best[:, :, 0:2]))
                    dve.tensor_tensor(away[:, :, :], logits[:, :, 0:EXPERTS],
                                      best[:, :, 0:1].to_broadcast([P, NT, EXPERTS]), ALU.subtract).then_inc(away_sb.sem, 1)
                    own.wait_apart(s_go)
                    for t in range(NT):
                        ins = dve.match_replace(out=left[:, t, :], in_to_replace=drop[:, t, :],
                                                in_values=logits[:, t, :], imm_value=TAKEN)
                    own(ins)
                    own.wait()
                    own(dve.tensor_scalar(taken[:, :, :], left[:, :, 0:EXPERTS], TAKEN, None, ALU.is_equal))
                    own.wait()
                    dve.wait_ge(share_sb.sem, share_sb(b, 1))
                    own(dve.tensor_tensor(gates[:, :, :], share[:, :, :], taken[:, :, :], ALU.mult))
                    own.wait()
                    own(dve.tensor_reduce(total[:, :], gates[:, :, :], AX.X, ALU.add))
                    own.wait()
                    own(dve.reciprocal(total[:, :], total[:, :]))
                    own.wait()
                    own(dve.tensor_tensor(gates[:, :, :], gates[:, :, :],
                                          total[:, :].unsqueeze(2).to_broadcast([P, NT, EXPERTS]), ALU.mult))
                    own.wait()
                    for e in range(EXPERTS):
                        dve.wait_ge(out_ps.sem, out_ps(b, e + 1))
                        if e > 0:
                            weighed.wait()
                        O = bank[2 + e % 2]
                        for t in range(NT):
                            tok = k.y[:, b * NT + t, :]
                            ins = dve.scalar_tensor_tensor(out=tok, in0=O[:, P * t:P * t + P], scalar=gates[:, t, e:e + 1],
                                                           in1=tok, op0=ALU.mult, op1=ALU.add)
                        weighed(ins)
                    weighed.wait()
                    for t in range(NT):
                        tok = k.x[:, b * NT + t, :]
                        dve.scalar_tensor_tensor(out=tok, in0=k.y[:, b * NT + t, :], scalar=0.5, in1=tok,
                                                 op0=ALU.mult, op1=ALU.add)
                    own.end()
                    weighed.end()

            @block.tensor
            def _(pe):
                pe.wait_ge(s_w, 64)
                with pe.Fori(0, B) as b:
                    pe.wait_ge(h_ready.sem, h_ready(b, 1))
                    for t in range(NT):
                        ins = pe.transpose(T[:, P * t:P * t + P], h[:, t, :], k.ident[:, :])
                    ins.then_inc(hT_ps.sem, 1)
                    pe.wait_ge(hT_sb.sem, hT_sb(b, 1))
                    for t in range(NT):
                        ins = pe.matmul(G[:, EXPERTS * t:EXPERTS * t + EXPERTS], hT[:, P * t:P * t + P],
                                        gate_w[:, :], start=True, stop=True)
                    ins.then_inc(gate_ps.sem, 1)

                    def up(e):
                        if e >= 2:
                            pe.wait_ge(hid_sb.sem, hid_sb(b, e - 1))
                        for c in range(CH):
                            ins = pe.matmul(bank[4 + 2 * (e % 2) + c][:, :], w1[:, e, P * c:P * c + P], hT[:, :],
                                            start=True, stop=True)
                        ins.then_inc(hid_ps.sem, 1)

                    def down(e):
                        pe.wait_ge(hid_sb.sem, hid_sb(b, e + 1))
                        if e >= 2:
                            pe.wait_ge(s_weighed, b * EXPERTS + e - 1)
                        for t in range(NT):
                            for c in range(CH):
                                ins = pe.matmul(bank[2 + e % 2][:, P * t:P * t + P], hidden[:, e % 2, c, P * t:P * t + P],
                                                w2[:, e, c, :], start=c == 0, stop=c == CH - 1)
                        ins.then_inc(out_ps.sem, 1)

                    up(0)
                    for e in range(EXPERTS):
                        if e + 1 < EXPERTS:
                            up(e + 1)
                        down(e)


def rope_table():
    half = ROT // 2
    inv = (np.float32(1.0) / np.power(np.float32(10000.0), np.arange(half, dtype=np.float32)
                                      * np.float32(2.0) / np.float32(ROT))).astype(np.float32)
    ang = (np.arange(N, dtype=np.float32)[:, None] * inv).astype(np.float32)
    c, s = np.cos(ang).astype(np.float32), np.sin(ang).astype(np.float32)
    return np.ascontiguousarray(np.concatenate([c, c, s, s], axis=1))


def mosa(nc, k, a, name):
    with ExitStack() as ctx:
        ctx.callback(end_module, nc)

        def sb(n, shape, dt=F32):
            return ctx.enter_context(nc.sbuf_tensor(f"{name}_{n}", shape, dt))

        def sem(n):
            return take_semaphore(nc, ctx, f"{name}_{n}")

        def signal(n, per):
            return Signal(sem(n), per)

        E = MEXP
        PAIRS = E // 2
        TAKEN = -1.0
        router = sb("router", [P, 32])
        router_rows = sb("router_rows", [E, P])
        w_qkv = sb("w_qkv", [P, E, 3 * D])
        w_rot = sb("w_rot", [P, E, 2, ROT])
        w_out = sb("w_out", [P, E, D])
        rope = sb("rope", [P, NT, P])
        stats = sb("stats", [P, TILES, 6])
        mv = sb("mv", [P, TILES, 2])
        var = sb("var", [P, TILES])
        rstd = sb("rstd", [P, TILES])
        hT = sb("hT", [P, N])
        grow = sb("grow", [P, N])
        gate = sb("gate", [P, N])
        work = sb("work", [P, 2, N])
        best = sb("best", [P, 8])
        chosen = sb("chosen", [P, N], BF16)
        chosenT = sb("chosenT", [P, NT, P], BF16)
        upto = sb("upto", [P, NT, N], BF16)
        rank = sb("rank", [P, N], BF16)
        rankT = sb("rankT", [P, NT, P])
        gate_part = sb("gate_part", [P, 3, N], BF16)
        gate_rest = sb("gate_rest", [P, 2, N])
        select = sb("select", [P, B * PAIRS, P], BF16)
        count = sb("count", [P, E, MK])
        slot = sb("slot", [P, 1])
        order_mask = sb("order_mask", [P, MK])
        onehot = sb("onehot", [P, NT, E * MK])
        h = sb("h", [P, NT, D])
        xg = sb("xg", [P, E * MK])
        turn = sb("turn", [P, E * MK])
        rot_a = sb("rot_a", [ROT, 2, E * MK])
        rot_b = sb("rot_b", [ROT, 2, E * MK])
        qr = sb("qr", [P, E * MK])
        kr = sb("kr", [P, E * MK])
        v = sb("v", [P, PAIRS, D])
        scores = sb("scores", [P, PAIRS, MK])
        top = sb("top", [P, PAIRS])
        total = sb("total", [P, PAIRS])
        probs = sb("probs", [P, PAIRS, MK])
        diag = sb("diag", [P, PAIRS, P])
        diagT = sb("diagT", [P, PAIRS, P])
        avT = sb("avT", [P, PAIRS, P])
        pre = sb("pre", [P, PAIRS, D])
        gate_sb = sb("gate_sb", [P, PAIRS, N])
        scatter = sb("scatter", [P, PAIRS, N])
        bank = k.bank

        s_w, s_wr, s_made, s_made2, s_stat, s_ms, s_rstd = (sem(n) for n in (
            "weights", "router_in", "made", "made2", "stat", "rstd_step", "rstd_done"))
        s_rot = sem("rot_weights")
        s_rps, s_rsb = sem("router_ps"), sem("router_sb")
        s_h, s_hps, s_hsb, s_logit = sem("h_ready"), sem("hT_ps"), sem("hT_sb"), sem("logit_ps")
        s_grow, s_chosen, s_cps, s_csb, s_rank, s_rkm, s_rtps, s_ranked = (sem(n) for n in (
            "grown", "chosen_done", "chosenT_ps", "chosenT_sb", "rank_ps", "rank_done", "rankT_ps", "ranked"))
        copied = signal("h_copied", 1)
        hot = signal("onehot_done", 1)
        xg_ps, xg_sb = signal("xg_ps", 1), signal("xg_sb", 1)
        tab_ps, tab_sb = signal("turn_ps", 1), signal("turn_sb", 1)
        proj_ps = signal("qkv_ps", 1)
        v_ps, v_sb = signal("v_ps", 1), signal("v_sb", 1)
        rest_sb = signal("unturned_sb", 1)
        qk_sb = signal("qk_sb", 1)
        sc_ps = signal("score_ps", 1)
        away_sb = signal("away_sb", 1)
        exp_sb = signal("exp_sb", 1)
        diag_sb = signal("diag_sb", 1)
        dT_ps, dT_sb = signal("diagT_ps", 1), signal("diagT_sb", 1)
        av_ps, av_sb = signal("av_ps", 1), signal("av_sb", 1)
        pre_ps, pre_sb = signal("pre_ps", 1), signal("pre_sb", 1)
        bc_ps, g_sb, sc_sb = signal("broadcast_ps", PAIRS), signal("gate_sb_done", PAIRS), signal("scatter_sb", PAIRS)
        out_ps = signal("out_ps", 1)

        with nc.Block() as block:
            @block.sync
            def _(sp):
                sp.dma_start(router_rows[:, :], a["L1_ffn_Wr"]).then_inc(s_wr, 16)
                sp.dma_start(w_qkv[:, :, :], a["L1_ffn_Wqkv"].rearrange("e d j -> d e j")).then_inc(s_w, 16)
                sp.dma_start(w_out[:, :, :], a["L1_ffn_Wo"].rearrange("e d j -> d e j")).then_inc(s_w, 16)
                sp.dma_start(rope[:, :, :], a["rope"].rearrange("(t p) j -> p t j", p=P)).then_inc(s_w, 16)
                sp.wait_ge(s_wr, 16)
                sp.wait_ge(s_w, 48)

            @block.gpsimd
            def _(pool):
                n = 0

                def step(ins):
                    nonlocal n
                    ins.then_inc(s_ms, 1)
                    n += 1
                    pool.wait_ge(s_ms, n)

                pool.memset(upto[:, :, :], 1.0).then_inc(s_made, 1)
                pool.memset(select[:, :, :], 0.0).then_inc(s_made, 1)
                pool.memset(order_mask[:, :], 0.0).then_inc(s_made, 1)
                pool.memset(diag[:, :, :], 0.0).then_inc(s_made, 1)
                pool.iota(count[:, :, :], pattern=[[0, E], [1, MK]], base=1, channel_multiplier=0,
                          allow_small_or_imprecise_dtypes=True).then_inc(s_made, 1)
                pool.iota(slot[:, :], pattern=[[0, 1]], base=1, channel_multiplier=1,
                          allow_small_or_imprecise_dtypes=True).then_inc(s_made, 1)
                pool.wait_ge(s_made, 6)
                pool.affine_select(out=upto[:, :, :], in_=upto[:, :, :], compare_op=ALU.is_ge, fill=0.0, base=0,
                                   pattern=[[-P, NT], [1, N]], channel_multiplier=-1).then_inc(s_made2, 1)
                for e2 in range(2):
                    for b in range(B):
                        ins = pool.affine_select(out=select[:, PAIRS * b:PAIRS * b + PAIRS, MK * e2:MK * e2 + MK],
                                                 in_=select[:, PAIRS * b:PAIRS * b + PAIRS, MK * e2:MK * e2 + MK],
                                                 compare_op=ALU.not_equal, fill=1.0, base=-32 * b - e2,
                                                 pattern=[[-2, PAIRS], [0, MK]], channel_multiplier=1)
                        ins.then_inc(s_made2, 1)
                pool.affine_select(out=order_mask[:, :], in_=order_mask[:, :],
                                   compare_op=ALU.is_ge, fill=NEG, base=0, pattern=[[-1, MK]],
                                   channel_multiplier=1).then_inc(s_made2, 1)
                pool.wait_ge(s_stat, 1)
                step(pool.tensor_scalar(var[:, :], mv[:, :, 1], 1e-5, None, ALU.add))
                pool.tensor_tensor(rstd[:, :], var[:, :], k.half[:, :], ALU.pow).then_inc(s_rstd, 1)
                pool.wait_ge(s_w, 48)
                for i in range(2):
                    pool.tensor_scalar(w_rot[:, :, i, 0:ROT // 2], w_qkv[:, :, D * i + ROT // 2:D * i + ROT], -1.0, None,
                                       ALU.mult).then_inc(s_rot, 1)
                    pool.tensor_copy(w_rot[:, :, i, ROT // 2:ROT], w_qkv[:, :, D * i:D * i + ROT // 2]).then_inc(s_rot, 1)

            @block.scalar
            def _(act):
                for b in range(B):
                    act.wait_ge(s_hps, b + 1)
                    if b > 0:
                        act.wait_ge(s_logit, b)
                    act.copy(hT[:, :], bank[b % 2][:, :]).then_inc(s_hsb, 1)
                act.wait_ge(s_logit, B)
                act.activation(grow[:, :], bank[2][:, :], ACT.Exp, scale=-1.0).then_inc(s_grow, 1)
                with act.Fori(0, B) as b:
                    act.copy(h[:, :, :], k.y[:, bass.ds(b * NT, NT), :]).then_inc(copied.sem, 1)
                    act.wait_ge(xg_ps.sem, xg_ps(b, 1))
                    act.copy(xg[:, :], bank[0][:, :]).then_inc(xg_sb.sem, 1)
                    act.wait_ge(tab_ps.sem, tab_ps(b, 1))
                    act.copy(turn[:, :], bank[1][:, :]).then_inc(tab_sb.sem, 1)
                    act.wait_ge(proj_ps.sem, proj_ps(b, 1))
                    act.copy(qr[ROT:P, :], bank[2][ROT:P, :])
                    act.copy(kr[ROT:P, :], bank[3][ROT:P, :]).then_inc(rest_sb.sem, 1)
                    act.wait_ge(v_ps.sem, v_ps(b, 1))
                    act.copy(v[:, :, :].rearrange("p a d -> p (a d)"), bank[0][:, :]).then_inc(v_sb.sem, 1)
                    for i in range(PAIRS):
                        act.wait_ge(bc_ps.sem, bc_ps(b, i + 1))
                        act.copy(gate_sb[:, i, :], bank[6 + i % 2][:, :]).then_inc(g_sb.sem, 1)
                    act.wait_ge(away_sb.sem, away_sb(b, 1))
                    act.activation(probs[:, :, :], scores[:, :, :], ACT.Exp).then_inc(exp_sb.sem, 1)
                    act.wait_ge(dT_ps.sem, dT_ps(b, 1))
                    act.copy(diagT[:, :, :].rearrange("p a d -> p (a d)"), bank[1][:, :]).then_inc(dT_sb.sem, 1)
                    act.wait_ge(av_ps.sem, av_ps(b, 1))
                    act.copy(avT[:, :, :].rearrange("p a d -> p (a d)"), bank[0][:, :]).then_inc(av_sb.sem, 1)
                    act.wait_ge(pre_ps.sem, pre_ps(b, 1))
                    act.copy(pre[:, :, :].rearrange("p a d -> p (a d)"), bank[2][:, :]).then_inc(pre_sb.sem, 1)

            @block.vector
            def _(dve):
                first = Chain(dve, sem("dve_first"), 0)
                own = Chain(dve, sem("dve_step"), 6)
                for t in range(TILES):
                    ins = dve.bn_stats(stats[:, t, :], k.x[:, t, :])
                first(ins)
                first.wait()
                for t in range(TILES):
                    ins = dve.bn_aggr(mv[:, t, :], stats[:, t, :])
                ins.then_inc(s_stat, 1)
                dve.wait_ge(s_stat, 1)
                first(dve.memset(router[:, :], 0.0))
                first.wait()
                dve.wait_ge(s_rps, 1)
                dve.tensor_copy(router[:, 0:E], bank[3][:, 0:E]).then_inc(s_rsb, 1)
                dve.wait_ge(s_rstd, 1)
                for t in range(TILES):
                    ins = dve.tensor_scalar(k.y[:, t, :], k.x[:, t, :], mv[:, t, 0:1], rstd[:, t:t + 1],
                                            ALU.subtract, ALU.mult)
                    if t % NT == NT - 1:
                        ins.then_inc(s_h, 1)
                dve.wait_ge(s_grow, 1)
                first(dve.tensor_scalar(grow[:, :], grow[:, :], 1.0, None, ALU.add))
                first.wait()
                first(dve.reciprocal(gate[:, :], grow[:, :]))
                first.wait()
                for r in range(MK // 8):
                    src = gate[:, :] if r == 0 else work[:, (r - 1) % 2, :]
                    first(dve.max(best[:, :], src))
                    first.wait()
                    first(dve.match_replace(out=work[:, r % 2, :], in_to_replace=best[:, :], in_values=src,
                                            imm_value=TAKEN))
                    first.wait()
                dve.tensor_scalar(chosen[:, :], work[:, (MK // 8 - 1) % 2, :], TAKEN, None,
                                  ALU.is_equal).then_inc(s_chosen, 1)
                first(dve.tensor_copy(gate_part[:, 0, :], gate[:, :]))
                first.wait()
                first(dve.tensor_tensor(gate_rest[:, 0, :], gate[:, :], gate_part[:, 0, :], ALU.subtract))
                first.wait()
                first(dve.tensor_copy(gate_part[:, 1, :], gate_rest[:, 0, :]))
                first.wait()
                first(dve.tensor_tensor(gate_part[:, 2, :], gate_rest[:, 0, :], gate_part[:, 1, :], ALU.subtract))
                dve.wait_ge(s_cps, 1)
                dve.tensor_copy(chosenT[:, :, :].rearrange("p t r -> p (t r)"),
                                bank[0][:, 0:256].bitcast(BF16)).then_inc(s_csb, 1)
                dve.wait_ge(s_rank, 1)
                dve.wait_ge(s_chosen, 1)
                dve.tensor_tensor(rank[:, :], bank[1][:, :], chosen[:, :], ALU.mult).then_inc(s_rkm, 1)
                dve.wait_ge(s_rtps, 1)
                dve.tensor_copy(rankT[:, :, :].rearrange("p t r -> p (t r)"),
                                bank[0][:, 0:256].bitcast(BF16)).then_inc(s_ranked, 1)
                dve.wait_ge(s_ranked, 1)
                dve.wait_ge(s_made2, 10)
                first(dve.tensor_scalar(slot[MK:P, :], slot[MK:P, :], float(-MK), None, ALU.add))
                first(dve.tensor_copy(order_mask[MK:P, :], order_mask[0:MK, :]))
                first.wait()
                with dve.Fori(0, B) as b:
                    own.start(b)
                    for c in range(NT):
                        ins = dve.tensor_tensor(onehot[:, c, :].rearrange("p (e j) -> p e j", e=E),
                                                rankT[:, c, bass.ds(b * 32, E)].unsqueeze(2).to_broadcast([P, E, MK]),
                                                count[:, :, :], ALU.is_equal)
                    ins.then_inc(hot.sem, 1)
                    dve.wait_ge(tab_sb.sem, tab_sb(b, 1))
                    dve.wait_ge(proj_ps.sem, proj_ps(b, 1))
                    for i, src in enumerate((bank[2], bank[3])):
                        dve.wait_ge(rest_sb.sem, rest_sb(b, 1))
                        dve.tensor_tensor(rot_a[:, i, :], src[0:ROT, :], turn[0:ROT, :], ALU.mult)
                        own(dve.tensor_tensor(rot_b[:, i, :], bank[4 + i][ROT:P, :], turn[ROT:P, :], ALU.mult))
                    own.wait()
                    dve.tensor_tensor(qr[0:ROT, :], rot_a[:, 0, :], rot_b[:, 0, :], ALU.add)
                    dve.tensor_tensor(kr[0:ROT, :], rot_a[:, 1, :], rot_b[:, 1, :], ALU.add).then_inc(qk_sb.sem, 1)
                    for i in range(PAIRS):
                        dve.wait_ge(g_sb.sem, g_sb(b, i + 1))
                        dve.scalar_tensor_tensor(out=scatter[:, i, :], in0=bank[4 + i % 2][:, :], scalar=slot[:, 0:1],
                                                 in1=gate_sb[:, i, :], op0=ALU.is_equal, op1=ALU.mult).then_inc(sc_sb.sem, 1)
                    dve.wait_ge(sc_ps.sem, sc_ps(b, 1))
                    own(dve.scalar_tensor_tensor(out=scores[:, :, :],
                                                 in0=bank[3][:, 0:PAIRS * MK].rearrange("p (a m) -> p a m", a=PAIRS),
                                                 scalar=D ** -0.5,
                                                 in1=order_mask[:, :].unsqueeze(1).to_broadcast([P, PAIRS, MK]),
                                                 op0=ALU.mult, op1=ALU.add))
                    own.wait()
                    own(dve.tensor_reduce(top[:, :], scores[:, :, :], AX.X, ALU.max))
                    own.wait()
                    dve.tensor_tensor(scores[:, :, :], scores[:, :, :], top[:, :].unsqueeze(2).to_broadcast([P, PAIRS, MK]),
                                      ALU.subtract).then_inc(away_sb.sem, 1)
                    dve.wait_ge(exp_sb.sem, exp_sb(b, 1))
                    own(dve.tensor_reduce(total[:, :], probs[:, :, :], AX.X, ALU.add))
                    own.wait()
                    own(dve.reciprocal(total[:, :], total[:, :]))
                    own.wait()
                    for e2 in range(2):
                        rows = slice(MK * e2, MK * e2 + MK)
                        ins = dve.tensor_tensor(diag[rows, :, MK * e2:MK * e2 + MK], probs[rows, :, :],
                                                total[rows, :].unsqueeze(2).to_broadcast([MK, PAIRS, MK]), ALU.mult)
                    ins.then_inc(diag_sb.sem, 1)
                    dve.wait_ge(out_ps.sem, out_ps(b, 1))
                    for t in range(NT):
                        tok = k.x[:, b * NT + t, :]
                        dve.scalar_tensor_tensor(out=tok, in0=bank[3][:, P * t:P * t + P], scalar=0.5, in1=tok,
                                                 op0=ALU.mult, op1=ALU.add)
                    own.end()

            @block.tensor
            def _(pe):
                pe.wait_ge(s_wr, 16)
                pe.transpose(bank[3][:, 0:E], router_rows[:, :], k.ident[0:E, 0:E]).then_inc(s_rps, 1)
                for b in range(B):
                    pe.wait_ge(s_h, b + 1)
                    if b >= 2:
                        pe.wait_ge(s_hsb, b - 1)
                    for t in range(NT):
                        ins = pe.transpose(bank[b % 2][:, P * t:P * t + P], k.y[:, NT * b + t, :], k.ident[:, :])
                    ins.then_inc(s_hps, 1)
                    if b == 0:
                        pe.wait_ge(s_rsb, 1)
                    pe.wait_ge(s_hsb, b + 1)
                    pe.matmul(bank[2][32 * b:32 * b + 32, :], router[:, :], hT[:, :], start=True,
                              stop=True).then_inc(s_logit, 1)
                pe.wait_ge(s_chosen, 1)
                for c in range(NT):
                    ins = pe.transpose(bank[0][:, 64 * c:64 * c + 64].bitcast(BF16), chosen[:, P * c:P * c + P], k.identb[:, :])
                ins.then_inc(s_cps, 1)
                pe.wait_ge(s_csb, 1)
                pe.wait_ge(s_made2, 10)
                for c in range(NT):
                    ins = pe.matmul(bank[1][:, :], chosenT[:, c, :], upto[:, c, :], start=c == 0, stop=c == NT - 1)
                ins.then_inc(s_rank, 1)
                pe.wait_ge(s_rkm, 1)
                for c in range(NT):
                    ins = pe.transpose(bank[0][:, 64 * c:64 * c + 64].bitcast(BF16), rank[:, P * c:P * c + P], k.identb[:, :])
                ins.then_inc(s_rtps, 1)
                pe.wait_ge(s_w, 48)
                pe.wait_ge(s_rot, 4)
                with pe.Fori(0, B) as b:
                    pe.wait_ge(copied.sem, copied(b, 1))
                    pe.wait_ge(hot.sem, hot(b, 1))
                    for c in range(NT):
                        ins = pe.matmul(bank[0][:, :], h[:, c, :], onehot[:, c, :], start=c == 0, stop=c == NT - 1)
                    ins.then_inc(xg_ps.sem, 1)
                    for c in range(NT):
                        ins = pe.matmul(bank[1][:, :], rope[:, c, :], onehot[:, c, :], start=c == 0, stop=c == NT - 1)
                    ins.then_inc(tab_ps.sem, 1)
                    pe.wait_ge(xg_sb.sem, xg_sb(b, 1))
                    for e in range(E):
                        cols = slice(MK * e, MK * e + MK)
                        for i in range(2):
                            pe.matmul(bank[2 + i][:, cols], w_qkv[:, e, D * i:D * i + D], xg[:, cols], start=True, stop=True)
                            ins = pe.matmul(bank[4 + i][ROT:P, cols], w_rot[:, e, i, :], xg[:, cols], start=True, stop=True)
                    ins.then_inc(proj_ps.sem, 1)
                    for e in range(E):
                        half = slice(MK * (e % 2), MK * (e % 2) + MK)
                        ins = pe.matmul(bank[0][half, D * (e // 2):D * (e // 2) + D], xg[:, MK * e:MK * e + MK],
                                        w_qkv[:, e, 2 * D:3 * D], start=True, stop=True)
                    ins.then_inc(v_ps.sem, 1)
                    pe.wait_ge(qk_sb.sem, qk_sb(b, 1))
                    for e in range(E):
                        half = slice(MK * (e % 2), MK * (e % 2) + MK)
                        cols = slice(MK * e, MK * e + MK)
                        ins = pe.matmul(bank[3][half, MK * (e // 2):MK * (e // 2) + MK], qr[:, cols], kr[:, cols],
                                        start=True, stop=True)
                    ins.then_inc(sc_ps.sem, 1)
                    for i in range(PAIRS):
                        if i >= 2:
                            pe.wait_ge(sc_sb.sem, sc_sb(b, i - 1))
                        sel = select[:, b * PAIRS + i, :]
                        pe.matmul(bank[4 + i % 2][:, :], sel, rank[:, :], start=True, stop=True)
                        for part in range(3):
                            ins = pe.matmul(bank[6 + i % 2][:, :], sel, gate_part[:, part, :], start=part == 0, stop=part == 2)
                        ins.then_inc(bc_ps.sem, 1)
                    pe.wait_ge(diag_sb.sem, diag_sb(b, 1))
                    for i in range(PAIRS):
                        ins = pe.transpose(bank[1][:, P * i:P * i + P], diag[:, i, :], k.ident[:, :])
                    ins.then_inc(dT_ps.sem, 1)
                    pe.wait_ge(dT_sb.sem, dT_sb(b, 1))
                    for i in range(PAIRS):
                        ins = pe.matmul(bank[0][:, P * i:P * i + P], v[:, i, :], diagT[:, i, :], start=True, stop=True)
                    ins.then_inc(av_ps.sem, 1)
                    pe.wait_ge(av_sb.sem, av_sb(b, 1))
                    for e in range(E):
                        half = slice(MK * (e % 2), MK * (e % 2) + MK)
                        ins = pe.matmul(bank[2][half, D * (e // 2):D * (e // 2) + D],
                                        avT[:, e // 2, MK * (e % 2):MK * (e % 2) + MK], w_out[:, e, :],
                                        start=True, stop=True)
                    ins.then_inc(pre_ps.sem, 1)
                    pe.wait_ge(pre_sb.sem, pre_sb(b, 1))
                    pe.wait_ge(sc_sb.sem, sc_sb(b, PAIRS))
                    for t in range(NT):
                        for i in range(PAIRS):
                            ins = pe.matmul(bank[3][:, P * t:P * t + P], scatter[:, i, P * t:P * t + P], pre[:, i, :],
                                            start=i == 0, stop=i == PAIRS - 1)
                    ins.then_inc(out_ps.sem, 1)


def additive(nc, k, a, name="add"):
    with ExitStack() as ctx:
        ctx.callback(end_module, nc)

        def sb(n, shape, dt=F32):
            return ctx.enter_context(nc.sbuf_tensor(f"{name}_{n}", shape, dt))

        def sem(n):
            return take_semaphore(nc, ctx, f"{name}_{n}")

        def signal(n, per):
            return Signal(sem(n), per)

        C2 = ADIM // P
        CH = HID // P
        TOKEN_SCALE = 16 ** -0.5
        W = D + 1
        z = k.y
        wqk = sb("wqk", [P, 2, ADIM])
        wp = sb("wp", [P, C2, ADIM])
        wfg = sb("wfg", [P, C2, W])
        bqkp = sb("bqkp", [P, 3, C2])
        bqk_rows = sb("bqk_rows", [P, 2, ADIM])
        bf_rows = sb("bf_rows", [P, D])
        w1 = sb("w1", [P, HID])
        w2 = sb("w2", [P, CH, D])
        b1 = sb("b1", [P, CH])
        b2_rows = sb("b2_rows", [P, D])
        ln = sb("ln", [P, 4])
        wpT = sb("wpT", [P, C2, ADIM])
        wqkT = sb("wqkT", [P, 2, C2, D])
        wpf = sb("wpf", [P, C2, D])
        wqfg = sb("wqfg", [P, W])
        bqfg_rows = sb("bqfg_rows", [P, W])
        bpf_rows = sb("bpf_rows", [P, D])
        b_hi = sb("b_hi", [P, 2 * ADIM], BF16)
        b_mid = sb("b_mid", [P, 2 * ADIM], BF16)
        b_rest = sb("b_rest", [P, 2 * ADIM])
        b_lo = sb("b_lo", [P, 2 * ADIM], BF16)
        b_sum = sb("b_sum", [P, 2 * ADIM])
        b_parts = sb("b_parts", [P, 2 * ADIM], BF16)
        row_is = sb("row_is", [P, 3])
        three = sb("three", [P, P], BF16)
        ones = sb("ones", [P, P])
        stats = sb("stats", [P, TILES, 6])
        mv = sb("mv", [P, TILES, 2])
        var = sb("var", [P, TILES])
        rstd = sb("rstd", [P, TILES])
        zn = sb("zn", [P, TILES, D])
        hT = sb("hT", [P, B, N])
        squares = sb("squares", [P, ADIM])
        kstats = sb("kstats", [P, TILES, 6])
        kmv = sb("kmv", [P, TILES, 2])
        ss = sb("ss", [P, 2, TILES])
        inv = sb("inv", [P, 2, TILES])
        half2 = sb("half2", [P, 2, TILES])
        qf = sb("qf", [P, TILES, W])
        alpha = sb("alpha", [P, TILES])
        token_sums = sb("token_sums", [P, 2, TILES])
        over = sb("over", [P, 2, B])
        inv_a = sb("inv_a", [P, B])
        u = sb("u", [P, B])
        coef = sb("coef", [P, B])
        G = sb("G", [P, C2, B])
        bkG = sb("bkG", [P, C2, B])
        wG = sb("wG", [P, C2, B, D])
        M = sb("M", [P, B, D])
        bkM_rows = sb("bkM_rows", [P, B, D])
        kp4 = sb("kp4", [P, 2, NT, D])
        hidden = sb("hidden", [P, 2, CH, N])
        bank = k.bank

        s_w = [signal(f"w_{n}", 16 * c) for n, c in (("attn", 9), ("mlp", 6))]
        s_rows = signal("rows_in", 64)
        s_made, s_first, s_go = sem("made"), sem("first"), sem("go")
        ln_step, ln_done = signal("ln_step", 2), signal("ln_done", 2)
        zn_ok = signal("zn_ready", 2 * B)
        hT_ps, hT_sb = signal("hT_ps", 2 * B), signal("hT_sb", 2 * B)
        fold_ps, fold_sb = signal("fold_ps", 4), signal("fold_sb", 4)
        b_ok = signal("bias_parts", 1)
        q_ps, q_sq = signal("q_ps", TILES), signal("q_sq", TILES)
        k_ps, k_sq = signal("k_ps", TILES), signal("k_sq", TILES)
        f_ps, f_sb = signal("f_ps", TILES), signal("f_sb", TILES)
        ss_ok, inv_ok = signal("ss_ready", 1), signal("inv_ready", 1)
        sums_ok, sums_ps = signal("sums_ready", 1), signal("sums_ps", 1)
        over_ok, inva_ok = signal("over_ready", 1), signal("inva_ready", 1)
        u_ok, g_ps, g_ok = signal("u_ready", 1), signal("g_ps", 1), signal("g_ready", 1)
        wg_ok, m_ps, m_sb, bm_sb = signal("wg_ready", C2), signal("m_ps", 2), signal("m_sb", 1), signal("bm_sb", 1)
        kp_ps, kp_read = signal("kp_ps", B), signal("kp_read", B)
        hid_ps, hid_sb = signal("hid_ps", B * CH), signal("hid_sb", B * CH)
        out_ps, out_read = signal("out_ps", B), signal("out_read", B)
        attn_free, mlp_free = signal("attn_free", 1), signal("mlp_free", 1)

        def cols(x, n):
            return x.rearrange("o (c p) -> p (o c)", p=P)

        with nc.Block() as block:
            @block.sync
            def _(sp):
                with sp.Fori(0, DEPTH) as i:
                    one = bass.ds(i, 1)
                    sp.wait_ge(attn_free.sem, attn_free(i, 1))
                    for dst, src in (
                            (wqk[:, 0, :], a["L1_attn_Wq"][one].rearrange("o p n -> p (o n)")),
                            (wqk[:, 1, :], a["L1_attn_Wk"][one].rearrange("o p n -> p (o n)")),
                            (wp[:, :, :], a["L1_attn_Wp"][one].rearrange("o (c p) n -> p (o c) n", p=P)),
                            (wfg[:, :, 0:D], a["L1_attn_Wf"][one].rearrange("o (c p) n -> p (o c) n", p=P)),
                            (wfg[:, :, D:W], a["L1_attn_w_g"][one].rearrange("o (c p) n -> p (o c) n", p=P)),
                            (bqkp[:, 0, :], cols(a["L1_attn_bq"][one], C2)),
                            (bqkp[:, 1, :], cols(a["L1_attn_bk"][one], C2)),
                            (bqkp[:, 2, :], cols(a["L1_attn_bp"][one], C2)),
                            (ln[:, 0:1], cols(a["L1_attn_ln1_g"][one], 1))):
                        sp.dma_start(dst, src, allow_slow_non_contiguous=True).then_inc(s_w[0].sem, 16)
                    sp.wait_ge(mlp_free.sem, mlp_free(i, 1))
                    for dst, src in (
                            (w1[:, :], a["L1_attn_W1"][one].rearrange("o p n -> p (o n)")),
                            (w2[:, :, :], a["L1_attn_W2"][one].rearrange("o (c p) n -> p (o c) n", p=P)),
                            (b1[:, :], cols(a["L1_attn_b1"][one], CH)),
                            (ln[:, 2:3], cols(a["L1_attn_ln2_g"][one], 1)),
                            (ln[:, 3:4], cols(a["L1_attn_ln2_b"][one], 1)),
                            (b2_rows[:, :], a["L1_attn_b2"][one].to_broadcast([P, D]))):
                        sp.dma_start(dst, src, allow_slow_non_contiguous=True).then_inc(s_w[1].sem, 16)

            @block.gpsimd
            def _(pool):
                pool.memset(ones[:, :], 1.0).then_inc(s_made, 1)
                pool.memset(half2[:, :, :], -0.5).then_inc(s_made, 1)
                pool.memset(three[:, :], 1.0).then_inc(s_made, 1)
                pool.memset(row_is[:, :], 0.0).then_inc(s_made, 1)
                pool.wait_ge(s_made, 4)
                pool.affine_select(out=three[:, :], in_=three[:, :], compare_op=ALU.is_ge, fill=0.0, base=2,
                                   pattern=[[0, P]], channel_multiplier=-1).then_inc(s_made, 1)
                pool.affine_select(out=row_is[:, :], in_=row_is[:, :], compare_op=ALU.not_equal, fill=1.0, base=0,
                                   pattern=[[-1, 3]], channel_multiplier=1).then_inc(s_made, 1)
                pool.wait_ge(s_first, 1)
                pool.tensor_scalar(var[:, :], mv[:, :, 1], 1e-5, None, ALU.add).then_inc(s_made, 1)
                pool.wait_ge(s_made, 7)
                pool.tensor_tensor(rstd[:, :], var[:, :], k.half[:, :], ALU.pow).then_inc(s_made, 1)
                with pool.Fori(0, DEPTH) as i:
                    def rsqrt_var(j):
                        pool.wait_ge(ln_step.sem, ln_step(i, j + 1))
                        pool.tensor_tensor(rstd[:, :], var[:, :], k.half[:, :], ALU.pow).then_inc(ln_done.sem, 1)

                    rsqrt_var(0)
                    pool.wait_ge(ss_ok.sem, ss_ok(i, 1))
                    pool.tensor_tensor(inv[:, :, :], ss[:, :, :], half2[:, :, :], ALU.pow).then_inc(inv_ok.sem, 1)
                    pool.wait_ge(over_ok.sem, over_ok(i, 1))
                    pool.tensor_tensor(inv_a[:, :], over[:, 0, :], half2[:, 0, 0:B], ALU.pow).then_inc(inva_ok.sem, 1)
                    rsqrt_var(1)

            @block.scalar
            def _(act):
                with act.Fori(0, DEPTH) as i:
                    one = bass.ds(i, 1)
                    act.wait_ge(attn_free.sem, attn_free(i, 1))
                    for dst, src in (
                            (ln[:, 1:2], cols(a["L1_attn_ln1_b"][one], 1)),
                            (bqk_rows[:, 0, :], a["L1_attn_bq"][one].to_broadcast([P, ADIM])),
                            (bqk_rows[:, 1, :], a["L1_attn_bk"][one].to_broadcast([P, ADIM])),
                            (bf_rows[:, :], a["L1_attn_bf"][one].to_broadcast([P, D]))):
                        act.dma_start(dst, src, allow_slow_non_contiguous=True).then_inc(s_rows.sem, 16)

                    act.wait_ge(fold_ps.sem, fold_ps(i, 1))
                    act.copy(wpT[:, :, :].rearrange("p c n -> p (c n)"), bank[6][:, :]).then_inc(fold_sb.sem, 1)
                    act.wait_ge(fold_ps.sem, fold_ps(i, 2))
                    act.copy(wqkT[:, :, :, :].rearrange("p s c n -> p (s c n)"), bank[7][:, :]).then_inc(fold_sb.sem, 1)
                    act.wait_ge(fold_ps.sem, fold_ps(i, 3))
                    act.copy(wpf[:, :, :].rearrange("p c n -> p (c n)"), bank[6][:, 0:C2 * D])
                    act.copy(wqfg[:, :], bank[6][:, C2 * D:C2 * D + W]).then_inc(fold_sb.sem, 1)
                    act.wait_ge(s_w[0].sem, s_w[0](i, 144))
                    act.wait_ge(s_rows.sem, s_rows(i, 64))
                    for b in range(B):
                        act.wait_ge(hT_ps.sem, hT_ps(i, b + 1))
                        act.activation(hT[:, b, :], bank[b % 2][:, :], ACT.Identity, bias=ln[:, 1:2],
                                       scale=ln[:, 0:1]).then_inc(hT_sb.sem, 1)
                    for t in range(TILES):
                        act.wait_ge(q_ps.sem, q_ps(i, t + 1))
                        act.activation(squares[:, :], bank[2 + t % 2][:, 0:ADIM], ACT.Square,
                                       accum_out=ss[:, 0, t:t + 1]).then_inc(q_sq.sem, 1)
                        act.wait_ge(q_sq.sem, q_sq(i, t + 1))
                    act.wait_ge(g_ok.sem, g_ok(i, 1))
                    for b in range(B):
                        ins = act.mul(wG[:, 1, b, :], wpf[:, 1, :], G[:, 1, b:b + 1])
                    ins.then_inc(wg_ok.sem, 1)
                    act.wait_ge(m_ps.sem, m_ps(i, 1))
                    act.copy(M[:, :, :].rearrange("p b d -> p (b d)"), bank[4][:, :]).then_inc(m_sb.sem, 1)
                    act.wait_ge(s_w[1].sem, s_w[1](i, 96))
                    for b in range(B):
                        act.wait_ge(hT_ps.sem, hT_ps(i, B + b + 1))
                        act.activation(hT[:, b, :], bank[b % 2][:, :], ACT.Identity, bias=ln[:, 3:4],
                                       scale=ln[:, 2:3]).then_inc(hT_sb.sem, 1)
                    for b in range(B):
                        for c in range(CH):
                            n = CH * b + c
                            act.wait_ge(hid_ps.sem, hid_ps(i, n + 1))
                            if b >= 2 and c == 0:
                                act.wait_ge(out_ps.sem, out_ps(i, b - 1))
                            act.activation(hidden[:, b % 2, c, :], bank[4 + c][:, :], ACT.Gelu,
                                           bias=b1[:, c:c + 1]).then_inc(hid_sb.sem, 1)

            @block.vector
            def _(dve):
                own = Chain(dve, sem("dve_step"), 22)
                first = Chain(dve, sem("dve_first"), 0)
                dve.sem_inc(attn_free.sem, 1)
                dve.sem_inc(mlp_free.sem, 1)
                for t in range(TILES):
                    ins = dve.bn_stats(stats[:, t, :], k.x[:, t, :])
                first(ins)
                first.wait()
                for t in range(TILES):
                    ins = dve.bn_aggr(mv[:, t, :], stats[:, t, :])
                ins.then_inc(s_first, 1)
                dve.wait_ge(s_made, 8)
                for t in range(TILES):
                    ins = dve.tensor_scalar(z[:, t, :], k.x[:, t, :], mv[:, t, 0:1], rstd[:, t:t + 1],
                                            ALU.subtract, ALU.mult)
                first(ins)
                first.wait()
                with dve.Fori(0, DEPTH) as i:
                    own.start(i)

                    def normal(j):
                        for t in range(TILES):
                            ins = dve.bn_stats(stats[:, t, :], z[:, t, :])
                        own(ins)
                        own.wait_apart(s_go)
                        for t in range(TILES):
                            ins = dve.bn_aggr(mv[:, t, :], stats[:, t, :])
                        own(ins)
                        own.wait()
                        dve.tensor_scalar(var[:, :], mv[:, :, 1], 1e-6, None, ALU.add).then_inc(ln_step.sem, 1)
                        dve.wait_ge(ln_done.sem, ln_done(i, j + 1))
                        for t in range(TILES):
                            ins = dve.tensor_scalar(zn[:, t, :], z[:, t, :], mv[:, t, 0:1], rstd[:, t:t + 1],
                                                    ALU.subtract, ALU.mult)
                            if t % NT == NT - 1:
                                ins.then_inc(zn_ok.sem, 1)

                    normal(0)
                    dve.wait_ge(s_rows.sem, s_rows(i, 64))
                    rows = bqk_rows[:, :, :].rearrange("p s n -> p (s n)")
                    own(dve.tensor_copy(b_hi[:, :], rows))
                    own.wait()
                    own(dve.tensor_tensor(b_rest[:, :], rows, b_hi[:, :], ALU.subtract))
                    own.wait()
                    own(dve.tensor_copy(b_mid[:, :], b_rest[:, :]))
                    own.wait()
                    own(dve.tensor_tensor(b_lo[:, :], b_rest[:, :], b_mid[:, :], ALU.subtract))
                    own(dve.tensor_scalar(b_sum[:, :], b_hi[:, :], row_is[:, 0:1], None, ALU.mult))
                    own.wait()
                    own(dve.scalar_tensor_tensor(out=b_rest[:, :], in0=b_mid[:, :], scalar=row_is[:, 1:2],
                                                 in1=b_sum[:, :], op0=ALU.mult, op1=ALU.add))
                    own.wait()
                    dve.scalar_tensor_tensor(out=b_parts[:, :], in0=b_lo[:, :], scalar=row_is[:, 2:3],
                                             in1=b_rest[:, :], op0=ALU.mult, op1=ALU.add).then_inc(b_ok.sem, 1)
                    dve.wait_ge(fold_ps.sem, fold_ps(i, 4))
                    dve.tensor_copy(bqfg_rows[:, :], bank[7][:, 0:W])
                    dve.tensor_tensor(bpf_rows[:, :], bank[7][:, W:W + D], bf_rows[:, :], ALU.add).then_inc(fold_sb.sem, 1)
                    dve.wait_ge(fold_sb.sem, fold_sb(i, 4))
                    for t in range(TILES):
                        dve.wait_ge(k_ps.sem, k_ps(i, t + 1))
                        dve.bn_stats(kstats[:, t, :], bank[4 + t % 2][:, 0:ADIM]).then_inc(k_sq.sem, 1)
                        dve.wait_ge(f_ps.sem, f_ps(i, t + 1))
                        dve.tensor_tensor(qf[:, t, :], bank[6 + t % 2][:, 0:W], bqfg_rows[:, :], ALU.add).then_inc(f_sb.sem, 1)
                    dve.wait_ge(s_w[0].sem, s_w[0](i, 144))
                    dve.wait_ge(k_sq.sem, k_sq(i, TILES))
                    dve.sem_inc(s_go, 1)
                    for t in range(TILES):
                        ins = dve.bn_aggr(kmv[:, t, :], kstats[:, t, :])
                    own(ins)
                    own.wait()
                    own(dve.tensor_tensor(ss[:, 1, :], kmv[:, :, 0], kmv[:, :, 0], ALU.mult))
                    own.wait()
                    own(dve.tensor_tensor(ss[:, 1, :], ss[:, 1, :], kmv[:, :, 1], ALU.add))
                    own.wait()
                    own(dve.tensor_scalar(ss[:, 1, :], ss[:, 1, :], float(ADIM), None, ALU.mult))
                    own.wait()
                    dve.wait_ge(q_sq.sem, q_sq(i, TILES))
                    dve.tensor_scalar(ss[:, :, :], ss[:, :, :], 1e-24, None, ALU.max).then_inc(ss_ok.sem, 1)
                    dve.wait_ge(inv_ok.sem, inv_ok(i, 1))
                    dve.wait_ge(f_sb.sem, f_sb(i, TILES))
                    own(dve.scalar_tensor_tensor(out=alpha[:, :], in0=qf[:, :, D], scalar=TOKEN_SCALE, in1=inv[:, 0, :],
                                                 op0=ALU.mult, op1=ALU.mult))
                    own.wait()
                    dve.tensor_tensor(token_sums[:, 0, :], alpha[:, :], alpha[:, :], ALU.mult)
                    dve.tensor_tensor(token_sums[:, 1, :], alpha[:, :], inv[:, 0, :], ALU.mult).then_inc(sums_ok.sem, 1)
                    dve.wait_ge(sums_ps.sem, sums_ps(i, 1))
                    own(dve.tensor_reduce(over[:, :, :], bank[0][:, 0:2 * TILES].rearrange("p (s b t) -> p s b t", s=2, b=B),
                                          AX.X, ALU.add))
                    own.wait()
                    dve.tensor_scalar(over[:, 0, :], over[:, 0, :], 1e-24, None, ALU.max).then_inc(over_ok.sem, 1)
                    own(dve.tensor_scalar(u[:, :], bank[0][:, 64:64 + B], ln[:, 0:1], None, ALU.mult))
                    own.wait()
                    own(dve.scalar_tensor_tensor(out=coef[:, :], in0=over[:, 1, :], scalar=ln[:, 1:2], in1=u[:, :],
                                                 op0=ALU.mult, op1=ALU.add))
                    own.wait()
                    dve.wait_ge(inva_ok.sem, inva_ok(i, 1))
                    own(dve.tensor_tensor(u[:, :], coef[:, :], inv_a[:, :], ALU.mult))
                    own.wait()
                    dve.tensor_tensor(coef[:, :], over[:, 1, :], inv_a[:, :], ALU.mult).then_inc(u_ok.sem, 1)
                    dve.wait_ge(g_ps.sem, g_ps(i, 1))
                    dve.wait_ge(u_ok.sem, u_ok(i, 1))
                    for c in range(C2):
                        ins = dve.scalar_tensor_tensor(out=G[:, c, :], in0=coef[:, :], scalar=bqkp[:, 0, c:c + 1],
                                                       in1=bank[1][:, B * c:B * c + B], op0=ALU.mult, op1=ALU.add)
                    ins.then_inc(g_ok.sem, 1)
                    dve.wait_ge(g_ok.sem, g_ok(i, 1))
                    for b in range(B):
                        dve.tensor_scalar(wG[:, 0, b, :], wpf[:, 0, :], G[:, 0, b:b + 1], None, ALU.mult)
                    for c in range(C2):
                        ins = dve.tensor_scalar(bkG[:, c, :], G[:, c, :], bqkp[:, 1, c:c + 1], None, ALU.mult)
                    ins.then_inc(wg_ok.sem, 1)
                    for t in range(TILES):
                        ins = dve.scalar_tensor_tensor(out=z[:, t, :], in0=qf[:, t, 0:D], scalar=inv[:, 0, t:t + 1],
                                                       in1=z[:, t, :], op0=ALU.mult, op1=ALU.add)
                    own(ins)
                    own.wait()
                    own(dve.tensor_tensor(z[:, :, :], z[:, :, :], bpf_rows[:, :].unsqueeze(1).to_broadcast([P, TILES, D]),
                                          ALU.add))
                    own.wait()
                    dve.wait_ge(m_ps.sem, m_ps(i, 2))
                    dve.tensor_copy(bkM_rows[:, :, :].rearrange("p b d -> p (b d)"), bank[5][:, :]).then_inc(bm_sb.sem, 1)
                    dve.wait_ge(bm_sb.sem, bm_sb(i, 1))
                    for b in range(B):
                        dve.wait_ge(kp_ps.sem, kp_ps(i, b + 1))
                        pk = bank[2 + b % 2][:, :].rearrange("p (t d) -> p t d", t=NT)
                        dve.tensor_tensor(kp4[:, b % 2, :, :], pk,
                                          bkM_rows[:, b, :].unsqueeze(1).to_broadcast([P, NT, D]), ALU.add
                                          ).then_inc(kp_read.sem, 1)
                        dve.wait_ge(kp_read.sem, kp_read(i, b + 1))
                        for t in range(NT):
                            tok = z[:, NT * b + t, :]
                            ins = dve.scalar_tensor_tensor(out=tok, in0=kp4[:, b % 2, t, :],
                                                           scalar=inv[:, 1, NT * b + t:NT * b + t + 1], in1=tok,
                                                           op0=ALU.mult, op1=ALU.add)
                    ins.then_inc(attn_free.sem, 1)
                    dve.wait_ge(attn_free.sem, attn_free(i, 2))
                    normal(1)
                    dve.wait_ge(s_w[1].sem, s_w[1](i, 96))
                    dve.wait_ge(zn_ok.sem, zn_ok(i, 2 * B))
                    own(dve.tensor_tensor(z[:, :, :], z[:, :, :], b2_rows[:, :].unsqueeze(1).to_broadcast([P, TILES, D]),
                                          ALU.add))
                    own.wait()
                    for b in range(B):
                        dve.wait_ge(out_ps.sem, out_ps(i, b + 1))
                        tok = z[:, NT * b:NT * b + NT, :]
                        dve.tensor_tensor(tok, bank[2 + b % 2][:, :].rearrange("p (t d) -> p t d", t=NT), tok,
                                          ALU.add).then_inc(out_read.sem, 1)
                    dve.wait_ge(out_read.sem, out_read(i, B))
                    dve.sem_inc(mlp_free.sem, 1)
                    own.end()
                dve.tensor_tensor(k.x[:, :, :], k.x[:, :, :], z[:, :, :], ALU.add)

            @block.tensor
            def _(pe):
                pe.wait_ge(s_made, 6)
                with pe.Fori(0, DEPTH) as i:
                    pe.wait_ge(s_w[0].sem, s_w[0](i, 144))
                    for m in range(C2):
                        for c in range(C2):
                            ins = pe.transpose(bank[6][:, ADIM * m + P * c:ADIM * m + P * c + P],
                                               wp[:, c, P * m:P * m + P], k.ident[:, :])
                    ins.then_inc(fold_ps.sem, 1)
                    for s in range(2):
                        for c in range(C2):
                            ins = pe.transpose(bank[7][:, ADIM * s + P * c:ADIM * s + P * c + P],
                                               wqk[:, s, P * c:P * c + P], k.ident[:, :])
                    ins.then_inc(fold_ps.sem, 1)
                    pe.wait_ge(fold_sb.sem, fold_sb(i, 2))
                    for c in range(C2):
                        for m in range(C2):
                            pe.matmul(bank[6][:, D * c:D * c + D], wpT[:, m, P * c:P * c + P], wfg[:, m, 0:D],
                                      start=m == 0, stop=m == C2 - 1)
                    for c in range(C2):
                        ins = pe.matmul(bank[6][:, C2 * D:C2 * D + W], wqkT[:, 0, c, :], wfg[:, c, :],
                                        start=c == 0, stop=c == C2 - 1)
                    ins.then_inc(fold_ps.sem, 1)
                    for c in range(C2):
                        pe.matmul(bank[7][:, 0:W], bqkp[:, 0, c:c + 1].to_broadcast([P, P]), wfg[:, c, :],
                                  start=c == 0, stop=c == C2 - 1)
                    for c in range(C2):
                        ins = pe.matmul(bank[7][:, W:W + D], bqkp[:, 2, c:c + 1].to_broadcast([P, P]), wfg[:, c, 0:D],
                                        start=c == 0, stop=c == C2 - 1)
                    ins.then_inc(fold_ps.sem, 1)

                    def turn(j):
                        for b in range(B):
                            n = B * j + b
                            pe.wait_ge(zn_ok.sem, zn_ok(i, n + 1))
                            if b >= 2:
                                pe.wait_ge(hT_sb.sem, hT_sb(i, n - 1))
                            for t in range(NT):
                                ins = pe.transpose(bank[b % 2][:, P * t:P * t + P], zn[:, NT * b + t, :], k.ident[:, :])
                            ins.then_inc(hT_ps.sem, 1)

                    turn(0)
                    pe.wait_ge(b_ok.sem, b_ok(i, 1))
                    pe.wait_ge(fold_sb.sem, fold_sb(i, 4))
                    for t in range(TILES):
                        b = t // NT
                        if t % NT == 0:
                            pe.wait_ge(hT_sb.sem, hT_sb(i, b + 1))
                        lhs = hT[:, b, P * (t % NT):P * (t % NT) + P]
                        for s, base, ps, rd in ((0, 2, q_ps, q_sq), (1, 4, k_ps, k_sq)):
                            if t >= 2:
                                pe.wait_ge(rd.sem, rd(i, t - 1))
                            out = bank[base + t % 2][:, 0:ADIM]
                            pe.matmul(out, lhs, wqk[:, s, :], start=True, stop=False)
                            pe.matmul(out, three[:, :], b_parts[:, ADIM * s:ADIM * s + ADIM], start=False,
                                      stop=True).then_inc(ps.sem, 1)
                        if t >= 2:
                            pe.wait_ge(f_sb.sem, f_sb(i, t - 1))
                        pe.matmul(bank[6 + t % 2][:, 0:W], lhs, wqfg[:, :], start=True, stop=True).then_inc(f_ps.sem, 1)
                    pe.wait_ge(sums_ok.sem, sums_ok(i, 1))
                    pe.matmul(bank[0][:, 0:2 * TILES], ones[:, :], token_sums[:, :, :].rearrange("p s t -> p (s t)"),
                              start=True, stop=True)
                    for b in range(B):
                        for t in range(NT):
                            ins = pe.matmul(bank[0][:, 64 + b:65 + b], zn[:, NT * b + t, :],
                                            token_sums[:, 1, NT * b + t:NT * b + t + 1], start=t == 0, stop=t == NT - 1)
                    ins.then_inc(sums_ps.sem, 1)
                    pe.wait_ge(u_ok.sem, u_ok(i, 1))
                    for c in range(C2):
                        ins = pe.matmul(bank[1][:, B * c:B * c + B], wqk[:, 0, P * c:P * c + P], u[:, :],
                                        start=True, stop=True)
                    ins.then_inc(g_ps.sem, 1)
                    pe.wait_ge(wg_ok.sem, wg_ok(i, 2))
                    for b in range(B):
                        for c in range(C2):
                            ins = pe.matmul(bank[4][:, D * b:D * b + D], wqkT[:, 1, c, :], wG[:, c, b, :],
                                            start=c == 0, stop=c == C2 - 1)
                    ins.then_inc(m_ps.sem, 1)
                    for b in range(B):
                        for c in range(C2):
                            ins = pe.matmul(bank[5][:, D * b:D * b + D], bkG[:, c, b:b + 1].to_broadcast([P, P]),
                                            wpf[:, c, :], start=c == 0, stop=c == C2 - 1)
                    ins.then_inc(m_ps.sem, 1)
                    pe.wait_ge(m_sb.sem, m_sb(i, 1))
                    for b in range(B):
                        if b >= 2:
                            pe.wait_ge(kp_read.sem, kp_read(i, b - 1))
                        for t in range(NT):
                            ins = pe.matmul(bank[2 + b % 2][:, P * t:P * t + P], hT[:, b, P * t:P * t + P], M[:, b, :],
                                            start=True, stop=True)
                        ins.then_inc(kp_ps.sem, 1)
                    turn(1)
                    pe.wait_ge(s_w[1].sem, s_w[1](i, 96))

                    def up(b):
                        pe.wait_ge(hT_sb.sem, hT_sb(i, B + b + 1))
                        for c in range(CH):
                            if b > 0:
                                pe.wait_ge(hid_sb.sem, hid_sb(i, CH * (b - 1) + c + 1))
                            pe.matmul(bank[4 + c][:, :], w1[:, P * c:P * c + P], hT[:, b, :], start=True,
                                      stop=True).then_inc(hid_ps.sem, 1)

                    def down(b):
                        pe.wait_ge(hid_sb.sem, hid_sb(i, CH * (b + 1)))
                        if b >= 2:
                            pe.wait_ge(out_read.sem, out_read(i, b - 1))
                        for t in range(NT):
                            for c in range(CH):
                                ins = pe.matmul(bank[2 + b % 2][:, P * t:P * t + P], hidden[:, b % 2, c, P * t:P * t + P],
                                                w2[:, c, :], start=c == 0, stop=c == CH - 1)
                        ins.then_inc(out_ps.sem, 1)

                    up(0)
                    for b in range(B):
                        if b + 1 < B:
                            up(b + 1)
                        down(b)


def whole(nc, k, a):
    attention(nc, k, "mla1", True)
    experts(nc, k, a, "moe1")
    attention(nc, k, "att", False)
    attention(nc, k, "mla2", True)
    experts(nc, k, a, "moe2")
    mosa(nc, k, a, "mosa1")
    additive(nc, k, a)
    mosa(nc, k, a, "mosa2")


def macaron_kernel(nc, out, **a):
    with ExitStack() as ctx:
        k = Kernel()
        open_buffers(nc, ctx, k)
        setup(nc, k, a)
        whole(nc, k, a)
        stored = ctx.enter_context(nc.semaphore("stored"))
        with nc.Block() as block:
            @block.sync
            def _(sp):
                sp.dma_start(out.rearrange("b (t p) d -> p (b t) d", p=P), k.x[:, :, :]).then_inc(stored, 16)
                sp.wait_ge(stored, 16)


_INS = ["L0_attn_x", "L0_attn_w_qkv", "L0_attn_w_proj", "L0_attn_b_proj", "L0_ffn_g1", "L0_ffn_Wq", "L0_ffn_Wdkv",
        "L0_ffn_Wuk", "L0_ffn_Wuv", "L0_ffn_Wo", "L0_ffn_g2", "L0_ffn_gate_w", "L0_ffn_w1", "L0_ffn_w2",
        "L1_attn_ln1_g", "L1_attn_ln1_b", "L1_attn_Wq", "L1_attn_bq", "L1_attn_Wk", "L1_attn_bk", "L1_attn_w_g",
        "L1_attn_Wp", "L1_attn_bp", "L1_attn_Wf", "L1_attn_bf", "L1_attn_ln2_g", "L1_attn_ln2_b", "L1_attn_W1",
        "L1_attn_b1", "L1_attn_W2", "L1_attn_b2", "L1_ffn_Wr", "L1_ffn_Wqkv", "L1_ffn_Wo"]


def kernel(**inputs):
    import concourse.bacc as _bacc
    from concourse.bass_utils import run_bass_kernel_spmd as _run

    nc = _bacc.Bacc("TRN2", target_bir_lowering=False, num_devices=1)
    arrays, args = {}, {}
    for name in _INS + ["rope"]:
        arr = np.ascontiguousarray(rope_table() if name == "rope" else inputs[name])
        arrays[f"in_{name}"] = arr
        args[name] = nc.dram_tensor(f"in_{name}", arr.shape, mybir.dt.from_np(arr.dtype), kind="ExternalInput").ap()
    out = nc.dram_tensor("out_0", (B, N, D), F32, kind="ExternalOutput").ap()
    macaron_kernel(nc, out, **args)
    r = _run(nc, [arrays], core_ids=[0])
    return r.results[0]["out_0"]
```

```python
from contextlib import ExitStack

import numpy as np

import concourse.bass as bass
from concourse import mybir

P = 128
B = 4
N = 512
D = 128
NT = N // P
TILES = B * NT
H = 16
HD = D // H
QUADS = H // 4
SLOT = 64
EXPERTS = 8
EXP_DIM = 256
DEPTH = 4
ADIM = 256
HID = 512
MEXP = 8
MK = 64
ROT = 64
NEG = -1.0e30

ALU = mybir.AluOpType
ACT = mybir.ActivationFunctionType
F32 = mybir.dt.float32
BF16 = mybir.dt.bfloat16
I32 = mybir.dt.int32
AX = mybir.AxisListType


class Signal:

    def __init__(self, sem, per):
        self.sem, self.per = sem, per

    def __call__(self, b, k):
        return b * self.per + k


class Chain:

    def __init__(self, eng, sem, per):
        self.eng, self.sem, self.per, self.n, self.b = eng, sem, per, 0, 0

    def start(self, b):
        self.b, self.n = b, 0

    def __call__(self, ins):
        ins.then_inc(self.sem, 1)
        self.n += 1

    def wait(self):
        self.eng.wait_ge(self.sem, self.b * self.per + self.n)

    def wait_apart(self, go):
        self.wait()
        self.eng.sem_inc(go, 1)

    def end(self):
        assert self.n == self.per, (self.sem.name, self.n)


def take_semaphore(nc, ctx, name):
    handle = nc.alloc_semaphore(name)
    ctx.callback(lambda: nc.clear_and_free_semaphores([handle]))
    return handle


def end_module(nc):
    nc.all_engine_barrier()


class Kernel:
    pass


def open_buffers(nc, ctx, k):
    def sb(name, shape, dt=F32):
        return ctx.enter_context(nc.sbuf_tensor(name, shape, dt))

    k.x = sb("x", [P, TILES, D])
    k.y = sb("y", [P, TILES, D])
    k.ident = sb("ident", [P, P])
    k.identb = sb("identb", [P, P], BF16)
    k.mask_qk = sb("mask_qk", [P, P], BF16)
    k.mask_kq = sb("mask_kq", [P, P], BF16)
    k.half = sb("half", [P, TILES])
    k.w_mla = sb("w_mla", [P, 3 * D])
    k.w_mla_out = sb("w_mla_out", [P, D])
    k.w_att = sb("w_att", [P, 3 * D])
    k.w_att_out = sb("w_att_out", [P, D])
    k.b_att = sb("b_att", [P, D])
    k.bank = [ctx.enter_context(nc.psum_tensor(f"bank{i}", [P, 512], F32)) for i in range(8)]


def setup(nc, k, a):
    with ExitStack() as ctx:
        ctx.callback(end_module, nc)

        def sb(name, shape, dt=F32):
            return ctx.enter_context(nc.sbuf_tensor(name, shape, dt))

        def sem(name):
            return take_semaphore(nc, ctx, name)

        wdkv = sb("wdkv", [P, 64])
        wukv = sb("wukv", [64, 2 * D])
        wdkvT = sb("wdkvT", [64, P])
        g1 = sb("g1", [P, 1])
        loaded, weights, consts, ident_ok, step, ps, evac, done = (
            sem(n) for n in ("x_loaded", "weights_loaded", "consts_made", "ident_made", "setup_step",
                             "fold_ps", "fold_sb", "fold_done"))
        with nc.Block() as block:
            @block.sync
            def _(sp):
                sp.dma_start(wdkv[:, :], a["L0_ffn_Wdkv"]).then_inc(weights, 16)
                sp.dma_start(wukv[:, 0:D], a["L0_ffn_Wuk"]).then_inc(weights, 16)
                sp.dma_start(wukv[:, D:2 * D], a["L0_ffn_Wuv"]).then_inc(weights, 16)
                sp.dma_start(g1[:, :], a["L0_ffn_g1"].rearrange("(p o) -> p o", o=1)).then_inc(weights, 16)
                sp.dma_start(k.w_mla[:, 0:D], a["L0_ffn_Wq"]).then_inc(weights, 16)
                sp.dma_start(k.w_mla_out[:, :], a["L0_ffn_Wo"]).then_inc(weights, 16)
                sp.dma_start(k.w_att[:, :], a["L0_attn_w_qkv"]).then_inc(weights, 16)
                sp.dma_start(k.w_att_out[:, :], a["L0_attn_w_proj"]).then_inc(weights, 16)
                sp.dma_start(k.b_att[:, :], a["L0_attn_b_proj"].partition_broadcast(P)).then_inc(weights, 16)
                sp.wait_ge(loaded, 16)
                sp.wait_ge(weights, 16 * 9)

            @block.scalar
            def _(act):
                act.dma_start(k.x[:, :, :], a["L0_attn_x"].rearrange("b (t p) d -> p (b t) d", p=P)).then_inc(loaded, 16)

            @block.gpsimd
            def _(pool):
                pool.memset(k.ident[:, :], 0.0).then_inc(consts, 1)
                pool.memset(k.mask_qk[:, :], 0.0).then_inc(consts, 1)
                pool.memset(k.mask_kq[:, :], 0.0).then_inc(consts, 1)
                pool.memset(k.half[:, :], -0.5).then_inc(consts, 1)
                pool.wait_ge(consts, 4)
                pool.affine_select(out=k.ident[:, :], in_=k.ident[:, :], compare_op=ALU.not_equal, fill=1.0,
                                   base=0, pattern=[[-1, P]], channel_multiplier=1).then_inc(ident_ok, 1)
                pool.affine_select(out=k.mask_qk[:, :], in_=k.mask_qk[:, :], compare_op=ALU.is_ge, fill=NEG,
                                   base=0, pattern=[[-1, P]], channel_multiplier=1).then_inc(ident_ok, 1)
                pool.affine_select(out=k.mask_kq[:, :], in_=k.mask_kq[:, :], compare_op=ALU.is_ge, fill=NEG,
                                   base=0, pattern=[[1, P]], channel_multiplier=-1).then_inc(ident_ok, 1)
                pool.wait_ge(ident_ok, 3)
                pool.tensor_copy(k.identb[:, :], k.ident[:, :]).then_inc(consts, 1)

            @block.tensor
            def _(pe):
                pe.wait_ge(ident_ok, 3)
                pe.wait_ge(weights, 16 * 9)
                pe.transpose(k.bank[0][0:64, 0:P], wdkv[:, :], k.ident[:, :]).then_inc(ps, 1)
                pe.wait_ge(evac, 1)
                pe.matmul(k.bank[1][:, 0:2 * D], wdkvT[:, :], wukv[:, :], start=True, stop=True).then_inc(ps, 1)

            @block.vector
            def _(dve):
                dve.wait_ge(ps, 1)
                dve.tensor_copy(wdkvT[:, :], k.bank[0][0:64, 0:P]).then_inc(evac, 1)
                dve.wait_ge(weights, 16 * 9)
                dve.tensor_scalar(k.w_mla[:, 0:D], k.w_mla[:, 0:D], g1[:, 0:1], HD ** -0.5,
                                  ALU.mult, ALU.mult).then_inc(done, 1)
                dve.tensor_scalar(k.w_att[:, 0:D], k.w_att[:, 0:D], HD ** -0.5, None, ALU.mult).then_inc(done, 1)
                dve.wait_ge(ps, 2)
                dve.tensor_scalar(k.w_mla[:, D:3 * D], k.bank[1][:, 0:2 * D], g1[:, 0:1], None,
                                  ALU.mult).then_inc(done, 1)


def attention(nc, k, name, causal):
    with ExitStack() as ctx:
        ctx.callback(end_module, nc)

        def sb(n, shape, dt=F32):
            return ctx.enter_context(nc.sbuf_tensor(f"{name}_{n}", shape, dt))

        def sem(n):
            return take_semaphore(nc, ctx, f"{name}_{n}")

        def signal(n, per):
            return Signal(sem(n), per)

        w_in, w_out = (k.w_mla, k.w_mla_out) if causal else (k.w_att, k.w_att_out)
        eps = 1e-5
        stats = sb("stats", [P, TILES, 6])
        mv = sb("mv", [P, TILES, 2])
        half2 = sb("half2", [P, 2, TILES])
        var = sb("var", [P, 2, TILES])
        scale = sb("scale", [P, 2, TILES])
        h = sb("h", [P, NT, D])
        hT = sb("hT", [P, N])
        qk32 = sb("qk32", [P, NT, 2, D])
        v_new = sb("v_new", [P, NT, D])
        rest = sb("rest", [P, NT, 2, D])
        hi = sb("hi", [P, NT, 2, D], BF16)
        mid = sb("mid", [P, NT, 2, D], BF16)
        lo = sb("lo", [P, NT, 2, D], BF16)
        q_parts = sb("q_parts", [P, NT, H, SLOT], BF16)
        k_parts = sb("k_parts", [P, NT, H, SLOT], BF16)
        v_ones = sb("v_ones", [P, NT, H, 32])
        qT_max = sb("qT_max", [P, 2, N], BF16)
        qT = sb("qT", [P, 2, 2, N], BF16)
        kT = sb("kT", [P, 2, 4, N], BF16)
        negmax = sb("negmax", [P, H, NT])
        nm_rest = sb("nm_rest", [P, H, NT])
        nm_hi = sb("nm_hi", [P, H, NT], BF16)
        nm_mid = sb("nm_mid", [P, H, NT], BF16)
        probs = sb("probs", [P, 2, 4, NT * N])
        oT = sb("oT", [P, 2, N])
        rsum = sb("rsum", [P, 2, NT, 4])
        o = sb("o", [P, NT, D])
        oTn = sb("oTn", [P, N])

        bank = k.bank
        TQ = bank[0][:, 0:256].bitcast(BF16)
        TK = bank[0][:, 256:512].bitcast(BF16)
        S1 = [bank[1], bank[2]]
        AV = bank[3]
        S2 = [bank[4], bank[5], bank[6]]
        X = bank[7]
        XQ = bank[7][:, 0:256].bitcast(BF16)

        if causal:
            at = {0: 0, 1: 512, 3: 896, 2: 1024}
            rounds = [r for j in range(4) for r in ([(j, 0, 0)], [(j, 1, 0), (j, 3, 384)])]
            rounds[4:4] = [[(0, 2, 0), (1, 2, 256)]]
            rounds.append([(2, 2, 0), (3, 2, 256)])
        else:
            at = {kt: 512 * kt for kt in range(NT)}
            rounds = [[(j, kt, 0)] for j in range(4) for kt in range(NT)]
        R = len(rounds)
        assert QUADS * R % 3 == 1
        PAIRS = H // 2

        def q_from(kt):
            return P * kt if causal else 0

        def keys(t):
            return P * (t + 1) if causal else N

        s_go, s_init, s_var, s_scale = sem("pool_go"), sem("init"), sem("var_done"), sem("scale_done")
        s_aggr = sem("aggr_done")
        h_ready = signal("h_ready", 1)
        hT_ps = signal("hT_ps", 1)
        hT_sb = signal("hT_sb", 1)
        qkv_ps = signal("qkv_ps", NT)
        qk_sb = signal("qk_sb", NT)
        v_sb = signal("v_sb", NT)
        v_placed = signal("v_placed", 1)
        hi_sb = signal("hi_sb", 1)
        s_stats = sem("stats_done")
        rest_sb = signal("rest_sb", 2)
        parts_placed = signal("parts_placed", 1)
        mid_sb = signal("mid_sb", 1)
        turned_max = signal("turned_max", PAIRS)
        q_max_sb = signal("q_max_sb", PAIRS)
        k_sb = signal("k_sb", PAIRS)
        max_ps = signal("max_ps", PAIRS * 2 * NT)
        max_read = signal("max_read", PAIRS * 2 * NT)
        max_part = signal("max_part", 3 * PAIRS)
        max_rows = signal("max_rows", PAIRS)
        turned_q = signal("turned_q", PAIRS)
        q_sb = signal("q_sb", PAIRS)
        score_ps = signal("score_ps", QUADS * R)
        probs_sb = signal("probs_sb", QUADS * R)
        av_ps = signal("av_ps", QUADS)
        av_sb = signal("av_sb", QUADS)
        turned_o = signal("turned_o", QUADS)
        sum_inv = signal("sum_inv", QUADS)
        o_sb = signal("o_sb", QUADS)
        oT_ps = signal("oT_ps", 1)
        oT_sb = signal("oT_sb", 1)
        proj_ps = signal("proj_ps", 1)
        out_sb = signal("out_sb", 2)

        def fronts(d, g):
            a, b = 2 * g, 2 * g + 1
            return [("turn_max", d, a), ("max", d, a, 0), ("max", d, a, 1), ("turn_max", d, b), ("max", d, a, 2),
                    ("max", d, a, 3), ("max_rows", d, a), ("max", d, b, 0), ("max", d, b, 1), ("max", d, b, 2), ("turn_q", d, a), ("max", d, b, 3), ("max_rows", d, b)]

        def prep(d):
            return [("h", d)] + [("qkv", d, t) for t in range(NT)] + [("split", d)]

        def after(d, g):
            return [("av", d, g, kt) for kt in range(NT)] + [("o", d, g)]

        def merged(a, b):
            a, end = a[:-4], a[-4:]
            out, n = [], 0
            for i, step in enumerate(a):
                out.append(step)
                while n < len(b) and n * len(a) < (i + 1) * len(b):
                    out.append(b[n])
                    n += 1
            return out + b[n:] + end

        def beside(d, g, side):
            side = side[:LATE] + [("turn_q", d, 2 * g + 1)] + side[LATE:]
            out = []
            for r in range(R):
                out.append(("score", d, g, r))
                take = -(-len(side) // (R - r))
                out += side[:take]
                side = side[take:]
            return out

        LATE = 4
        quads = [beside(0, g, merged(fronts(0, g + 1), after(0, g - 1) if g else [])) for g in range(2)]
        tail = after(0, QUADS - 1) + [("turn_o", 0), ("proj", 0)]
        prologue = prep(0) + [("place", 0), ("place_v", 0)] + fronts(0, 0) + quads[0]
        steady = (quads[1] + beside(0, 2, merged(merged(fronts(0, 3), prep(1)[:4]) + prep(1)[4:], after(0, 1))) +
                  beside(0, 3, after(0, 2)[:LATE] + [("place", 1)] + merged(fronts(1, 0), after(0, 2)[LATE:])) +
                  beside(1, 0, merged(fronts(1, 1), tail[:NT] + [("place_v", 1)] + tail[NT:])))
        epilogue = (quads[1] + beside(0, 2, merged(fronts(0, 3), after(0, 1))) +
                    beside(0, 3, after(0, 2)) + tail)
        phases = (("first", prologue), ("loop", steady), ("last", epilogue))
        in_x = ("h", "qkv", "turn_q", "o", "turn_o", "proj")
        assert [s for s in prologue if s[0] in in_x][-1] == ("turn_q", 0, 2)
        assert [s for s in steady if s[0] in in_x][-1] == ("turn_q", 1, 2)

        def run(eng, does):
            for phase, steps in phases:
                if phase == "loop":
                    with eng.Fori(0, B - 1) as b:
                        play(b, steps, does, prologue, 0)
                else:
                    play(0 if phase == "first" else B - 1, steps, does,
                         [] if phase == "first" else steady, 0 if phase == "first" else 1)

        def play(b, steps, does, before, shift):
            last = [(s[0], s[1] - shift) + s[2:] for s in before if s[0] in in_x][-1:]
            for s in steps:
                if s[0] in does:
                    does[s[0]](b + s[1], *s[2:], **({"x_was": (b, last[0] if last else None)}
                                                    if s[0] in in_x and does is PE_DOES else {}))
                if s[0] in in_x:
                    last = [s]

        PE_DOES = {}

        def wait_x_free(eng, x_was):
            b, s = x_was
            if s is None:
                return
            b = b + s[1]
            if s[0] == "h":
                eng.wait_ge(hT_sb.sem, hT_sb(b, 1))
            elif s[0] == "qkv":
                eng.wait_ge(v_sb.sem, v_sb(b, s[2] + 1))
            elif s[0] == "turn_q":
                eng.wait_ge(q_sb.sem, q_sb(b, s[2] + 1))
            elif s[0] == "o":
                eng.wait_ge(o_sb.sem, o_sb(b, s[2] + 1))
            elif s[0] == "turn_o":
                eng.wait_ge(oT_sb.sem, oT_sb(b, 1))
            elif s[0] == "proj":
                eng.wait_ge(out_sb.sem, out_sb(b, 1))

        with nc.Block() as block:
            @block.sync
            def _(sp):
                sp.nop()

            @block.gpsimd
            def _(pool):
                pool.memset(half2[:, :, :], -0.5).then_inc(s_init, 1)
                pool.wait_ge(s_init, 1)
                for i, tiles in enumerate((slice(0, NT), slice(NT, TILES))):
                    pool.wait_ge(s_var, i + 1)
                    pool.tensor_tensor(scale[:, :, tiles], var[:, :, tiles], half2[:, :, tiles],
                                       ALU.pow).then_inc(s_scale, 1)
                    if i == 0:
                        pool.memset(kT[:, :, :, :], 0.0).then_inc(s_init, 1)
                pool.memset(v_ones[:, :, :, :], 0.0).then_inc(s_init, 1)
                pool.wait_ge(s_init, 3)
                pool.memset(v_ones[:, :, :, HD:HD + 1], 1.0).then_inc(s_init, 1)

                def wait_apart(s, value):
                    pool.wait_ge(s.sem, value)
                    pool.sem_inc(s_go, 1)

                def place_v_step(b):
                    wait_apart(v_sb, v_sb(b, NT))
                    wait_apart(av_ps, av_ps(b, 0)) if not isinstance(b, int) or b > 0 else None
                    pool.tensor_copy(v_ones[:, :, :, 0:HD],
                                     v_new[:, :, :].rearrange("p t (h e) -> p t h e", e=HD)).then_inc(v_placed.sem, 1)

                def max_rows_step(b, p):
                    hs = slice(2 * p, 2 * p + 2)

                    def rows(i):
                        return q_parts[:, :, hs, 48 + i].rearrange("p t h -> p h t")

                    wait_apart(max_read, max_read(b, 8 * (p + 1)))
                    pool.tensor_copy(nm_hi[:, hs, :], negmax[:, hs, :]).then_inc(max_part.sem, 1)
                    pool.wait_ge(max_part.sem, max_part(b, 3 * p + 1))
                    pool.tensor_tensor(nm_rest[:, hs, :], negmax[:, hs, :], nm_hi[:, hs, :],
                                       ALU.subtract).then_inc(max_part.sem, 1)
                    pool.tensor_copy(rows(0), nm_hi[:, hs, :])
                    wait_apart(max_part, max_part(b, 3 * p + 2))
                    pool.tensor_copy(nm_mid[:, hs, :], nm_rest[:, hs, :]).then_inc(max_part.sem, 1)
                    pool.wait_ge(max_part.sem, max_part(b, 3 * p + 3))
                    pool.tensor_tensor(rows(2), nm_rest[:, hs, :], nm_mid[:, hs, :], ALU.subtract)
                    pool.tensor_copy(rows(1), nm_mid[:, hs, :]).then_inc(max_rows.sem, 1)

                run(pool, { "place_v": place_v_step, "max_rows": max_rows_step})

            @block.scalar
            def _(act):
                def h_step(b):
                    act.wait_ge(hT_ps.sem, hT_ps(b, 1))
                    act.copy(hT[:, :], X[:, :]).then_inc(hT_sb.sem, 1)

                def qkv_step(b, t):
                    act.wait_ge(qkv_ps.sem, qkv_ps(b, t + 1))
                    act.copy(qk32[:, t, :, :].rearrange("p s d -> p (s d)"), X[:, 0:2 * D]).then_inc(qk_sb.sem, 1)
                    act.copy(v_new[:, t, :], X[:, 2 * D:3 * D]).then_inc(v_sb.sem, 1)

                def turn_max_step(b, p):
                    g, i = p // 2, 2 * (p % 2)
                    act.wait_ge(turned_max.sem, turned_max(b, p + 1))
                    if isinstance(b, int) and b == 0 and p == 0:
                        act.wait_ge(s_init, 2)
                    if not (isinstance(b, int) and b == 0 and g < 2):
                        act.wait_ge(score_ps.sem, score_ps(b, R * (g - 1)))
                        act.wait_ge(max_ps.sem, max_ps(b, 8 * (p - 1)))
                    act.copy(qT_max[:, p % 2, :], TQ[:, :]).then_inc(q_max_sb.sem, 1)
                    act.copy(kT[0:64, g % 2, i, :], TK[0:64, :])
                    act.copy(kT[64:128, g % 2, i + 1, :], TK[64:128, :]).then_inc(k_sb.sem, 1)

                def score_step(b, g, r):
                    n = R * g + r
                    act.wait_ge(score_ps.sem, score_ps(b, n + 1))
                    if r == 0 and not (isinstance(b, int) and b == 0 and g < 2):
                        act.wait_ge(av_ps.sem, av_ps(b, g - 1))
                    j, kt = rounds[r][0][:2]
                    if causal and kt == 2:
                        dst = probs[:, g % 2, j:j + 2, at[2]:at[2] + 256]
                        src = S2[n % 3][:, :].rearrange("p (j q) -> p j q", j=2)
                    else:
                        dst = probs[:, g % 2, j, at[kt]:at[kt] + N]
                        src = S2[n % 3][:, :]
                    act.activation(dst, src, ACT.Exp).then_inc(probs_sb.sem, 1)

                def av_step(b, g, kt):
                    if kt < NT - 1:
                        return
                    act.wait_ge(av_ps.sem, av_ps(b, g + 1))
                    act.copy(oT[:, g % 2, :], AV[:, :]).then_inc(av_sb.sem, 1)

                def turn_o_step(b):
                    act.wait_ge(oT_ps.sem, oT_ps(b, 1))
                    act.copy(oTn[:, :], X[:, :]).then_inc(oT_sb.sem, 1)

                run(act, {"h": h_step, "qkv": qkv_step, "turn_max": turn_max_step, "score": score_step,
                          "av": av_step, "turn_o": turn_o_step})

            @block.vector
            def _(dve):
                def variances(i, tiles):
                    for t in tiles:
                        ins = dve.bn_stats(stats[:, t, :], k.x[:, t, :])
                    ins.then_inc(s_stats, 1)
                    dve.wait_ge(s_stats, i + 1)
                    for t in tiles:
                        ins = dve.bn_aggr(mv[:, t, :], stats[:, t, :])
                    ins.then_inc(s_aggr, 1)
                    dve.wait_ge(s_aggr, i + 1)
                    own = slice(tiles[0], tiles[-1] + 1)
                    dve.tensor_scalar(var[:, 0, own], mv[:, own, 1], eps, None, ALU.add)
                    dve.tensor_scalar(var[:, 1, own], mv[:, own, 1], 1.0 + 1e-6 if causal else 1.0,
                                      1e-6 * eps if causal else eps, ALU.mult, ALU.add).then_inc(s_var, 1)

                variances(0, range(NT))
                dve.memset(q_parts[:, :, :, 51:SLOT], 0.0)
                dve.memset(k_parts[:, :, :, 51:SLOT], 0.0)
                dve.memset(k_parts[:, :, :, 48:51], 1.0)

                def h_step(b):
                    first = isinstance(b, int) and b == 0
                    dve.wait_ge(s_scale, 1 if first else 2)
                    for t in range(NT):
                        tok = k.x[:, b * NT + t, :]
                        if causal:
                            dve.tensor_scalar(k.y[:, b * NT + t, :], tok, mv[:, b * NT + t, 0:1],
                                              scale[:, 0, bass.ds(b * NT + t, 1)], ALU.subtract, ALU.mult)
                        ins = dve.tensor_scalar(h[:, t, :], tok, mv[:, b * NT + t, 0:1],
                                                scale[:, 1, bass.ds(b * NT + t, 1)], ALU.subtract, ALU.mult)
                    ins.then_inc(h_ready.sem, 1)
                    if first:
                        variances(1, range(NT, TILES))

                def split_step(b):
                    dve.wait_ge(qk_sb.sem, qk_sb(b, NT))
                    dve.tensor_copy(hi[:, :, :, :], qk32[:, :, :, :]).then_inc(hi_sb.sem, 1)
                    dve.wait_ge(hi_sb.sem, hi_sb(b, 1))
                    dve.tensor_tensor(rest[:, :, :, :], qk32[:, :, :, :], hi[:, :, :, :],
                                      ALU.subtract).then_inc(rest_sb.sem, 1)
                    dve.wait_ge(rest_sb.sem, rest_sb(b, 1))
                    dve.tensor_copy(mid[:, :, :, :], rest[:, :, :, :]).then_inc(mid_sb.sem, 1)
                    dve.wait_ge(mid_sb.sem, mid_sb(b, 1))
                    dve.tensor_tensor(lo[:, :, :, :], rest[:, :, :, :], mid[:, :, :, :],
                                      ALU.subtract).then_inc(rest_sb.sem, 1)

                def place_step(b):
                    dve.wait_ge(rest_sb.sem, rest_sb(b, 2))
                    dve.memset(q_parts[:, :, :, 48:51], 0.0)
                    for dst, i, slots in ((q_parts, 0, (hi, hi, hi, mid, mid, lo)), (k_parts, 1, (hi, mid, lo, hi, mid, hi))):
                        for s, part in enumerate(slots):
                            ins = dve.tensor_copy(dst[:, :, :, 8 * s:8 * s + 8],
                                                  part[:, :, i, :].rearrange("p t (h e) -> p t h e", e=HD))
                    ins.then_inc(parts_placed.sem, 1)

                def max_step(b, p, t):
                    for j in range(2):
                        n = 8 * p + 2 * t + j
                        dve.wait_ge(max_ps.sem, max_ps(b, n + 1))
                        dve.tensor_reduce(negmax[:, 2 * p + j, t:t + 1], S1[j][:, 0:keys(t)], AX.X, ALU.max,
                                          negate=True).then_inc(max_read.sem, 1)

                def turn_q_step(b, p):
                    dve.wait_ge(turned_q.sem, turned_q(b, p + 1))
                    if not (isinstance(b, int) and b == 0 and p < 4):
                        dve.wait_ge(score_ps.sem, score_ps(b, R * (p // 2 - 1)))
                    dve.tensor_copy(qT[:, (p // 2) % 2, p % 2, :], XQ[:, :]).then_inc(q_sb.sem, 1)

                def o_step(b, g):
                    dve.wait_ge(turned_o.sem, turned_o(b, g + 1))
                    Xo = X[:, :].rearrange("p (t j e) -> p t j e", t=NT, j=4)
                    dve.reciprocal(rsum[:, g % 2, :, :], Xo[:, :, :, HD]).then_inc(sum_inv.sem, 1)
                    dve.wait_ge(sum_inv.sem, sum_inv(b, g + 1))
                    oo = o[:, :, :].rearrange("p t (g j e) -> p t g j e", g=QUADS, j=4)
                    dve.tensor_tensor(oo[:, :, g, :, :], Xo[:, :, :, 0:HD],
                                      rsum[:, g % 2, :, :].unsqueeze(3).to_broadcast([P, NT, 4, HD]),
                                      ALU.mult).then_inc(o_sb.sem, 1)

                def proj_step(b):
                    dve.wait_ge(proj_ps.sem, proj_ps(b, 1))
                    dst = k.y if causal else k.x
                    tok = dst[:, bass.ds(b * NT, NT), :]
                    dve.tensor_tensor(tok, X[:, :].rearrange("p (t d) -> p t d", t=NT), tok,
                                      ALU.add).then_inc(out_sb.sem, 1)
                    dve.wait_ge(out_sb.sem, out_sb(b, 1))
                    if causal:
                        dve.sem_inc(out_sb.sem, 1)
                    else:
                        dve.tensor_tensor(tok, k.b_att[:, :].unsqueeze(1).to_broadcast([P, NT, D]), tok,
                                          ALU.add).then_inc(out_sb.sem, 1)

                run(dve, {"h": h_step, "split": split_step, "place": place_step, "max": max_step, "turn_q": turn_q_step,
                          "o": o_step, "proj": proj_step})

            @block.tensor
            def _(pe):
                def h_step(b, x_was):
                    pe.wait_ge(h_ready.sem, h_ready(b, 1))
                    wait_x_free(pe, x_was)
                    for t in range(NT):
                        ins = pe.transpose(X[:, P * t:P * t + P], h[:, t, :], k.ident[:, :])
                    ins.then_inc(hT_ps.sem, 1)

                def qkv_step(b, t, x_was):
                    wait_x_free(pe, x_was)
                    if t == 0:
                        pe.wait_ge(hT_sb.sem, hT_sb(b, 1))
                    pe.matmul(X[:, 0:3 * D], hT[:, P * t:P * t + P], w_in[:, :],
                              start=True, stop=True).then_inc(qkv_ps.sem, 1)

                def turn(dst, parts, p):
                    for t in range(NT):
                        ins = pe.transpose(dst[:, P * t:P * t + P],
                                           parts[:, t, 2 * p:2 * p + 2, :].rearrange("p h s -> p (h s)"),
                                           k.identb[:, :])
                    return ins

                def turn_max_step(b, p):
                    if p == 0:
                        pe.wait_ge(parts_placed.sem, parts_placed(b, 1))
                    if not (isinstance(b, int) and b == 0 and p == 0):
                        pe.wait_ge(k_sb.sem, k_sb(b, p))
                    turn(TQ, q_parts, p)
                    turn(TK, k_parts, p).then_inc(turned_max.sem, 1)

                def max_step(b, p, t):
                    if t == 0:
                        pe.wait_ge(k_sb.sem, k_sb(b, p + 1))
                    for j in range(2):
                        n = 8 * p + 2 * t + j
                        if not (isinstance(b, int) and b == 0 and n < 2):
                            pe.wait_ge(max_read.sem, max_read(b, n - 1))
                        kt = kT[:, (p // 2) % 2, 2 * (p % 2) + j, 0:keys(t)]
                        ins = pe.matmul(S1[j][:, 0:keys(t)], qT_max[:, p % 2, P * t:P * t + P], kt,
                                        start=True, stop=not causal)
                        if causal:
                            ins = pe.matmul(S1[j][:, P * t:P * t + P], k.identb[:, :], k.mask_qk[:, :],
                                            start=False, stop=True)
                        ins.then_inc(max_ps.sem, 1)

                def turn_q_step(b, p, x_was):
                    pe.wait_ge(max_rows.sem, max_rows(b, p + 1))
                    wait_x_free(pe, x_was)
                    turn(XQ, q_parts, p).then_inc(turned_q.sem, 1)

                def score_step(b, g, r):
                    n = R * g + r
                    if r == 0:
                        pe.wait_ge(q_sb.sem, q_sb(b, 2 * g + 1))
                    elif rounds[r][0][0] == 2 and rounds[r - 1][0][0] < 2:
                        pe.wait_ge(q_sb.sem, q_sb(b, 2 * g + 2))
                    if not (isinstance(b, int) and b == 0 and n < 3):
                        pe.wait_ge(probs_sb.sem, probs_sb(b, n - 2 if n else 0))
                    for j, kt, col in rounds[r]:
                        w = N - q_from(kt)
                        out = S2[n % 3]
                        ins = pe.matmul(out[:, col:col + w], kT[:, g % 2, j, P * kt:P * kt + P],
                                        qT[:, g % 2, j // 2, q_from(kt):N], start=True, stop=not causal)
                        if causal:
                            ins = pe.matmul(out[:, col:col + P], k.identb[:, :], k.mask_kq[:, :],
                                            start=False, stop=True)
                    ins.then_inc(score_ps.sem, 1)

                def av_step(b, g, kt):
                    if kt == 0:
                        pe.wait_ge(probs_sb.sem, probs_sb(b, R * (g + 1)))
                        if g == 0:
                            pe.wait_ge(v_placed.sem, v_placed(b, 1))
                        if not (isinstance(b, int) and b == 0 and g == 0):
                            pe.wait_ge(av_sb.sem, av_sb(b, g))
                    for j in range(4):
                        w = N - q_from(kt)
                        ins = pe.matmul(AV[32 * j:32 * j + 32, q_from(kt):N], v_ones[:, kt, 4 * g + j, :],
                                        probs[:, g % 2, j, at[kt]:at[kt] + w], start=kt == 0, stop=kt == NT - 1)
                    if kt == NT - 1:
                        ins.then_inc(av_ps.sem, 1)

                def o_step(b, g, x_was):
                    pe.wait_ge(av_sb.sem, av_sb(b, g + 1))
                    wait_x_free(pe, x_was)
                    for t in range(NT):
                        ins = pe.transpose(X[:, P * t:P * t + P], oT[:, g % 2, P * t:P * t + P], k.ident[:, :])
                    ins.then_inc(turned_o.sem, 1)

                def turn_o_step(b, x_was):
                    pe.wait_ge(o_sb.sem, o_sb(b, QUADS))
                    wait_x_free(pe, x_was)
                    for t in range(NT):
                        ins = pe.transpose(X[:, P * t:P * t + P], o[:, t, :], k.ident[:, :])
                    ins.then_inc(oT_ps.sem, 1)

                def proj_step(b, x_was):
                    pe.wait_ge(oT_sb.sem, oT_sb(b, 1))
                    wait_x_free(pe, x_was)
                    for t in range(NT):
                        ins = pe.matmul(X[:, P * t:P * t + P], oTn[:, P * t:P * t + P], w_out[:, :],
                                        start=True, stop=True)
                    ins.then_inc(proj_ps.sem, 1)

                PE_DOES.update({"h": h_step, "qkv": qkv_step, "turn_max": turn_max_step, "max": max_step,
                                "turn_q": turn_q_step, "score": score_step, "av": av_step, "o": o_step,
                                "turn_o": turn_o_step, "proj": proj_step})
                run(pe, PE_DOES)


def experts(nc, k, a, name):
    with ExitStack() as ctx:
        ctx.callback(end_module, nc)

        def sb(n, shape, dt=F32):
            return ctx.enter_context(nc.sbuf_tensor(f"{name}_{n}", shape, dt))

        def sem(n):
            return take_semaphore(nc, ctx, f"{name}_{n}")

        def signal(n, per):
            return Signal(sem(n), per)

        CH = EXP_DIM // P
        FAR = -3.0e38
        TAKEN = 3.0e38
        w1 = sb("w1", [P, EXPERTS, EXP_DIM])
        w2 = sb("w2", [P, EXPERTS, CH, D])
        gate_w = sb("gate_w", [P, EXPERTS])
        g2 = sb("g2", [P, 1])
        squares = sb("squares", [P, TILES, D])
        ms = sb("ms", [P, TILES])
        rms = sb("rms", [P, TILES])
        h = sb("h", [P, NT, D])
        hT = sb("hT", [P, N])
        logits = sb("logits", [P, NT, 16])
        left = sb("left", [P, NT, 16])
        best = sb("best", [P, NT, 8])
        drop = sb("drop", [P, NT, 8])
        taken = sb("taken", [P, NT, EXPERTS])
        away = sb("away", [P, NT, EXPERTS])
        share = sb("share", [P, NT, EXPERTS])
        total = sb("total", [P, NT])
        gates = sb("gates", [P, NT, EXPERTS])
        hidden = sb("hidden", [P, 2, CH, N])
        bank = k.bank
        T, G = bank[0], bank[1]

        s_weighed, s_go = sem("weighed"), sem("go")
        s_w, s_init, s_ms, s_rms, s_sq = sem("weights"), sem("init"), sem("rms_step"), sem("rms_done"), sem("squares_done")
        h_ready = signal("h_ready", 1)
        hT_ps = signal("hT_ps", 1)
        hT_sb = signal("hT_sb", 1)
        gate_ps = signal("gate_ps", 1)
        away_sb = signal("away_sb", 1)
        share_sb = signal("share_sb", 1)
        hid_ps = signal("hid_ps", EXPERTS)
        hid_sb = signal("hid_sb", EXPERTS)
        out_ps = signal("out_ps", EXPERTS)

        with nc.Block() as block:
            @block.sync
            def _(sp):
                sp.dma_start(gate_w[:, :], a["L0_ffn_gate_w"]).then_inc(s_w, 16)
                sp.dma_start(g2[:, :], a["L0_ffn_g2"].rearrange("(p o) -> p o", o=1)).then_inc(s_w, 16)
                sp.dma_start(w1[:, :, :], a["L0_ffn_w1"].rearrange("e d h -> d e h")).then_inc(s_w, 16)
                sp.dma_start(w2[:, :, :, :], a["L0_ffn_w2"].rearrange("e (c p) d -> p e c d", p=P)).then_inc(s_w, 16)
                sp.wait_ge(s_w, 64)

            @block.gpsimd
            def _(pool):
                pool.memset(drop[:, :, :], FAR).then_inc(s_init, 1)
                pool.memset(logits[:, :, :], FAR).then_inc(s_init, 1)
                pool.wait_ge(s_sq, 2)
                pool.tensor_scalar(rms[:, :], ms[:, :], 1.0 / D, 1e-6, ALU.mult, ALU.add).then_inc(s_ms, 1)
                pool.wait_ge(s_ms, 1)
                pool.tensor_tensor(ms[:, :], rms[:, :], k.half[:, :], ALU.pow).then_inc(s_rms, 1)

            @block.scalar
            def _(act):
                for t in range(TILES // 2, TILES):
                    ins = act.activation(squares[:, t, :], k.y[:, t, :], ACT.Square, accum_out=ms[:, t:t + 1])
                ins.then_inc(s_sq, 1)
                act.wait_ge(s_w, 64)

                def copy_h(b):
                    act.wait_ge(hT_ps.sem, hT_ps(b, 1))
                    act.mul(hT[:, :], T[:, :], g2[:, 0:1]).then_inc(hT_sb.sem, 1)

                def batch(b, more):
                    for e in range(EXPERTS):
                        act.wait_ge(hid_ps.sem, hid_ps(b, e + 1))
                        if more and e == EXPERTS - 1:
                            copy_h(b + 1)
                        if e >= 2:
                            act.wait_ge(out_ps.sem, out_ps(b, e - 1))
                        for c in range(CH):
                            ins = act.activation(hidden[:, e % 2, c, :], bank[4 + 2 * (e % 2) + c][:, :], ACT.Silu)
                        ins.then_inc(hid_sb.sem, 1)
                        if e == 0:
                            act.wait_ge(away_sb.sem, away_sb(b, 1))
                            act.activation(share[:, :, :], away[:, :, :], ACT.Exp).then_inc(share_sb.sem, 1)

                copy_h(0)
                with act.Fori(0, B - 1) as b:
                    batch(b, True)
                batch(B - 1, False)

            @block.vector
            def _(dve):
                own = Chain(dve, sem("dve_step"), 9)
                weighed = Chain(dve, s_weighed, EXPERTS)
                for t in range(TILES // 2):
                    ins = dve.tensor_tensor_reduce(squares[:, t, :], k.y[:, t, :], k.y[:, t, :], 1.0, 0.0,
                                                   ALU.mult, ALU.add, ms[:, t:t + 1])
                ins.then_inc(s_sq, 1)
                dve.wait_ge(s_rms, 1)
                dve.wait_ge(s_init, 2)

                def scale_h(b):
                    for t in range(NT):
                        ins = dve.tensor_scalar(h[:, t, :], k.y[:, b * NT + t, :], ms[:, bass.ds(b * NT + t, 1)],
                                                None, ALU.mult)
                    ins.then_inc(h_ready.sem, 1)

                def batch(b, more):
                    own.start(b)
                    weighed.start(b)
                    dve.wait_ge(gate_ps.sem, gate_ps(b, 1))
                    own(dve.tensor_copy(logits[:, :, 0:EXPERTS],
                                        G[:, 0:NT * EXPERTS].rearrange("p (t e) -> p t e", t=NT)))
                    own.wait_apart(s_go)
                    for t in range(NT):
                        ins = dve.max(best[:, t, :], logits[:, t, 0:EXPERTS])
                    own(ins)
                    own.wait()
                    own(dve.tensor_copy(drop[:, :, 0:2], best[:, :, 0:2]))
                    dve.tensor_tensor(away[:, :, :], logits[:, :, 0:EXPERTS],
                                      best[:, :, 0:1].to_broadcast([P, NT, EXPERTS]), ALU.subtract).then_inc(away_sb.sem, 1)
                    own.wait_apart(s_go)
                    for t in range(NT):
                        ins = dve.match_replace(out=left[:, t, :], in_to_replace=drop[:, t, :],
                                                in_values=logits[:, t, :], imm_value=TAKEN)
                    own(ins)
                    own.wait()
                    own(dve.tensor_scalar(taken[:, :, :], left[:, :, 0:EXPERTS], TAKEN, None, ALU.is_equal))
                    own.wait()
                    dve.wait_ge(share_sb.sem, share_sb(b, 1))
                    own(dve.tensor_tensor(gates[:, :, :], share[:, :, :], taken[:, :, :], ALU.mult))
                    own.wait()
                    own(dve.tensor_reduce(total[:, :], gates[:, :, :], AX.X, ALU.add))
                    own.wait()
                    own(dve.reciprocal(total[:, :], total[:, :]))
                    own.wait()
                    own(dve.tensor_tensor(gates[:, :, :], gates[:, :, :],
                                          total[:, :].unsqueeze(2).to_broadcast([P, NT, EXPERTS]), ALU.mult))
                    own.wait()
                    if more:
                        scale_h(b + 1)
                    for e in range(EXPERTS):
                        dve.wait_ge(out_ps.sem, out_ps(b, e + 1))
                        if e > 0:
                            weighed.wait()
                        O = bank[2 + e % 2]
                        for t in range(NT):
                            tok = k.y[:, b * NT + t, :]
                            ins = dve.scalar_tensor_tensor(out=tok, in0=O[:, P * t:P * t + P], scalar=gates[:, t, e:e + 1],
                                                           in1=tok, op0=ALU.mult, op1=ALU.add)
                        weighed(ins)
                    weighed.wait()
                    for t in range(NT):
                        tok = k.x[:, b * NT + t, :]
                        dve.scalar_tensor_tensor(out=tok, in0=k.y[:, b * NT + t, :], scalar=0.5, in1=tok,
                                                 op0=ALU.mult, op1=ALU.add)
                    own.end()
                    weighed.end()

                scale_h(0)
                with dve.Fori(0, B - 1) as b:
                    batch(b, True)
                batch(B - 1, False)

            @block.tensor
            def _(pe):
                pe.wait_ge(s_w, 64)

                def turn_h(b):
                    pe.wait_ge(h_ready.sem, h_ready(b, 1))
                    for t in range(NT):
                        ins = pe.transpose(T[:, P * t:P * t + P], h[:, t, :], k.ident[:, :])
                    ins.then_inc(hT_ps.sem, 1)

                def batch(b, more):
                    pe.wait_ge(hT_sb.sem, hT_sb(b, 1))
                    for t in range(NT):
                        ins = pe.matmul(G[:, EXPERTS * t:EXPERTS * t + EXPERTS], hT[:, P * t:P * t + P],
                                        gate_w[:, :], start=True, stop=True)
                    ins.then_inc(gate_ps.sem, 1)

                    def up(e):
                        if e >= 2:
                            pe.wait_ge(hid_sb.sem, hid_sb(b, e - 1))
                        for c in range(CH):
                            ins = pe.matmul(bank[4 + 2 * (e % 2) + c][:, :], w1[:, e, P * c:P * c + P], hT[:, :],
                                            start=True, stop=True)
                        ins.then_inc(hid_ps.sem, 1)

                    def down(e):
                        pe.wait_ge(hid_sb.sem, hid_sb(b, e + 1))
                        if not isinstance(b, int) or b > 0 or e >= 2:
                            pe.wait_ge(s_weighed, b * EXPERTS + max(e - 1, 0))
                        for t in range(NT):
                            for c in range(CH):
                                ins = pe.matmul(bank[2 + e % 2][:, P * t:P * t + P], hidden[:, e % 2, c, P * t:P * t + P],
                                                w2[:, e, c, :], start=c == 0, stop=c == CH - 1)
                        ins.then_inc(out_ps.sem, 1)

                    up(0)
                    for e in range(EXPERTS):
                        if e + 1 < EXPERTS:
                            up(e + 1)
                        if more and e == EXPERTS // 2:
                            turn_h(b + 1)
                        down(e)

                turn_h(0)
                with pe.Fori(0, B - 1) as b:
                    batch(b, True)
                batch(B - 1, False)


def rope_table():
    half = ROT // 2
    inv = (np.float32(1.0) / np.power(np.float32(10000.0), np.arange(half, dtype=np.float32)
                                      * np.float32(2.0) / np.float32(ROT))).astype(np.float32)
    ang = (np.arange(N, dtype=np.float32)[:, None] * inv).astype(np.float32)
    c, s = np.cos(ang).astype(np.float32), np.sin(ang).astype(np.float32)
    return np.ascontiguousarray(np.concatenate([c, c, s, s], axis=1))


def mosa(nc, k, a, name):
    with ExitStack() as ctx:
        ctx.callback(end_module, nc)

        def sb(n, shape, dt=F32):
            return ctx.enter_context(nc.sbuf_tensor(f"{name}_{n}", shape, dt))

        def sem(n):
            return take_semaphore(nc, ctx, f"{name}_{n}")

        def signal(n, per):
            return Signal(sem(n), per)

        E = MEXP
        PAIRS = E // 2
        TAKEN = -1.0
        router = sb("router", [P, 32])
        router_rows = sb("router_rows", [E, P])
        w_qkv = sb("w_qkv", [P, E, 3 * D])
        w_rot = sb("w_rot", [P, E, 2, ROT])
        w_out = sb("w_out", [P, E, D])
        rope = sb("rope", [P, NT, P])
        stats = sb("stats", [P, TILES, 6])
        mv = sb("mv", [P, TILES, 2])
        var = sb("var", [P, TILES])
        rstd = sb("rstd", [P, TILES])
        hT = sb("hT", [P, N])
        grow = sb("grow", [P, N])
        gate = sb("gate", [P, N])
        work = sb("work", [P, 2, N])
        best = sb("best", [P, 8])
        chosen = sb("chosen", [P, N], BF16)
        chosenT = sb("chosenT", [P, NT, P], BF16)
        upto = sb("upto", [P, NT, N], BF16)
        rank = sb("rank", [P, N], BF16)
        rankT = sb("rankT", [P, NT, P])
        gate_part = sb("gate_part", [P, 3, N], BF16)
        gate_rest = sb("gate_rest", [P, 2, N])
        select = sb("select", [P, B * PAIRS, P], BF16)
        count = sb("count", [P, E, MK])
        slot = sb("slot", [P, 1])
        order_mask = sb("order_mask", [P, MK])
        onehot = sb("onehot", [P, NT, E * MK])
        h = sb("h", [P, NT, D])
        xg = sb("xg", [P, E * MK])
        turn = sb("turn", [P, E * MK])
        rot_a = sb("rot_a", [ROT, 2, E * MK])
        rot_b = sb("rot_b", [ROT, 2, E * MK])
        qr = sb("qr", [P, E * MK])
        kr = sb("kr", [P, E * MK])
        v = sb("v", [P, PAIRS, D])
        scores = sb("scores", [P, PAIRS, MK])
        top = sb("top", [P, PAIRS])
        total = sb("total", [P, PAIRS])
        probs = sb("probs", [P, PAIRS, MK])
        diag = sb("diag", [P, PAIRS, P])
        diagT = sb("diagT", [P, PAIRS, P])
        avT = sb("avT", [P, PAIRS, P])
        pre = sb("pre", [P, PAIRS, D])
        gate_sb = sb("gate_sb", [P, PAIRS, N])
        scatter = sb("scatter", [P, PAIRS, N])
        bank = k.bank

        s_w, s_wr, s_made, s_made2, s_stat, s_ms, s_rstd = (sem(n) for n in (
            "weights", "router_in", "made", "made2", "stat", "rstd_step", "rstd_done"))
        s_rot = sem("rot_weights")
        s_rps, s_rsb = sem("router_ps"), sem("router_sb")
        s_h, s_hps, s_hsb, s_logit = sem("h_ready"), sem("hT_ps"), sem("hT_sb"), sem("logit_ps")
        s_grow, s_chosen, s_cps, s_csb, s_rank, s_rkm, s_rtps, s_ranked = (sem(n) for n in (
            "grown", "chosen_done", "chosenT_ps", "chosenT_sb", "rank_ps", "rank_done", "rankT_ps", "ranked"))
        copied = signal("h_copied", 1)
        hot = signal("onehot_done", 1)
        xg_ps, xg_sb = signal("xg_ps", 1), signal("xg_sb", 1)
        tab_ps, tab_sb = signal("turn_ps", 1), signal("turn_sb", 1)
        proj_ps = signal("qk_ps", 2)
        v_ps, v_sb = signal("v_ps", 1), signal("v_sb", 1)
        rest_sb = signal("unturned_sb", 2)
        qk_sb = signal("qk_sb", 1)
        sc_ps = signal("score_ps", 1)
        away_sb = signal("away_sb", 1)
        exp_sb = signal("exp_sb", 1)
        diag_sb = signal("diag_sb", 1)
        dT_ps, dT_sb = signal("diagT_ps", 1), signal("diagT_sb", 1)
        av_ps, av_sb = signal("av_ps", 1), signal("av_sb", 1)
        pre_ps, pre_sb = signal("pre_ps", 1), signal("pre_sb", 1)
        bc_ps, g_sb, sc_sb = signal("broadcast_ps", PAIRS), signal("gate_sb_done", PAIRS), signal("scatter_sb", PAIRS)
        out_ps = signal("out_ps", 1)

        with nc.Block() as block:
            @block.sync
            def _(sp):
                sp.dma_start(router_rows[:, :], a["L1_ffn_Wr"]).then_inc(s_wr, 16)
                sp.dma_start(w_qkv[:, :, :], a["L1_ffn_Wqkv"].rearrange("e d j -> d e j")).then_inc(s_w, 16)
                sp.dma_start(w_out[:, :, :], a["L1_ffn_Wo"].rearrange("e d j -> d e j")).then_inc(s_w, 16)
                sp.dma_start(rope[:, :, :], a["rope"].rearrange("(t p) j -> p t j", p=P)).then_inc(s_w, 16)
                sp.wait_ge(s_wr, 16)
                sp.wait_ge(s_w, 48)

            @block.gpsimd
            def _(pool):
                n = 0

                def step(ins):
                    nonlocal n
                    ins.then_inc(s_ms, 1)
                    n += 1
                    pool.wait_ge(s_ms, n)

                pool.memset(upto[:, :, :], 1.0).then_inc(s_made, 1)
                pool.memset(select[:, :, :], 0.0).then_inc(s_made, 1)
                pool.memset(order_mask[:, :], 0.0).then_inc(s_made, 1)
                pool.memset(diag[:, :, :], 0.0).then_inc(s_made, 1)
                pool.iota(count[:, :, :], pattern=[[0, E], [1, MK]], base=1, channel_multiplier=0,
                          allow_small_or_imprecise_dtypes=True).then_inc(s_made, 1)
                pool.iota(slot[:, :], pattern=[[0, 1]], base=1, channel_multiplier=1,
                          allow_small_or_imprecise_dtypes=True).then_inc(s_made, 1)
                pool.wait_ge(s_made, 6)
                pool.affine_select(out=upto[:, :, :], in_=upto[:, :, :], compare_op=ALU.is_ge, fill=0.0, base=0,
                                   pattern=[[-P, NT], [1, N]], channel_multiplier=-1).then_inc(s_made2, 1)
                for e2 in range(2):
                    for b in range(B):
                        ins = pool.affine_select(out=select[:, PAIRS * b:PAIRS * b + PAIRS, MK * e2:MK * e2 + MK],
                                                 in_=select[:, PAIRS * b:PAIRS * b + PAIRS, MK * e2:MK * e2 + MK],
                                                 compare_op=ALU.not_equal, fill=1.0, base=-32 * b - e2,
                                                 pattern=[[-2, PAIRS], [0, MK]], channel_multiplier=1)
                        ins.then_inc(s_made2, 1)
                pool.affine_select(out=order_mask[:, :], in_=order_mask[:, :],
                                   compare_op=ALU.is_ge, fill=NEG, base=0, pattern=[[-1, MK]],
                                   channel_multiplier=1).then_inc(s_made2, 1)
                pool.wait_ge(s_stat, 1)
                step(pool.tensor_scalar(var[:, :], mv[:, :, 1], 1e-5, None, ALU.add))
                pool.tensor_tensor(rstd[:, :], var[:, :], k.half[:, :], ALU.pow).then_inc(s_rstd, 1)
                pool.wait_ge(s_w, 48)
                for i in range(2):
                    pool.tensor_scalar(w_rot[:, :, i, 0:ROT // 2], w_qkv[:, :, D * i + ROT // 2:D * i + ROT], -1.0, None,
                                       ALU.mult).then_inc(s_rot, 1)
                    pool.tensor_copy(w_rot[:, :, i, ROT // 2:ROT], w_qkv[:, :, D * i:D * i + ROT // 2]).then_inc(s_rot, 1)

            @block.scalar
            def _(act):
                for b in range(B):
                    act.wait_ge(s_hps, b + 1)
                    if b > 0:
                        act.wait_ge(s_logit, b)
                    act.copy(hT[:, :], bank[b % 2][:, :]).then_inc(s_hsb, 1)
                act.wait_ge(s_logit, B)
                act.activation(grow[:, :], bank[2][:, :], ACT.Exp, scale=-1.0).then_inc(s_grow, 1)

                def copy_h(b):
                    act.copy(h[:, :, :], k.y[:, bass.ds(b * NT, NT), :]).then_inc(copied.sem, 1)

                def chosen_tokens(b):
                    act.wait_ge(xg_ps.sem, xg_ps(b, 1))
                    act.copy(xg[:, :], bank[0][:, :]).then_inc(xg_sb.sem, 1)

                def chosen_turns(b):
                    act.wait_ge(tab_ps.sem, tab_ps(b, 1))
                    act.copy(turn[:, :], bank[1][:, :]).then_inc(tab_sb.sem, 1)

                def gate_copy(b, i):
                    act.wait_ge(bc_ps.sem, bc_ps(b, i + 1))
                    act.copy(gate_sb[:, i, :], bank[2 + i % 2][:, :]).then_inc(g_sb.sem, 1)

                def batch(b, more):
                    if more:
                        copy_h(b + 1)
                    for i, dst in enumerate((qr, kr)):
                        act.wait_ge(proj_ps.sem, proj_ps(b, i + 1))
                        act.copy(dst[ROT:P, :], bank[2 + i][ROT:P, :]).then_inc(rest_sb.sem, 1)
                    act.wait_ge(v_ps.sem, v_ps(b, 1))
                    act.copy(v[:, :, :].rearrange("p a d -> p (a d)"), bank[6][:, :]).then_inc(v_sb.sem, 1)
                    gate_copy(b, 0)
                    gate_copy(b, 1)
                    act.wait_ge(away_sb.sem, away_sb(b, 1))
                    act.activation(probs[:, :, :], scores[:, :, :], ACT.Exp).then_inc(exp_sb.sem, 1)
                    act.wait_ge(dT_ps.sem, dT_ps(b, 1))
                    act.copy(diagT[:, :, :].rearrange("p a d -> p (a d)"), bank[6][:, :]).then_inc(dT_sb.sem, 1)
                    gate_copy(b, 2)
                    gate_copy(b, 3)
                    act.wait_ge(av_ps.sem, av_ps(b, 1))
                    act.copy(avT[:, :, :].rearrange("p a d -> p (a d)"), bank[6][:, :]).then_inc(av_sb.sem, 1)
                    if more:
                        chosen_tokens(b + 1)
                    act.wait_ge(pre_ps.sem, pre_ps(b, 1))
                    act.copy(pre[:, :, :].rearrange("p a d -> p (a d)"), bank[3][:, :]).then_inc(pre_sb.sem, 1)
                    if more:
                        chosen_turns(b + 1)

                copy_h(0)
                chosen_tokens(0)
                chosen_turns(0)
                with act.Fori(0, B - 1) as b:
                    batch(b, True)
                batch(B - 1, False)

            @block.vector
            def _(dve):
                first = Chain(dve, sem("dve_first"), 0)
                own = Chain(dve, sem("dve_step"), 6)
                for t in range(TILES):
                    ins = dve.bn_stats(stats[:, t, :], k.x[:, t, :])
                first(ins)
                first.wait()
                for t in range(TILES):
                    ins = dve.bn_aggr(mv[:, t, :], stats[:, t, :])
                ins.then_inc(s_stat, 1)
                dve.wait_ge(s_stat, 1)
                first(dve.memset(router[:, :], 0.0))
                first.wait()
                dve.wait_ge(s_rps, 1)
                dve.tensor_copy(router[:, 0:E], bank[3][:, 0:E]).then_inc(s_rsb, 1)
                dve.wait_ge(s_rstd, 1)
                for t in range(TILES):
                    ins = dve.tensor_scalar(k.y[:, t, :], k.x[:, t, :], mv[:, t, 0:1], rstd[:, t:t + 1],
                                            ALU.subtract, ALU.mult)
                    if t % NT == NT - 1:
                        ins.then_inc(s_h, 1)
                dve.wait_ge(s_grow, 1)
                first(dve.tensor_scalar(grow[:, :], grow[:, :], 1.0, None, ALU.add))
                first.wait()
                first(dve.reciprocal(gate[:, :], grow[:, :]))
                first.wait()
                for r in range(MK // 8):
                    src = gate[:, :] if r == 0 else work[:, (r - 1) % 2, :]
                    first(dve.max(best[:, :], src))
                    first.wait()
                    first(dve.match_replace(out=work[:, r % 2, :], in_to_replace=best[:, :], in_values=src,
                                            imm_value=TAKEN))
                    first.wait()
                dve.tensor_scalar(chosen[:, :], work[:, (MK // 8 - 1) % 2, :], TAKEN, None,
                                  ALU.is_equal).then_inc(s_chosen, 1)
                first(dve.tensor_copy(gate_part[:, 0, :], gate[:, :]))
                first.wait()
                first(dve.tensor_tensor(gate_rest[:, 0, :], gate[:, :], gate_part[:, 0, :], ALU.subtract))
                first.wait()
                first(dve.tensor_copy(gate_part[:, 1, :], gate_rest[:, 0, :]))
                first.wait()
                first(dve.tensor_tensor(gate_part[:, 2, :], gate_rest[:, 0, :], gate_part[:, 1, :], ALU.subtract))
                dve.wait_ge(s_cps, 1)
                dve.tensor_copy(chosenT[:, :, :].rearrange("p t r -> p (t r)"),
                                bank[0][:, 0:256].bitcast(BF16)).then_inc(s_csb, 1)
                dve.wait_ge(s_rank, 1)
                dve.wait_ge(s_chosen, 1)
                dve.tensor_tensor(rank[:, :], bank[1][:, :], chosen[:, :], ALU.mult).then_inc(s_rkm, 1)
                dve.wait_ge(s_rtps, 1)
                dve.tensor_copy(rankT[:, :, :].rearrange("p t r -> p (t r)"),
                                bank[0][:, 0:256].bitcast(BF16)).then_inc(s_ranked, 1)
                dve.wait_ge(s_ranked, 1)
                dve.wait_ge(s_made2, 10)
                first(dve.tensor_scalar(slot[MK:P, :], slot[MK:P, :], float(-MK), None, ALU.add))
                first(dve.tensor_copy(order_mask[MK:P, :], order_mask[0:MK, :]))
                first.wait()

                def make_onehot(b):
                    for c in range(NT):
                        ins = dve.tensor_tensor(onehot[:, c, :].rearrange("p (e j) -> p e j", e=E),
                                                rankT[:, c, bass.ds(b * 32, E)].unsqueeze(2).to_broadcast([P, E, MK]),
                                                count[:, :, :], ALU.is_equal)
                    ins.then_inc(hot.sem, 1)

                def make_scatter(b, i):
                    dve.wait_ge(g_sb.sem, g_sb(b, i + 1))
                    dve.scalar_tensor_tensor(out=scatter[:, i, :], in0=bank[4 + i % 2][:, :], scalar=slot[:, 0:1],
                                             in1=gate_sb[:, i, :], op0=ALU.is_equal, op1=ALU.mult).then_inc(sc_sb.sem, 1)

                def batch(b, more):
                    own.start(b)
                    dve.wait_ge(tab_sb.sem, tab_sb(b, 1))
                    if more:
                        make_onehot(b + 1)
                    for i, (src, dst) in enumerate(((bank[2], qr), (bank[3], kr))):
                        dve.wait_ge(rest_sb.sem, rest_sb(b, i + 1))
                        dve.tensor_tensor(rot_a[:, i, :], src[0:ROT, :], turn[0:ROT, :], ALU.mult)
                        own(dve.tensor_tensor(rot_b[:, i, :], bank[4 + i][ROT:P, :], turn[ROT:P, :], ALU.mult))
                        own.wait()
                        ins = dve.tensor_tensor(dst[0:ROT, :], rot_a[:, i, :], rot_b[:, i, :], ALU.add)
                    ins.then_inc(qk_sb.sem, 1)
                    dve.wait_ge(sc_ps.sem, sc_ps(b, 1))
                    own(dve.scalar_tensor_tensor(out=scores[:, :, :],
                                                 in0=bank[7][:, 0:PAIRS * MK].rearrange("p (a m) -> p a m", a=PAIRS),
                                                 scalar=D ** -0.5,
                                                 in1=order_mask[:, :].unsqueeze(1).to_broadcast([P, PAIRS, MK]),
                                                 op0=ALU.mult, op1=ALU.add))
                    own.wait()
                    own(dve.tensor_reduce(top[:, :], scores[:, :, :], AX.X, ALU.max))
                    own.wait()
                    dve.tensor_tensor(scores[:, :, :], scores[:, :, :], top[:, :].unsqueeze(2).to_broadcast([P, PAIRS, MK]),
                                      ALU.subtract).then_inc(away_sb.sem, 1)
                    make_scatter(b, 0)
                    dve.wait_ge(exp_sb.sem, exp_sb(b, 1))
                    own(dve.tensor_reduce(total[:, :], probs[:, :, :], AX.X, ALU.add))
                    own.wait()
                    own(dve.reciprocal(total[:, :], total[:, :]))
                    own.wait()
                    for e2 in range(2):
                        rows = slice(MK * e2, MK * e2 + MK)
                        ins = dve.tensor_tensor(diag[rows, :, MK * e2:MK * e2 + MK], probs[rows, :, :],
                                                total[rows, :].unsqueeze(2).to_broadcast([MK, PAIRS, MK]), ALU.mult)
                    ins.then_inc(diag_sb.sem, 1)
                    for i in range(1, PAIRS):
                        make_scatter(b, i)
                    dve.wait_ge(out_ps.sem, out_ps(b, 1))
                    for t in range(NT):
                        tok = k.x[:, b * NT + t, :]
                        dve.scalar_tensor_tensor(out=tok, in0=bank[7][:, P * t:P * t + P], scalar=0.5, in1=tok,
                                                 op0=ALU.mult, op1=ALU.add)
                    own.end()

                make_onehot(0)
                with dve.Fori(0, B - 1) as b:
                    batch(b, True)
                batch(B - 1, False)

            @block.tensor
            def _(pe):
                pe.wait_ge(s_wr, 16)
                pe.transpose(bank[3][:, 0:E], router_rows[:, :], k.ident[0:E, 0:E]).then_inc(s_rps, 1)
                for b in range(B):
                    pe.wait_ge(s_h, b + 1)
                    if b >= 2:
                        pe.wait_ge(s_hsb, b - 1)
                    for t in range(NT):
                        ins = pe.transpose(bank[b % 2][:, P * t:P * t + P], k.y[:, NT * b + t, :], k.ident[:, :])
                    ins.then_inc(s_hps, 1)
                    if b == 0:
                        pe.wait_ge(s_rsb, 1)
                    pe.wait_ge(s_hsb, b + 1)
                    pe.matmul(bank[2][32 * b:32 * b + 32, :], router[:, :], hT[:, :], start=True,
                              stop=True).then_inc(s_logit, 1)
                pe.wait_ge(s_chosen, 1)
                for c in range(NT):
                    ins = pe.transpose(bank[0][:, 64 * c:64 * c + 64].bitcast(BF16), chosen[:, P * c:P * c + P], k.identb[:, :])
                ins.then_inc(s_cps, 1)
                pe.wait_ge(s_csb, 1)
                pe.wait_ge(s_made2, 10)
                for c in range(NT):
                    ins = pe.matmul(bank[1][:, :], chosenT[:, c, :], upto[:, c, :], start=c == 0, stop=c == NT - 1)
                ins.then_inc(s_rank, 1)
                pe.wait_ge(s_rkm, 1)
                for c in range(NT):
                    ins = pe.transpose(bank[0][:, 64 * c:64 * c + 64].bitcast(BF16), rank[:, P * c:P * c + P], k.identb[:, :])
                ins.then_inc(s_rtps, 1)
                pe.wait_ge(s_w, 48)
                pe.wait_ge(s_rot, 4)

                def gather_tokens(b, chunks):
                    if 0 in chunks:
                        pe.wait_ge(copied.sem, copied(b, 1))
                        pe.wait_ge(hot.sem, hot(b, 1))
                    for c in chunks:
                        ins = pe.matmul(bank[0][:, :], h[:, c, :], onehot[:, c, :], start=c == 0, stop=c == NT - 1)
                    if c == NT - 1:
                        ins.then_inc(xg_ps.sem, 1)

                def gather_turns(b, chunks):
                    for c in chunks:
                        ins = pe.matmul(bank[1][:, :], rope[:, c, :], onehot[:, c, :], start=c == 0, stop=c == NT - 1)
                    if c == NT - 1:
                        ins.then_inc(tab_ps.sem, 1)

                def spread(b, i):
                    if i >= 2:
                        pe.wait_ge(sc_sb.sem, sc_sb(b, i - 1))
                    sel = select[:, b * PAIRS + i, :]
                    pe.matmul(bank[4 + i % 2][:, :], sel, rank[:, :], start=True, stop=True)
                    for part in range(3):
                        ins = pe.matmul(bank[2 + i % 2][:, :], sel, gate_part[:, part, :], start=part == 0, stop=part == 2)
                    ins.then_inc(bc_ps.sem, 1)

                def batch(b, more):
                    pe.wait_ge(xg_sb.sem, xg_sb(b, 1))
                    for i in range(2):
                        for e in range(E):
                            cols = slice(MK * e, MK * e + MK)
                            pe.matmul(bank[2 + i][:, cols], w_qkv[:, e, D * i:D * i + D], xg[:, cols], start=True, stop=True)
                            ins = pe.matmul(bank[4 + i][ROT:P, cols], w_rot[:, e, i, :], xg[:, cols], start=True, stop=True)
                        ins.then_inc(proj_ps.sem, 1)
                    for e in range(E):
                        half = slice(MK * (e % 2), MK * (e % 2) + MK)
                        ins = pe.matmul(bank[6][half, D * (e // 2):D * (e // 2) + D], xg[:, MK * e:MK * e + MK],
                                        w_qkv[:, e, 2 * D:3 * D], start=True, stop=True)
                    ins.then_inc(v_ps.sem, 1)
                    if more:
                        gather_tokens(b + 1, (0,))
                    pe.wait_ge(qk_sb.sem, qk_sb(b, 1))
                    for e in range(E):
                        half = slice(MK * (e % 2), MK * (e % 2) + MK)
                        cols = slice(MK * e, MK * e + MK)
                        ins = pe.matmul(bank[7][half, MK * (e // 2):MK * (e // 2) + MK], qr[:, cols], kr[:, cols],
                                        start=True, stop=True)
                    ins.then_inc(sc_ps.sem, 1)
                    spread(b, 0)
                    spread(b, 1)
                    if more:
                        gather_tokens(b + 1, (1,))
                        gather_turns(b + 1, (0, 1))
                    pe.wait_ge(diag_sb.sem, diag_sb(b, 1))
                    pe.wait_ge(v_sb.sem, v_sb(b, 1))
                    for i in range(PAIRS):
                        ins = pe.transpose(bank[6][:, P * i:P * i + P], diag[:, i, :], k.ident[:, :])
                    ins.then_inc(dT_ps.sem, 1)
                    spread(b, 2)
                    spread(b, 3)
                    pe.wait_ge(dT_sb.sem, dT_sb(b, 1))
                    for i in range(PAIRS):
                        ins = pe.matmul(bank[6][:, P * i:P * i + P], v[:, i, :], diagT[:, i, :], start=True, stop=True)
                    ins.then_inc(av_ps.sem, 1)
                    if more:
                        gather_tokens(b + 1, (2, 3))
                    pe.wait_ge(av_sb.sem, av_sb(b, 1))
                    pe.wait_ge(sc_sb.sem, sc_sb(b, PAIRS))
                    for e in range(E):
                        half = slice(MK * (e % 2), MK * (e % 2) + MK)
                        ins = pe.matmul(bank[3][half, D * (e // 2):D * (e // 2) + D],
                                        avT[:, e // 2, MK * (e % 2):MK * (e % 2) + MK], w_out[:, e, :],
                                        start=True, stop=True)
                    ins.then_inc(pre_ps.sem, 1)
                    if more:
                        gather_turns(b + 1, (2, 3))
                    pe.wait_ge(pre_sb.sem, pre_sb(b, 1))
                    for t in range(NT):
                        for i in range(PAIRS):
                            ins = pe.matmul(bank[7][:, P * t:P * t + P], scatter[:, i, P * t:P * t + P], pre[:, i, :],
                                            start=i == 0, stop=i == PAIRS - 1)
                    ins.then_inc(out_ps.sem, 1)

                pe.wait_ge(s_ranked, 1)
                gather_tokens(0, range(NT))
                gather_turns(0, range(NT))
                with pe.Fori(0, B - 1) as b:
                    batch(b, True)
                batch(B - 1, False)


def additive(nc, k, a, name="add"):
    with ExitStack() as ctx:
        ctx.callback(end_module, nc)

        def sb(n, shape, dt=F32):
            return ctx.enter_context(nc.sbuf_tensor(f"{name}_{n}", shape, dt))

        def sem(n):
            return take_semaphore(nc, ctx, f"{name}_{n}")

        def signal(n, per):
            return Signal(sem(n), per)

        C2 = ADIM // P
        CH = HID // P
        TOKEN_SCALE = 16 ** -0.5
        W = D + 1
        z = k.y
        wqk = sb("wqk", [P, 2, ADIM])
        wp = sb("wp", [P, C2, ADIM])
        wfg = sb("wfg", [P, C2, W])
        bqkp = sb("bqkp", [P, 3, C2])
        bqk_rows = sb("bqk_rows", [P, 2, ADIM])
        bf_rows = sb("bf_rows", [P, D])
        w1 = sb("w1", [P, HID])
        w2 = sb("w2", [P, CH, D])
        b1 = sb("b1", [P, CH])
        b2_rows = sb("b2_rows", [P, D])
        ln = sb("ln", [P, 4])
        wpT = sb("wpT", [P, C2, ADIM])
        wqkT = sb("wqkT", [P, 2, C2, D])
        wpf = sb("wpf", [P, C2, D])
        wqfg = sb("wqfg", [P, W])
        bqfg_rows = sb("bqfg_rows", [P, W])
        bpf_rows = sb("bpf_rows", [P, D])
        b_hi = sb("b_hi", [P, 2 * ADIM], BF16)
        b_mid = sb("b_mid", [P, 2 * ADIM], BF16)
        b_rest = sb("b_rest", [P, 2 * ADIM])
        b_lo = sb("b_lo", [P, 2 * ADIM], BF16)
        b_sum = sb("b_sum", [P, 2 * ADIM])
        b_parts = sb("b_parts", [P, 2 * ADIM], BF16)
        row_is = sb("row_is", [P, 3])
        three = sb("three", [P, P], BF16)
        ones = sb("ones", [P, P])
        stats = sb("stats", [P, TILES, 6])
        mv = sb("mv", [P, TILES, 2])
        var = sb("var", [P, TILES])
        rstd = sb("rstd", [P, TILES])
        zn = sb("zn", [P, TILES, D])
        hT = sb("hT", [P, B, N])
        squares = sb("squares", [P, ADIM])
        kstats = sb("kstats", [P, TILES, 6])
        kmv = sb("kmv", [P, TILES, 2])
        ss = sb("ss", [P, 2, TILES])
        inv = sb("inv", [P, 2, TILES])
        half2 = sb("half2", [P, 2, TILES])
        qf = sb("qf", [P, TILES, W])
        alpha = sb("alpha", [P, TILES])
        token_sums = sb("token_sums", [P, 2, TILES])
        over = sb("over", [P, 2, B])
        inv_a = sb("inv_a", [P, B])
        u = sb("u", [P, B])
        coef = sb("coef", [P, B])
        G = sb("G", [P, C2, B])
        bkG = sb("bkG", [P, C2, B])
        wG = sb("wG", [P, C2, B, D])
        M = sb("M", [P, B, D])
        bkM_rows = sb("bkM_rows", [P, B, D])
        kp4 = sb("kp4", [P, 2, NT, D])
        hidden = sb("hidden", [P, 2, CH, N])
        bank = k.bank

        s_w = [signal(f"w_{n}", 16 * c) for n, c in (("attn", 9), ("mlp", 6))]
        s_rows = signal("rows_in", 64)
        s_made, s_first, s_go = sem("made"), sem("first"), sem("go")
        ln_step, ln_done = signal("ln_step", 2), signal("ln_done", 2)
        zn_ok = signal("zn_ready", 2 * B)
        hT_ps, hT_sb = signal("hT_ps", 2 * B), signal("hT_sb", 2 * B)
        fold_ps, fold_sb = signal("fold_ps", 4), signal("fold_sb", 4)
        b_ok = signal("bias_parts", 1)
        q_ps, q_sq = signal("q_ps", TILES), signal("q_sq", TILES)
        k_ps, k_sq = signal("k_ps", TILES), signal("k_sq", TILES)
        f_ps, f_sb = signal("f_ps", TILES), signal("f_sb", TILES)
        ss_ok, inv_ok = signal("ss_ready", 1), signal("inv_ready", 1)
        sums_ok, sums_ps = signal("sums_ready", 1), signal("sums_ps", 1)
        over_ok, inva_ok = signal("over_ready", 1), signal("inva_ready", 1)
        u_ok, g_ps, g_ok = signal("u_ready", 1), signal("g_ps", 1), signal("g_ready", 1)
        wg_ok, m_ps, m_sb, bm_sb = signal("wg_ready", C2), signal("m_ps", 2), signal("m_sb", 1), signal("bm_sb", 1)
        kp_ps, kp_read = signal("kp_ps", B), signal("kp_read", B)
        hid_ps, hid_sb = signal("hid_ps", B * CH), signal("hid_sb", B * CH)
        out_ps, out_read = signal("out_ps", B), signal("out_read", B)
        attn_free, mlp_free = signal("attn_free", 1), signal("mlp_free", 1)

        def cols(x, n):
            return x.rearrange("o (c p) -> p (o c)", p=P)

        with nc.Block() as block:
            @block.sync
            def _(sp):
                with sp.Fori(0, DEPTH) as i:
                    one = bass.ds(i, 1)
                    sp.wait_ge(attn_free.sem, attn_free(i, 1))
                    for dst, src in (
                            (wqk[:, 0, :], a["L1_attn_Wq"][one].rearrange("o p n -> p (o n)")),
                            (wqk[:, 1, :], a["L1_attn_Wk"][one].rearrange("o p n -> p (o n)")),
                            (wp[:, :, :], a["L1_attn_Wp"][one].rearrange("o (c p) n -> p (o c) n", p=P)),
                            (wfg[:, :, 0:D], a["L1_attn_Wf"][one].rearrange("o (c p) n -> p (o c) n", p=P)),
                            (wfg[:, :, D:W], a["L1_attn_w_g"][one].rearrange("o (c p) n -> p (o c) n", p=P)),
                            (bqkp[:, 0, :], cols(a["L1_attn_bq"][one], C2)),
                            (bqkp[:, 1, :], cols(a["L1_attn_bk"][one], C2)),
                            (bqkp[:, 2, :], cols(a["L1_attn_bp"][one], C2)),
                            (ln[:, 0:1], cols(a["L1_attn_ln1_g"][one], 1))):
                        sp.dma_start(dst, src, allow_slow_non_contiguous=True).then_inc(s_w[0].sem, 16)
                    sp.wait_ge(mlp_free.sem, mlp_free(i, 1))
                    for dst, src in (
                            (w1[:, :], a["L1_attn_W1"][one].rearrange("o p n -> p (o n)")),
                            (w2[:, :, :], a["L1_attn_W2"][one].rearrange("o (c p) n -> p (o c) n", p=P)),
                            (b1[:, :], cols(a["L1_attn_b1"][one], CH)),
                            (ln[:, 2:3], cols(a["L1_attn_ln2_g"][one], 1)),
                            (ln[:, 3:4], cols(a["L1_attn_ln2_b"][one], 1)),
                            (b2_rows[:, :], a["L1_attn_b2"][one].to_broadcast([P, D]))):
                        sp.dma_start(dst, src, allow_slow_non_contiguous=True).then_inc(s_w[1].sem, 16)

            @block.gpsimd
            def _(pool):
                pool.memset(ones[:, :], 1.0).then_inc(s_made, 1)
                pool.memset(half2[:, :, :], -0.5).then_inc(s_made, 1)
                pool.memset(three[:, :], 1.0).then_inc(s_made, 1)
                pool.memset(row_is[:, :], 0.0).then_inc(s_made, 1)
                pool.wait_ge(s_made, 4)
                pool.affine_select(out=three[:, :], in_=three[:, :], compare_op=ALU.is_ge, fill=0.0, base=2,
                                   pattern=[[0, P]], channel_multiplier=-1).then_inc(s_made, 1)
                pool.affine_select(out=row_is[:, :], in_=row_is[:, :], compare_op=ALU.not_equal, fill=1.0, base=0,
                                   pattern=[[-1, 3]], channel_multiplier=1).then_inc(s_made, 1)
                pool.wait_ge(s_first, 1)
                pool.tensor_scalar(var[:, :], mv[:, :, 1], 1e-5, None, ALU.add).then_inc(s_made, 1)
                pool.wait_ge(s_made, 7)
                pool.tensor_tensor(rstd[:, :], var[:, :], k.half[:, :], ALU.pow).then_inc(s_made, 1)
                with pool.Fori(0, DEPTH) as i:
                    def rsqrt_var(j):
                        pool.wait_ge(ln_step.sem, ln_step(i, j + 1))
                        pool.tensor_tensor(rstd[:, :], var[:, :], k.half[:, :], ALU.pow).then_inc(ln_done.sem, 1)

                    rsqrt_var(0)
                    pool.wait_ge(ss_ok.sem, ss_ok(i, 1))
                    pool.tensor_tensor(inv[:, :, :], ss[:, :, :], half2[:, :, :], ALU.pow).then_inc(inv_ok.sem, 1)
                    pool.wait_ge(over_ok.sem, over_ok(i, 1))
                    pool.tensor_tensor(inv_a[:, :], over[:, 0, :], half2[:, 0, 0:B], ALU.pow).then_inc(inva_ok.sem, 1)
                    rsqrt_var(1)

            @block.scalar
            def _(act):
                with act.Fori(0, DEPTH) as i:
                    one = bass.ds(i, 1)
                    act.wait_ge(attn_free.sem, attn_free(i, 1))
                    for dst, src in (
                            (ln[:, 1:2], cols(a["L1_attn_ln1_b"][one], 1)),
                            (bqk_rows[:, 0, :], a["L1_attn_bq"][one].to_broadcast([P, ADIM])),
                            (bqk_rows[:, 1, :], a["L1_attn_bk"][one].to_broadcast([P, ADIM])),
                            (bf_rows[:, :], a["L1_attn_bf"][one].to_broadcast([P, D]))):
                        act.dma_start(dst, src, allow_slow_non_contiguous=True).then_inc(s_rows.sem, 16)

                    act.wait_ge(fold_ps.sem, fold_ps(i, 1))
                    act.copy(wpT[:, :, :].rearrange("p c n -> p (c n)"), bank[6][:, :]).then_inc(fold_sb.sem, 1)
                    act.wait_ge(fold_ps.sem, fold_ps(i, 2))
                    act.copy(wqkT[:, :, :, :].rearrange("p s c n -> p (s c n)"), bank[7][:, :]).then_inc(fold_sb.sem, 1)
                    act.wait_ge(fold_ps.sem, fold_ps(i, 3))
                    act.copy(wpf[:, :, :].rearrange("p c n -> p (c n)"), bank[6][:, 0:C2 * D])
                    act.copy(wqfg[:, :], bank[6][:, C2 * D:C2 * D + W]).then_inc(fold_sb.sem, 1)
                    act.wait_ge(s_w[0].sem, s_w[0](i, 144))
                    act.wait_ge(s_rows.sem, s_rows(i, 64))
                    for b in range(B):
                        act.wait_ge(hT_ps.sem, hT_ps(i, b + 1))
                        act.activation(hT[:, b, :], bank[b % 2][:, :], ACT.Identity, bias=ln[:, 1:2],
                                       scale=ln[:, 0:1]).then_inc(hT_sb.sem, 1)
                    for t in range(TILES):
                        act.wait_ge(q_ps.sem, q_ps(i, t + 1))
                        act.activation(squares[:, :], bank[2 + t % 2][:, 0:ADIM], ACT.Square,
                                       accum_out=ss[:, 0, t:t + 1]).then_inc(q_sq.sem, 1)
                        act.wait_ge(q_sq.sem, q_sq(i, t + 1))
                    act.wait_ge(g_ok.sem, g_ok(i, 1))
                    for b in range(B):
                        ins = act.mul(wG[:, 1, b, :], wpf[:, 1, :], G[:, 1, b:b + 1])
                    ins.then_inc(wg_ok.sem, 1)
                    act.wait_ge(m_ps.sem, m_ps(i, 1))
                    act.copy(M[:, :, :].rearrange("p b d -> p (b d)"), bank[4][:, :]).then_inc(m_sb.sem, 1)
                    act.wait_ge(s_w[1].sem, s_w[1](i, 96))
                    for b in range(B):
                        act.wait_ge(hT_ps.sem, hT_ps(i, B + b + 1))
                        act.activation(hT[:, b, :], bank[b % 2][:, :], ACT.Identity, bias=ln[:, 3:4],
                                       scale=ln[:, 2:3]).then_inc(hT_sb.sem, 1)
                    for b in range(B):
                        for c in range(CH):
                            n = CH * b + c
                            act.wait_ge(hid_ps.sem, hid_ps(i, n + 1))
                            if b >= 2 and c == 0:
                                act.wait_ge(out_ps.sem, out_ps(i, b - 1))
                            act.activation(hidden[:, b % 2, c, :], bank[4 + c][:, :], ACT.Gelu,
                                           bias=b1[:, c:c + 1]).then_inc(hid_sb.sem, 1)

            @block.vector
            def _(dve):
                own = Chain(dve, sem("dve_step"), 22)
                first = Chain(dve, sem("dve_first"), 0)
                dve.sem_inc(attn_free.sem, 1)
                dve.sem_inc(mlp_free.sem, 1)
                for t in range(TILES):
                    ins = dve.bn_stats(stats[:, t, :], k.x[:, t, :])
                first(ins)
                first.wait()
                for t in range(TILES):
                    ins = dve.bn_aggr(mv[:, t, :], stats[:, t, :])
                ins.then_inc(s_first, 1)
                dve.wait_ge(s_made, 8)
                for t in range(TILES):
                    ins = dve.tensor_scalar(z[:, t, :], k.x[:, t, :], mv[:, t, 0:1], rstd[:, t:t + 1],
                                            ALU.subtract, ALU.mult)
                first(ins)
                first.wait()
                with dve.Fori(0, DEPTH) as i:
                    own.start(i)

                    def normal(j):
                        for t in range(TILES):
                            ins = dve.bn_stats(stats[:, t, :], z[:, t, :])
                        own(ins)
                        own.wait_apart(s_go)
                        for t in range(TILES):
                            ins = dve.bn_aggr(mv[:, t, :], stats[:, t, :])
                        own(ins)
                        own.wait()
                        dve.tensor_scalar(var[:, :], mv[:, :, 1], 1e-6, None, ALU.add).then_inc(ln_step.sem, 1)
                        dve.wait_ge(ln_done.sem, ln_done(i, j + 1))
                        for t in range(TILES):
                            ins = dve.tensor_scalar(zn[:, t, :], z[:, t, :], mv[:, t, 0:1], rstd[:, t:t + 1],
                                                    ALU.subtract, ALU.mult)
                            if t % NT == NT - 1:
                                ins.then_inc(zn_ok.sem, 1)

                    normal(0)
                    dve.wait_ge(s_rows.sem, s_rows(i, 64))
                    rows = bqk_rows[:, :, :].rearrange("p s n -> p (s n)")
                    own(dve.tensor_copy(b_hi[:, :], rows))
                    own.wait()
                    own(dve.tensor_tensor(b_rest[:, :], rows, b_hi[:, :], ALU.subtract))
                    own.wait()
                    own(dve.tensor_copy(b_mid[:, :], b_rest[:, :]))
                    own.wait()
                    own(dve.tensor_tensor(b_lo[:, :], b_rest[:, :], b_mid[:, :], ALU.subtract))
                    own(dve.tensor_scalar(b_sum[:, :], b_hi[:, :], row_is[:, 0:1], None, ALU.mult))
                    own.wait()
                    own(dve.scalar_tensor_tensor(out=b_rest[:, :], in0=b_mid[:, :], scalar=row_is[:, 1:2],
                                                 in1=b_sum[:, :], op0=ALU.mult, op1=ALU.add))
                    own.wait()
                    dve.scalar_tensor_tensor(out=b_parts[:, :], in0=b_lo[:, :], scalar=row_is[:, 2:3],
                                             in1=b_rest[:, :], op0=ALU.mult, op1=ALU.add).then_inc(b_ok.sem, 1)
                    dve.wait_ge(fold_ps.sem, fold_ps(i, 4))
                    dve.tensor_copy(bqfg_rows[:, :], bank[7][:, 0:W])
                    dve.tensor_tensor(bpf_rows[:, :], bank[7][:, W:W + D], bf_rows[:, :], ALU.add).then_inc(fold_sb.sem, 1)
                    dve.wait_ge(fold_sb.sem, fold_sb(i, 4))
                    for t in range(TILES):
                        dve.wait_ge(k_ps.sem, k_ps(i, t + 1))
                        dve.bn_stats(kstats[:, t, :], bank[4 + t % 2][:, 0:ADIM]).then_inc(k_sq.sem, 1)
                        dve.wait_ge(f_ps.sem, f_ps(i, t + 1))
                        dve.tensor_tensor(qf[:, t, :], bank[6 + t % 2][:, 0:W], bqfg_rows[:, :], ALU.add).then_inc(f_sb.sem, 1)
                    dve.wait_ge(s_w[0].sem, s_w[0](i, 144))
                    dve.wait_ge(k_sq.sem, k_sq(i, TILES))
                    dve.sem_inc(s_go, 1)
                    for t in range(TILES):
                        ins = dve.bn_aggr(kmv[:, t, :], kstats[:, t, :])
                    own(ins)
                    own.wait()
                    own(dve.tensor_tensor(ss[:, 1, :], kmv[:, :, 0], kmv[:, :, 0], ALU.mult))
                    own.wait()
                    own(dve.tensor_tensor(ss[:, 1, :], ss[:, 1, :], kmv[:, :, 1], ALU.add))
                    own.wait()
                    own(dve.tensor_scalar(ss[:, 1, :], ss[:, 1, :], float(ADIM), None, ALU.mult))
                    own.wait()
                    dve.wait_ge(q_sq.sem, q_sq(i, TILES))
                    dve.tensor_scalar(ss[:, :, :], ss[:, :, :], 1e-24, None, ALU.max).then_inc(ss_ok.sem, 1)
                    dve.wait_ge(inv_ok.sem, inv_ok(i, 1))
                    dve.wait_ge(f_sb.sem, f_sb(i, TILES))
                    own(dve.scalar_tensor_tensor(out=alpha[:, :], in0=qf[:, :, D], scalar=TOKEN_SCALE, in1=inv[:, 0, :],
                                                 op0=ALU.mult, op1=ALU.mult))
                    own.wait()
                    dve.tensor_tensor(token_sums[:, 0, :], alpha[:, :], alpha[:, :], ALU.mult)
                    dve.tensor_tensor(token_sums[:, 1, :], alpha[:, :], inv[:, 0, :], ALU.mult).then_inc(sums_ok.sem, 1)
                    dve.wait_ge(sums_ps.sem, sums_ps(i, 1))
                    own(dve.tensor_reduce(over[:, :, :], bank[0][:, 0:2 * TILES].rearrange("p (s b t) -> p s b t", s=2, b=B),
                                          AX.X, ALU.add))
                    own.wait()
                    dve.tensor_scalar(over[:, 0, :], over[:, 0, :], 1e-24, None, ALU.max).then_inc(over_ok.sem, 1)
                    own(dve.tensor_scalar(u[:, :], bank[0][:, 64:64 + B], ln[:, 0:1], None, ALU.mult))
                    own.wait()
                    own(dve.scalar_tensor_tensor(out=coef[:, :], in0=over[:, 1, :], scalar=ln[:, 1:2], in1=u[:, :],
                                                 op0=ALU.mult, op1=ALU.add))
                    own.wait()
                    dve.wait_ge(inva_ok.sem, inva_ok(i, 1))
                    own(dve.tensor_tensor(u[:, :], coef[:, :], inv_a[:, :], ALU.mult))
                    own.wait()
                    dve.tensor_tensor(coef[:, :], over[:, 1, :], inv_a[:, :], ALU.mult).then_inc(u_ok.sem, 1)
                    dve.wait_ge(g_ps.sem, g_ps(i, 1))
                    dve.wait_ge(u_ok.sem, u_ok(i, 1))
                    for c in range(C2):
                        ins = dve.scalar_tensor_tensor(out=G[:, c, :], in0=coef[:, :], scalar=bqkp[:, 0, c:c + 1],
                                                       in1=bank[1][:, B * c:B * c + B], op0=ALU.mult, op1=ALU.add)
                    ins.then_inc(g_ok.sem, 1)
                    dve.wait_ge(g_ok.sem, g_ok(i, 1))
                    for b in range(B):
                        dve.tensor_scalar(wG[:, 0, b, :], wpf[:, 0, :], G[:, 0, b:b + 1], None, ALU.mult)
                    for c in range(C2):
                        ins = dve.tensor_scalar(bkG[:, c, :], G[:, c, :], bqkp[:, 1, c:c + 1], None, ALU.mult)
                    ins.then_inc(wg_ok.sem, 1)
                    for t in range(TILES):
                        ins = dve.scalar_tensor_tensor(out=z[:, t, :], in0=qf[:, t, 0:D], scalar=inv[:, 0, t:t + 1],
                                                       in1=z[:, t, :], op0=ALU.mult, op1=ALU.add)
                    own(ins)
                    own.wait()
                    own(dve.tensor_tensor(z[:, :, :], z[:, :, :], bpf_rows[:, :].unsqueeze(1).to_broadcast([P, TILES, D]),
                                          ALU.add))
                    own.wait()
                    dve.wait_ge(m_ps.sem, m_ps(i, 2))
                    dve.tensor_copy(bkM_rows[:, :, :].rearrange("p b d -> p (b d)"), bank[5][:, :]).then_inc(bm_sb.sem, 1)
                    dve.wait_ge(bm_sb.sem, bm_sb(i, 1))
                    for b in range(B):
                        dve.wait_ge(kp_ps.sem, kp_ps(i, b + 1))
                        pk = bank[2 + b % 2][:, :].rearrange("p (t d) -> p t d", t=NT)
                        dve.tensor_tensor(kp4[:, b % 2, :, :], pk,
                                          bkM_rows[:, b, :].unsqueeze(1).to_broadcast([P, NT, D]), ALU.add
                                          ).then_inc(kp_read.sem, 1)
                        dve.wait_ge(kp_read.sem, kp_read(i, b + 1))
                        for t in range(NT):
                            tok = z[:, NT * b + t, :]
                            ins = dve.scalar_tensor_tensor(out=tok, in0=kp4[:, b % 2, t, :],
                                                           scalar=inv[:, 1, NT * b + t:NT * b + t + 1], in1=tok,
                                                           op0=ALU.mult, op1=ALU.add)
                    ins.then_inc(attn_free.sem, 1)
                    dve.wait_ge(attn_free.sem, attn_free(i, 2))
                    normal(1)
                    dve.wait_ge(s_w[1].sem, s_w[1](i, 96))
                    dve.wait_ge(zn_ok.sem, zn_ok(i, 2 * B))
                    own(dve.tensor_tensor(z[:, :, :], z[:, :, :], b2_rows[:, :].unsqueeze(1).to_broadcast([P, TILES, D]),
                                          ALU.add))
                    own.wait()
                    for b in range(B):
                        dve.wait_ge(out_ps.sem, out_ps(i, b + 1))
                        tok = z[:, NT * b:NT * b + NT, :]
                        dve.tensor_tensor(tok, bank[2 + b % 2][:, :].rearrange("p (t d) -> p t d", t=NT), tok,
                                          ALU.add).then_inc(out_read.sem, 1)
                    dve.wait_ge(out_read.sem, out_read(i, B))
                    dve.sem_inc(mlp_free.sem, 1)
                    own.end()
                dve.tensor_tensor(k.x[:, :, :], k.x[:, :, :], z[:, :, :], ALU.add)

            @block.tensor
            def _(pe):
                pe.wait_ge(s_made, 6)
                with pe.Fori(0, DEPTH) as i:
                    pe.wait_ge(s_w[0].sem, s_w[0](i, 144))
                    for m in range(C2):
                        for c in range(C2):
                            ins = pe.transpose(bank[6][:, ADIM * m + P * c:ADIM * m + P * c + P],
                                               wp[:, c, P * m:P * m + P], k.ident[:, :])
                    ins.then_inc(fold_ps.sem, 1)
                    for s in range(2):
                        for c in range(C2):
                            ins = pe.transpose(bank[7][:, ADIM * s + P * c:ADIM * s + P * c + P],
                                               wqk[:, s, P * c:P * c + P], k.ident[:, :])
                    ins.then_inc(fold_ps.sem, 1)
                    pe.wait_ge(fold_sb.sem, fold_sb(i, 2))
                    for c in range(C2):
                        for m in range(C2):
                            pe.matmul(bank[6][:, D * c:D * c + D], wpT[:, m, P * c:P * c + P], wfg[:, m, 0:D],
                                      start=m == 0, stop=m == C2 - 1)
                    for c in range(C2):
                        ins = pe.matmul(bank[6][:, C2 * D:C2 * D + W], wqkT[:, 0, c, :], wfg[:, c, :],
                                        start=c == 0, stop=c == C2 - 1)
                    ins.then_inc(fold_ps.sem, 1)
                    for c in range(C2):
                        pe.matmul(bank[7][:, 0:W], bqkp[:, 0, c:c + 1].to_broadcast([P, P]), wfg[:, c, :],
                                  start=c == 0, stop=c == C2 - 1)
                    for c in range(C2):
                        ins = pe.matmul(bank[7][:, W:W + D], bqkp[:, 2, c:c + 1].to_broadcast([P, P]), wfg[:, c, 0:D],
                                        start=c == 0, stop=c == C2 - 1)
                    ins.then_inc(fold_ps.sem, 1)

                    def turn(j):
                        for b in range(B):
                            n = B * j + b
                            pe.wait_ge(zn_ok.sem, zn_ok(i, n + 1))
                            if b >= 2:
                                pe.wait_ge(hT_sb.sem, hT_sb(i, n - 1))
                            for t in range(NT):
                                ins = pe.transpose(bank[b % 2][:, P * t:P * t + P], zn[:, NT * b + t, :], k.ident[:, :])
                            ins.then_inc(hT_ps.sem, 1)

                    turn(0)
                    pe.wait_ge(b_ok.sem, b_ok(i, 1))
                    pe.wait_ge(fold_sb.sem, fold_sb(i, 4))
                    for t in range(TILES):
                        b = t // NT
                        if t % NT == 0:
                            pe.wait_ge(hT_sb.sem, hT_sb(i, b + 1))
                        lhs = hT[:, b, P * (t % NT):P * (t % NT) + P]
                        for s, base, ps, rd in ((0, 2, q_ps, q_sq), (1, 4, k_ps, k_sq)):
                            if t >= 2:
                                pe.wait_ge(rd.sem, rd(i, t - 1))
                            out = bank[base + t % 2][:, 0:ADIM]
                            pe.matmul(out, lhs, wqk[:, s, :], start=True, stop=False)
                            pe.matmul(out, three[:, :], b_parts[:, ADIM * s:ADIM * s + ADIM], start=False,
                                      stop=True).then_inc(ps.sem, 1)
                        if t >= 2:
                            pe.wait_ge(f_sb.sem, f_sb(i, t - 1))
                        pe.matmul(bank[6 + t % 2][:, 0:W], lhs, wqfg[:, :], start=True, stop=True).then_inc(f_ps.sem, 1)
                    pe.wait_ge(sums_ok.sem, sums_ok(i, 1))
                    pe.matmul(bank[0][:, 0:2 * TILES], ones[:, :], token_sums[:, :, :].rearrange("p s t -> p (s t)"),
                              start=True, stop=True)
                    for b in range(B):
                        for t in range(NT):
                            ins = pe.matmul(bank[0][:, 64 + b:65 + b], zn[:, NT * b + t, :],
                                            token_sums[:, 1, NT * b + t:NT * b + t + 1], start=t == 0, stop=t == NT - 1)
                    ins.then_inc(sums_ps.sem, 1)
                    pe.wait_ge(u_ok.sem, u_ok(i, 1))
                    for c in range(C2):
                        ins = pe.matmul(bank[1][:, B * c:B * c + B], wqk[:, 0, P * c:P * c + P], u[:, :],
                                        start=True, stop=True)
                    ins.then_inc(g_ps.sem, 1)
                    pe.wait_ge(wg_ok.sem, wg_ok(i, 2))
                    for b in range(B):
                        for c in range(C2):
                            ins = pe.matmul(bank[4][:, D * b:D * b + D], wqkT[:, 1, c, :], wG[:, c, b, :],
                                            start=c == 0, stop=c == C2 - 1)
                    ins.then_inc(m_ps.sem, 1)
                    for b in range(B):
                        for c in range(C2):
                            ins = pe.matmul(bank[5][:, D * b:D * b + D], bkG[:, c, b:b + 1].to_broadcast([P, P]),
                                            wpf[:, c, :], start=c == 0, stop=c == C2 - 1)
                    ins.then_inc(m_ps.sem, 1)
                    pe.wait_ge(m_sb.sem, m_sb(i, 1))
                    for b in range(B):
                        if b >= 2:
                            pe.wait_ge(kp_read.sem, kp_read(i, b - 1))
                        for t in range(NT):
                            ins = pe.matmul(bank[2 + b % 2][:, P * t:P * t + P], hT[:, b, P * t:P * t + P], M[:, b, :],
                                            start=True, stop=True)
                        ins.then_inc(kp_ps.sem, 1)
                    turn(1)
                    pe.wait_ge(s_w[1].sem, s_w[1](i, 96))

                    def up(b):
                        pe.wait_ge(hT_sb.sem, hT_sb(i, B + b + 1))
                        for c in range(CH):
                            if b > 0:
                                pe.wait_ge(hid_sb.sem, hid_sb(i, CH * (b - 1) + c + 1))
                            pe.matmul(bank[4 + c][:, :], w1[:, P * c:P * c + P], hT[:, b, :], start=True,
                                      stop=True).then_inc(hid_ps.sem, 1)

                    def down(b):
                        pe.wait_ge(hid_sb.sem, hid_sb(i, CH * (b + 1)))
                        if b >= 2:
                            pe.wait_ge(out_read.sem, out_read(i, b - 1))
                        for t in range(NT):
                            for c in range(CH):
                                ins = pe.matmul(bank[2 + b % 2][:, P * t:P * t + P], hidden[:, b % 2, c, P * t:P * t + P],
                                                w2[:, c, :], start=c == 0, stop=c == CH - 1)
                        ins.then_inc(out_ps.sem, 1)

                    up(0)
                    for b in range(B):
                        if b + 1 < B:
                            up(b + 1)
                        down(b)


def whole(nc, k, a):
    attention(nc, k, "mla1", True)
    experts(nc, k, a, "moe1")
    attention(nc, k, "att", False)
    attention(nc, k, "mla2", True)
    experts(nc, k, a, "moe2")
    mosa(nc, k, a, "mosa1")
    additive(nc, k, a)
    mosa(nc, k, a, "mosa2")


def macaron_kernel(nc, out, **a):
    with ExitStack() as ctx:
        k = Kernel()
        open_buffers(nc, ctx, k)
        setup(nc, k, a)
        whole(nc, k, a)
        stored = ctx.enter_context(nc.semaphore("stored"))
        with nc.Block() as block:
            @block.sync
            def _(sp):
                sp.dma_start(out.rearrange("b (t p) d -> p (b t) d", p=P), k.x[:, :, :]).then_inc(stored, 16)
                sp.wait_ge(stored, 16)


_INS = ["L0_attn_x", "L0_attn_w_qkv", "L0_attn_w_proj", "L0_attn_b_proj", "L0_ffn_g1", "L0_ffn_Wq", "L0_ffn_Wdkv",
        "L0_ffn_Wuk", "L0_ffn_Wuv", "L0_ffn_Wo", "L0_ffn_g2", "L0_ffn_gate_w", "L0_ffn_w1", "L0_ffn_w2",
        "L1_attn_ln1_g", "L1_attn_ln1_b", "L1_attn_Wq", "L1_attn_bq", "L1_attn_Wk", "L1_attn_bk", "L1_attn_w_g",
        "L1_attn_Wp", "L1_attn_bp", "L1_attn_Wf", "L1_attn_bf", "L1_attn_ln2_g", "L1_attn_ln2_b", "L1_attn_W1",
        "L1_attn_b1", "L1_attn_W2", "L1_attn_b2", "L1_ffn_Wr", "L1_ffn_Wqkv", "L1_ffn_Wo"]


def kernel(**inputs):
    import concourse.bacc as _bacc
    from concourse.bass_utils import run_bass_kernel_spmd as _run

    nc = _bacc.Bacc("TRN2", target_bir_lowering=False, num_devices=1)
    arrays, args = {}, {}
    for name in _INS + ["rope"]:
        arr = np.ascontiguousarray(rope_table() if name == "rope" else inputs[name])
        arrays[f"in_{name}"] = arr
        args[name] = nc.dram_tensor(f"in_{name}", arr.shape, mybir.dt.from_np(arr.dtype), kind="ExternalInput").ap()
    out = nc.dram_tensor("out_0", (B, N, D), F32, kind="ExternalOutput").ap()
    macaron_kernel(nc, out, **args)
    r = _run(nc, [arrays], core_ids=[0])
    return r.results[0]["out_0"]
```

```python
from contextlib import ExitStack

import numpy as np

import concourse.bass as bass
from concourse import mybir

P = 128
B = 4
N = 512
D = 128
NT = N // P
TILES = B * NT
H = 16
HD = D // H
QUADS = H // 4
SLOT = 64
EXPERTS = 8
EXP_DIM = 256
DEPTH = 4
ADIM = 256
HID = 512
MEXP = 8
MK = 64
ROT = 64
NEG = -1.0e30

ALU = mybir.AluOpType
ACT = mybir.ActivationFunctionType
F32 = mybir.dt.float32
BF16 = mybir.dt.bfloat16
I32 = mybir.dt.int32
AX = mybir.AxisListType


class Signal:

    def __init__(self, sem, per):
        self.sem, self.per = sem, per

    def __call__(self, b, k):
        return b * self.per + k


class Chain:

    def __init__(self, eng, sem, per):
        self.eng, self.sem, self.per, self.n, self.b = eng, sem, per, 0, 0

    def start(self, b):
        self.b, self.n = b, 0

    def __call__(self, ins):
        ins.then_inc(self.sem, 1)
        self.n += 1

    def wait(self):
        self.eng.wait_ge(self.sem, self.b * self.per + self.n)

    def wait_apart(self, go):
        self.wait()
        self.eng.sem_inc(go, 1)

    def end(self):
        assert self.n == self.per, (self.sem.name, self.n)


class Semaphores:

    def __init__(self, nc, ctx):
        self.nc, self.taken = nc, []
        ctx.callback(self.give_back)

    def __call__(self, name):
        self.taken.append(self.nc.alloc_semaphore(name))
        return self.taken[-1]

    def give_back(self):
        self.nc.clear_and_free_semaphores(self.taken)
        self.nc.all_engine_barrier()


class Kernel:
    pass


def open_buffers(nc, ctx, k):
    def sb(name, shape, dt=F32):
        return ctx.enter_context(nc.sbuf_tensor(name, shape, dt))

    k.x = sb("x", [P, TILES, D])
    k.y = sb("y", [P, TILES, D])
    k.ident = sb("ident", [P, P])
    k.identb = sb("identb", [P, P], BF16)
    k.mask_qk = sb("mask_qk", [P, P], BF16)
    k.mask_kq = sb("mask_kq", [P, P], BF16)
    k.half = sb("half", [P, TILES])
    k.w_mla = sb("w_mla", [P, 3 * D])
    k.w_mla_out = sb("w_mla_out", [P, D])
    k.w_att = sb("w_att", [P, 3 * D])
    k.w_att_out = sb("w_att_out", [P, D])
    k.b_att = sb("b_att", [P, D])
    k.w1 = sb("expert_w1", [P, EXPERTS, EXP_DIM])
    k.w2 = sb("expert_w2", [P, EXPERTS, EXP_DIM // P, D])
    k.gate_w = sb("gate_w", [P, EXPERTS])
    k.g2 = sb("g2", [P, 1])
    k.router_rows = sb("router_rows", [MEXP, P])
    k.w_qkv = sb("mosa_w_qkv", [P, MEXP, 3 * D])
    k.w_rot = sb("mosa_w_rot", [P, MEXP, 2, ROT])
    k.w_out = sb("mosa_w_out", [P, MEXP, D])
    k.rope = sb("rope", [P, NT, P])
    k.experts_in = ctx.enter_context(nc.semaphore("experts_weights_in"))
    k.mosa_in = ctx.enter_context(nc.semaphore("mosa_weights_in"))
    k.rot_made = ctx.enter_context(nc.semaphore("rot_weights_made"))
    k.bank = [ctx.enter_context(nc.psum_tensor(f"bank{i}", [P, 512], F32)) for i in range(8)]


def setup(nc, k, a):
    with ExitStack() as ctx:
        take = Semaphores(nc, ctx)

        def sb(name, shape, dt=F32):
            return ctx.enter_context(nc.sbuf_tensor(name, shape, dt))

        def sem(name):
            return take(name)

        wdkv = sb("wdkv", [P, 64])
        wukv = sb("wukv", [64, 2 * D])
        wdkvT = sb("wdkvT", [64, P])
        g1 = sb("g1", [P, 1])
        loaded, weights, consts, ident_ok, step, ps, evac, done = (
            sem(n) for n in ("x_loaded", "weights_loaded", "consts_made", "ident_made", "setup_step",
                             "fold_ps", "fold_sb", "fold_done"))
        with nc.Block() as block:
            @block.sync
            def _(sp):
                sp.dma_start(wdkv[:, :], a["L0_ffn_Wdkv"]).then_inc(weights, 16)
                sp.dma_start(wukv[:, 0:D], a["L0_ffn_Wuk"]).then_inc(weights, 16)
                sp.dma_start(wukv[:, D:2 * D], a["L0_ffn_Wuv"]).then_inc(weights, 16)
                sp.dma_start(g1[:, :], a["L0_ffn_g1"].rearrange("(p o) -> p o", o=1)).then_inc(weights, 16)
                sp.dma_start(k.w_mla[:, 0:D], a["L0_ffn_Wq"]).then_inc(weights, 16)
                sp.dma_start(k.w_mla_out[:, :], a["L0_ffn_Wo"]).then_inc(weights, 16)
                sp.dma_start(k.w_att[:, :], a["L0_attn_w_qkv"]).then_inc(weights, 16)
                sp.dma_start(k.w_att_out[:, :], a["L0_attn_w_proj"]).then_inc(weights, 16)
                sp.dma_start(k.b_att[:, :], a["L0_attn_b_proj"].partition_broadcast(P)).then_inc(weights, 16)
                sp.dma_start(k.gate_w[:, :], a["L0_ffn_gate_w"]).then_inc(k.experts_in, 16)
                sp.dma_start(k.g2[:, :], a["L0_ffn_g2"].rearrange("(p o) -> p o", o=1)).then_inc(k.experts_in, 16)
                sp.dma_start(k.w1[:, :, :], a["L0_ffn_w1"].rearrange("e d h -> d e h")).then_inc(k.experts_in, 16)
                sp.dma_start(k.w2[:, :, :, :],
                             a["L0_ffn_w2"].rearrange("e (c p) d -> p e c d", p=P)).then_inc(k.experts_in, 16)
                sp.dma_start(k.router_rows[:, :], a["L1_ffn_Wr"]).then_inc(k.mosa_in, 16)
                sp.dma_start(k.w_qkv[:, :, :], a["L1_ffn_Wqkv"].rearrange("e d j -> d e j")).then_inc(k.mosa_in, 16)
                sp.dma_start(k.w_out[:, :, :], a["L1_ffn_Wo"].rearrange("e d j -> d e j")).then_inc(k.mosa_in, 16)
                sp.dma_start(k.rope[:, :, :], a["rope"].rearrange("(t p) j -> p t j", p=P)).then_inc(k.mosa_in, 16)
                sp.wait_ge(loaded, 16)
                sp.wait_ge(weights, 16 * 9)

            @block.scalar
            def _(act):
                act.dma_start(k.x[:, :, :], a["L0_attn_x"].rearrange("b (t p) d -> p (b t) d", p=P)).then_inc(loaded, 16)

            @block.gpsimd
            def _(pool):
                pool.memset(k.ident[:, :], 0.0).then_inc(consts, 1)
                pool.memset(k.mask_qk[:, :], 0.0).then_inc(consts, 1)
                pool.memset(k.mask_kq[:, :], 0.0).then_inc(consts, 1)
                pool.memset(k.half[:, :], -0.5).then_inc(consts, 1)
                pool.wait_ge(consts, 4)
                pool.affine_select(out=k.ident[:, :], in_=k.ident[:, :], compare_op=ALU.not_equal, fill=1.0,
                                   base=0, pattern=[[-1, P]], channel_multiplier=1).then_inc(ident_ok, 1)
                pool.affine_select(out=k.mask_qk[:, :], in_=k.mask_qk[:, :], compare_op=ALU.is_ge, fill=NEG,
                                   base=0, pattern=[[-1, P]], channel_multiplier=1).then_inc(ident_ok, 1)
                pool.affine_select(out=k.mask_kq[:, :], in_=k.mask_kq[:, :], compare_op=ALU.is_ge, fill=NEG,
                                   base=0, pattern=[[1, P]], channel_multiplier=-1).then_inc(ident_ok, 1)
                pool.wait_ge(ident_ok, 3)
                pool.tensor_copy(k.identb[:, :], k.ident[:, :]).then_inc(consts, 1)

            @block.tensor
            def _(pe):
                pe.wait_ge(ident_ok, 3)
                pe.wait_ge(weights, 16 * 9)
                pe.transpose(k.bank[0][0:64, 0:P], wdkv[:, :], k.ident[:, :]).then_inc(ps, 1)
                pe.wait_ge(evac, 1)
                pe.matmul(k.bank[1][:, 0:2 * D], wdkvT[:, :], wukv[:, :], start=True, stop=True).then_inc(ps, 1)

            @block.vector
            def _(dve):
                dve.wait_ge(ps, 1)
                dve.tensor_copy(wdkvT[:, :], k.bank[0][0:64, 0:P]).then_inc(evac, 1)
                dve.wait_ge(weights, 16 * 9)
                dve.tensor_scalar(k.w_mla[:, 0:D], k.w_mla[:, 0:D], g1[:, 0:1], HD ** -0.5,
                                  ALU.mult, ALU.mult).then_inc(done, 1)
                dve.tensor_scalar(k.w_att[:, 0:D], k.w_att[:, 0:D], HD ** -0.5, None, ALU.mult).then_inc(done, 1)
                dve.wait_ge(ps, 2)
                dve.tensor_scalar(k.w_mla[:, D:3 * D], k.bank[1][:, 0:2 * D], g1[:, 0:1], None,
                                  ALU.mult).then_inc(done, 1)


def attention(nc, k, name, causal):
    with ExitStack() as ctx:
        take = Semaphores(nc, ctx)

        def sb(n, shape, dt=F32):
            return ctx.enter_context(nc.sbuf_tensor(f"{name}_{n}", shape, dt))

        def sem(n):
            return take(f"{name}_{n}")

        def signal(n, per):
            return Signal(sem(n), per)

        w_in, w_out = (k.w_mla, k.w_mla_out) if causal else (k.w_att, k.w_att_out)
        eps = 1e-5
        stats = sb("stats", [P, TILES, 6])
        mv = sb("mv", [P, TILES, 2])
        half2 = sb("half2", [P, 2, TILES])
        var = sb("var", [P, 2, TILES])
        scale = sb("scale", [P, 2, TILES])
        h = sb("h", [P, NT, D])
        hT = sb("hT", [P, N])
        qk32 = sb("qk32", [P, NT, 2, D])
        v_new = sb("v_new", [P, NT, D])
        rest = sb("rest", [P, NT, 2, D])
        hi = sb("hi", [P, NT, 2, D], BF16)
        mid = sb("mid", [P, NT, 2, D], BF16)
        lo = sb("lo", [P, NT, 2, D], BF16)
        q_parts = sb("q_parts", [P, NT, H, SLOT], BF16)
        k_parts = sb("k_parts", [P, NT, H, SLOT], BF16)
        v_ones = sb("v_ones", [P, NT, H, 32])
        qT_max = sb("qT_max", [P, 2, N], BF16)
        qT = sb("qT", [P, 2, 2, N], BF16)
        kT = sb("kT", [P, 2, 4, N], BF16)
        negmax = sb("negmax", [P, H, NT])
        nm_rest = sb("nm_rest", [P, H, NT])
        nm_hi = sb("nm_hi", [P, H, NT], BF16)
        nm_mid = sb("nm_mid", [P, H, NT], BF16)
        probs = sb("probs", [P, 2, 4, NT * N])
        oT = sb("oT", [P, 2, N])
        rsum = sb("rsum", [P, 2, NT, 4])
        o = sb("o", [P, NT, D])
        oTn = sb("oTn", [P, N])

        bank = k.bank
        TQ = bank[0][:, 0:256].bitcast(BF16)
        TK = bank[0][:, 256:512].bitcast(BF16)
        S1 = [bank[1], bank[2]]
        AV = bank[3]
        S2 = [bank[4], bank[5], bank[6]]
        X = bank[7]
        XQ = bank[7][:, 0:256].bitcast(BF16)

        if causal:
            at = {0: 0, 1: 512, 3: 896, 2: 1024}
            rounds = [r for j in range(4) for r in ([(j, 0, 0)], [(j, 1, 0), (j, 3, 384)])]
            rounds[4:4] = [[(0, 2, 0), (1, 2, 256)]]
            rounds.append([(2, 2, 0), (3, 2, 256)])
        else:
            at = {kt: 512 * kt for kt in range(NT)}
            rounds = [[(j, kt, 0)] for j in range(4) for kt in range(NT)]
        R = len(rounds)
        assert QUADS * R % 3 == 1
        PAIRS = H // 2

        def q_from(kt):
            return P * kt if causal else 0

        def keys(t):
            return P * (t + 1) if causal else N

        s_go, s_init, s_var, s_scale = sem("pool_go"), sem("init"), sem("var_done"), sem("scale_done")
        s_aggr = sem("aggr_done")
        h_ready = signal("h_ready", 1)
        hT_ps = signal("hT_ps", 1)
        hT_sb = signal("hT_sb", 1)
        qkv_ps = signal("qkv_ps", NT)
        qk_sb = signal("qk_sb", NT)
        v_sb = signal("v_sb", NT)
        v_placed = signal("v_placed", 1)
        s_stats = sem("stats_done")
        split = signal("split", 4 * NT)
        parts_placed = signal("parts_placed", 2)
        turned_max = signal("turned_max", PAIRS)
        k_sb = signal("k_sb", PAIRS)
        max_ps = signal("max_ps", PAIRS * 2 * NT)
        max_read = signal("max_read", PAIRS * 2 * NT)
        max_part = signal("max_part", 3 * PAIRS)
        max_rows = signal("max_rows", PAIRS)
        turned_q = signal("turned_q", PAIRS)
        q_sb = signal("q_sb", PAIRS)
        score_ps = signal("score_ps", QUADS * R)
        probs_sb = signal("probs_sb", QUADS * R)
        av_ps = signal("av_ps", QUADS)
        av_sb = signal("av_sb", QUADS)
        turned_o = signal("turned_o", QUADS)
        sum_inv = signal("sum_inv", QUADS)
        o_sb = signal("o_sb", QUADS)
        oT_ps = signal("oT_ps", 1)
        oT_sb = signal("oT_sb", 1)
        proj_ps = signal("proj_ps", 1)
        out_sb = signal("out_sb", 2)

        def fronts(d, g):
            a, b = 2 * g, 2 * g + 1
            return [("turn_max", d, a), ("max", d, a, 0), ("max", d, a, 1), ("turn_max", d, b), ("max", d, a, 2),
                    ("max", d, a, 3), ("max_rows", d, a), ("max", d, b, 0), ("max", d, b, 1), ("max", d, b, 2),
                    ("turn_q", d, a), ("max", d, b, 3), ("max_rows", d, b)]

        def prep(d):
            return [("h", d), ("qkv", d, 0), ("qkv", d, 1), ("split", d, 0), ("qkv", d, 2), ("split", d, 1),
                    ("qkv", d, 3), ("split", d, 2), ("split", d, 3)]

        def after(d, g):
            return [("av", d, g, kt) for kt in range(NT)] + [("o", d, g)]

        def merged(a, b):
            a, end = a[:-4], a[-4:]
            out, n = [], 0
            for i, step in enumerate(a):
                out.append(step)
                while n < len(b) and n * len(a) < (i + 1) * len(b):
                    out.append(b[n])
                    n += 1
            return out + b[n:] + end

        def beside(d, g, side, placing=[]):
            side = side[:LATE] + [("turn_q", d, 2 * g + 1)] + placing + side[LATE:]
            out = []
            for r in range(R):
                out.append(("score", d, g, r))
                take = -(-len(side) // (R - r))
                out += side[:take]
                side = side[take:]
            return out

        LATE, AHEAD = 4, 7
        quads = [beside(0, g, merged(fronts(0, g + 1), after(0, g - 1) if g else [])) for g in range(2)]
        tail = after(0, QUADS - 1) + [("turn_o", 0), ("proj", 0)]
        prologue = prep(0) + [("place", 0), ("place_last", 0), ("place_v", 0)] + fronts(0, 0) + quads[0]
        steady = (quads[1] +
                  beside(0, 2, merged(merged(fronts(0, 3), prep(1)[:AHEAD]) + prep(1)[AHEAD:] + [("place", 1)],
                                      after(0, 1))) +
                  beside(0, 3, after(0, 2)[:4] + merged(fronts(1, 0), after(0, 2)[4:]), [("place_last", 1)]) +
                  beside(1, 0, tail[:2] + merged(fronts(1, 1), tail[2:NT] + [("place_v", 1)] + tail[NT:])))
        epilogue = (quads[1] + beside(0, 2, merged(fronts(0, 3), after(0, 1))) +
                    beside(0, 3, after(0, 2)) + tail)
        phases = (("first", prologue), ("loop", steady), ("last", epilogue))
        in_x = ("h", "qkv", "turn_q", "o", "turn_o", "proj")
        assert [s for s in prologue if s[0] in in_x][-1] == ("turn_q", 0, 2)
        assert [s for s in steady if s[0] in in_x][-1] == ("turn_q", 1, 2)

        def run(eng, does):
            for phase, steps in phases:
                if phase == "loop":
                    with eng.Fori(0, B - 1) as b:
                        play(b, steps, does, prologue, 0)
                else:
                    play(0 if phase == "first" else B - 1, steps, does,
                         [] if phase == "first" else steady, 0 if phase == "first" else 1)

        def play(b, steps, does, before, shift):
            last = [(s[0], s[1] - shift) + s[2:] for s in before if s[0] in in_x][-1:]
            for s in steps:
                if s[0] in does:
                    does[s[0]](b + s[1], *s[2:], **({"x_was": (b, last[0] if last else None)}
                                                    if s[0] in in_x and does is PE_DOES else {}))
                if s[0] in in_x:
                    last = [s]

        PE_DOES = {}

        def wait_x_free(eng, x_was):
            b, s = x_was
            if s is None:
                return
            b = b + s[1]
            if s[0] == "h":
                eng.wait_ge(hT_sb.sem, hT_sb(b, 1))
            elif s[0] == "qkv":
                eng.wait_ge(v_sb.sem, v_sb(b, s[2] + 1))
            elif s[0] == "turn_q":
                eng.wait_ge(q_sb.sem, q_sb(b, s[2] + 1))
            elif s[0] == "o":
                eng.wait_ge(o_sb.sem, o_sb(b, s[2] + 1))
            elif s[0] == "turn_o":
                eng.wait_ge(oT_sb.sem, oT_sb(b, 1))
            elif s[0] == "proj":
                eng.wait_ge(out_sb.sem, out_sb(b, 1))

        with nc.Block() as block:
            @block.sync
            def _(sp):
                sp.nop()

            @block.gpsimd
            def _(pool):
                pool.memset(half2[:, :, :], -0.5).then_inc(s_init, 1)
                pool.wait_ge(s_init, 1)
                for i, tiles in enumerate((slice(0, NT), slice(NT, TILES))):
                    pool.wait_ge(s_var, i + 1)
                    pool.tensor_tensor(scale[:, :, tiles], var[:, :, tiles], half2[:, :, tiles],
                                       ALU.pow).then_inc(s_scale, 1)
                    if i == 0:
                        pool.memset(kT[:, :, :, :], 0.0).then_inc(s_init, 1)
                pool.memset(v_ones[:, :, :, :], 0.0).then_inc(s_init, 1)
                pool.wait_ge(s_init, 3)
                pool.memset(v_ones[:, :, :, HD:HD + 1], 1.0).then_inc(s_init, 1)

                def wait_apart(s, value):
                    pool.wait_ge(s.sem, value)
                    pool.sem_inc(s_go, 1)

                def place_v_step(b):
                    wait_apart(v_sb, v_sb(b, NT))
                    wait_apart(av_ps, av_ps(b, 0)) if not isinstance(b, int) or b > 0 else None
                    pool.tensor_copy(v_ones[:, :, :, 0:HD],
                                     v_new[:, :, :].rearrange("p t (h e) -> p t h e", e=HD)).then_inc(v_placed.sem, 1)

                def max_rows_step(b, p):
                    hs = slice(2 * p, 2 * p + 2)

                    def rows(i):
                        return q_parts[:, :, hs, 48 + i].rearrange("p t h -> p h t")

                    wait_apart(max_read, max_read(b, 8 * (p + 1)))
                    pool.tensor_copy(nm_hi[:, hs, :], negmax[:, hs, :]).then_inc(max_part.sem, 1)
                    pool.wait_ge(max_part.sem, max_part(b, 3 * p + 1))
                    pool.tensor_tensor(nm_rest[:, hs, :], negmax[:, hs, :], nm_hi[:, hs, :],
                                       ALU.subtract).then_inc(max_part.sem, 1)
                    pool.tensor_copy(rows(0), nm_hi[:, hs, :])
                    wait_apart(max_part, max_part(b, 3 * p + 2))
                    pool.tensor_copy(nm_mid[:, hs, :], nm_rest[:, hs, :]).then_inc(max_part.sem, 1)
                    pool.wait_ge(max_part.sem, max_part(b, 3 * p + 3))
                    pool.tensor_tensor(rows(2), nm_rest[:, hs, :], nm_mid[:, hs, :], ALU.subtract)
                    pool.tensor_copy(rows(1), nm_mid[:, hs, :]).then_inc(max_rows.sem, 1)

                run(pool, {"place_v": place_v_step, "max_rows": max_rows_step})

            @block.scalar
            def _(act):
                def h_step(b):
                    act.wait_ge(hT_ps.sem, hT_ps(b, 1))
                    act.copy(hT[:, :], X[:, :]).then_inc(hT_sb.sem, 1)

                def qkv_step(b, t):
                    act.wait_ge(qkv_ps.sem, qkv_ps(b, t + 1))
                    act.copy(qk32[:, t, :, :].rearrange("p s d -> p (s d)"), X[:, 0:2 * D]).then_inc(qk_sb.sem, 1)
                    act.copy(v_new[:, t, :], X[:, 2 * D:3 * D]).then_inc(v_sb.sem, 1)

                def turn_max_step(b, p):
                    g, i = p // 2, 2 * (p % 2)
                    act.wait_ge(turned_max.sem, turned_max(b, p + 1))
                    if isinstance(b, int) and b == 0 and p == 0:
                        act.wait_ge(s_init, 2)
                    if not (isinstance(b, int) and b == 0 and g < 2):
                        act.wait_ge(score_ps.sem, score_ps(b, R * (g - 1)))
                        act.wait_ge(max_ps.sem, max_ps(b, 8 * (p - 1)))
                    act.copy(qT_max[:, p % 2, :], TQ[:, :])
                    act.copy(kT[0:64, g % 2, i, :], TK[0:64, :])
                    act.copy(kT[64:128, g % 2, i + 1, :], TK[64:128, :]).then_inc(k_sb.sem, 1)

                def score_step(b, g, r):
                    n = R * g + r
                    act.wait_ge(score_ps.sem, score_ps(b, n + 1))
                    if r == 0 and not (isinstance(b, int) and b == 0 and g < 2):
                        act.wait_ge(av_ps.sem, av_ps(b, g - 1))
                    j, kt = rounds[r][0][:2]
                    if causal and kt == 2:
                        dst = probs[:, g % 2, j:j + 2, at[2]:at[2] + 256]
                        src = S2[n % 3][:, :].rearrange("p (j q) -> p j q", j=2)
                    else:
                        dst = probs[:, g % 2, j, at[kt]:at[kt] + N]
                        src = S2[n % 3][:, :]
                    act.activation(dst, src, ACT.Exp).then_inc(probs_sb.sem, 1)

                def av_step(b, g, kt):
                    if kt < NT - 1:
                        return
                    act.wait_ge(av_ps.sem, av_ps(b, g + 1))
                    act.copy(oT[:, g % 2, :], AV[:, :]).then_inc(av_sb.sem, 1)

                def turn_o_step(b):
                    act.wait_ge(oT_ps.sem, oT_ps(b, 1))
                    act.copy(oTn[:, :], X[:, :]).then_inc(oT_sb.sem, 1)

                run(act, {"h": h_step, "qkv": qkv_step, "turn_max": turn_max_step, "score": score_step,
                          "av": av_step, "turn_o": turn_o_step})

            @block.vector
            def _(dve):
                def variances(i, tiles):
                    for t in tiles:
                        ins = dve.bn_stats(stats[:, t, :], k.x[:, t, :])
                    ins.then_inc(s_stats, 1)
                    dve.wait_ge(s_stats, i + 1)
                    for t in tiles:
                        ins = dve.bn_aggr(mv[:, t, :], stats[:, t, :])
                    ins.then_inc(s_aggr, 1)
                    dve.wait_ge(s_aggr, i + 1)
                    own = slice(tiles[0], tiles[-1] + 1)
                    dve.tensor_scalar(var[:, 0, own], mv[:, own, 1], eps, None, ALU.add)
                    dve.tensor_scalar(var[:, 1, own], mv[:, own, 1], 1.0 + 1e-6 if causal else 1.0,
                                      1e-6 * eps if causal else eps, ALU.mult, ALU.add).then_inc(s_var, 1)

                variances(0, range(NT))
                dve.memset(q_parts[:, :, :, 51:SLOT], 0.0)
                dve.memset(k_parts[:, :, :, 51:SLOT], 0.0)
                dve.memset(k_parts[:, :, :, 48:51], 1.0)

                def h_step(b):
                    first = isinstance(b, int) and b == 0
                    dve.wait_ge(s_scale, 1 if first else 2)
                    for t in range(NT):
                        tok = k.x[:, b * NT + t, :]
                        if causal:
                            dve.tensor_scalar(k.y[:, b * NT + t, :], tok, mv[:, b * NT + t, 0:1],
                                              scale[:, 0, bass.ds(b * NT + t, 1)], ALU.subtract, ALU.mult)
                        ins = dve.tensor_scalar(h[:, t, :], tok, mv[:, b * NT + t, 0:1],
                                                scale[:, 1, bass.ds(b * NT + t, 1)], ALU.subtract, ALU.mult)
                    ins.then_inc(h_ready.sem, 1)
                    if first:
                        variances(1, range(NT, TILES))

                def split_step(b, t):
                    n = 4 * t
                    dve.wait_ge(qk_sb.sem, qk_sb(b, t + 1))
                    dve.tensor_copy(hi[:, t, :, :], qk32[:, t, :, :]).then_inc(split.sem, 1)
                    dve.wait_ge(split.sem, split(b, n + 1))
                    dve.tensor_tensor(rest[:, t, :, :], qk32[:, t, :, :], hi[:, t, :, :],
                                      ALU.subtract).then_inc(split.sem, 1)
                    dve.wait_ge(split.sem, split(b, n + 2))
                    dve.tensor_copy(mid[:, t, :, :], rest[:, t, :, :]).then_inc(split.sem, 1)
                    dve.wait_ge(split.sem, split(b, n + 3))
                    dve.tensor_tensor(lo[:, t, :, :], rest[:, t, :, :], mid[:, t, :, :],
                                      ALU.subtract).then_inc(split.sem, 1)

                def place(dst, i, slots, heads):
                    for s, part in enumerate(slots):
                        ins = dve.tensor_copy(dst[:, :, heads, 8 * s:8 * s + 8],
                                              part[:, :, i, :].rearrange("p t (h e) -> p t h e", e=HD)[:, :, heads, :])
                    return ins

                def place_q(heads):
                    dve.memset(q_parts[:, :, heads, 48:51], 0.0)
                    place(q_parts, 0, (hi, hi, hi, mid, mid, lo), heads).then_inc(parts_placed.sem, 1)

                def place_step(b):
                    dve.wait_ge(split.sem, split(b, 4 * NT))
                    place(k_parts, 1, (hi, mid, lo, hi, mid, hi), slice(0, H))
                    place_q(slice(0, H - 2))

                def place_last_step(b):
                    dve.wait_ge(split.sem, split(b, 4 * NT))
                    place_q(slice(H - 2, H))

                def max_step(b, p, t):
                    for j in range(2):
                        n = 8 * p + 2 * t + j
                        dve.wait_ge(max_ps.sem, max_ps(b, n + 1))
                        dve.tensor_reduce(negmax[:, 2 * p + j, t:t + 1], S1[j][:, 0:keys(t)], AX.X, ALU.max,
                                          negate=True).then_inc(max_read.sem, 1)

                def turn_q_step(b, p):
                    dve.wait_ge(turned_q.sem, turned_q(b, p + 1))
                    if not (isinstance(b, int) and b == 0 and p < 4):
                        dve.wait_ge(score_ps.sem, score_ps(b, R * (p // 2 - 1)))
                    dve.tensor_copy(qT[:, (p // 2) % 2, p % 2, :], XQ[:, :]).then_inc(q_sb.sem, 1)

                def o_step(b, g):
                    dve.wait_ge(turned_o.sem, turned_o(b, g + 1))
                    Xo = X[:, :].rearrange("p (t j e) -> p t j e", t=NT, j=4)
                    dve.reciprocal(rsum[:, g % 2, :, :], Xo[:, :, :, HD]).then_inc(sum_inv.sem, 1)
                    dve.wait_ge(sum_inv.sem, sum_inv(b, g + 1))
                    oo = o[:, :, :].rearrange("p t (g j e) -> p t g j e", g=QUADS, j=4)
                    dve.tensor_tensor(oo[:, :, g, :, :], Xo[:, :, :, 0:HD],
                                      rsum[:, g % 2, :, :].unsqueeze(3).to_broadcast([P, NT, 4, HD]),
                                      ALU.mult).then_inc(o_sb.sem, 1)

                def proj_step(b):
                    dve.wait_ge(proj_ps.sem, proj_ps(b, 1))
                    dst = k.y if causal else k.x
                    tok = dst[:, bass.ds(b * NT, NT), :]
                    dve.tensor_tensor(tok, X[:, :].rearrange("p (t d) -> p t d", t=NT), tok,
                                      ALU.add).then_inc(out_sb.sem, 1)
                    dve.wait_ge(out_sb.sem, out_sb(b, 1))
                    if causal:
                        dve.sem_inc(out_sb.sem, 1)
                    else:
                        dve.tensor_tensor(tok, k.b_att[:, :].unsqueeze(1).to_broadcast([P, NT, D]), tok,
                                          ALU.add).then_inc(out_sb.sem, 1)

                run(dve, {"h": h_step, "split": split_step, "place": place_step, "place_last": place_last_step,
                          "max": max_step, "turn_q": turn_q_step,
                          "o": o_step, "proj": proj_step})

            @block.tensor
            def _(pe):
                def h_step(b, x_was):
                    pe.wait_ge(h_ready.sem, h_ready(b, 1))
                    wait_x_free(pe, x_was)
                    for t in range(NT):
                        ins = pe.transpose(X[:, P * t:P * t + P], h[:, t, :], k.ident[:, :])
                    ins.then_inc(hT_ps.sem, 1)

                def qkv_step(b, t, x_was):
                    wait_x_free(pe, x_was)
                    if t == 0:
                        pe.wait_ge(hT_sb.sem, hT_sb(b, 1))
                    pe.matmul(X[:, 0:3 * D], hT[:, P * t:P * t + P], w_in[:, :],
                              start=True, stop=True).then_inc(qkv_ps.sem, 1)

                def turn(dst, parts, p):
                    for t in range(NT):
                        ins = pe.transpose(dst[:, P * t:P * t + P],
                                           parts[:, t, 2 * p:2 * p + 2, :].rearrange("p h s -> p (h s)"),
                                           k.identb[:, :])
                    return ins

                def turn_max_step(b, p):
                    if p in (0, PAIRS - 1):
                        pe.wait_ge(parts_placed.sem, parts_placed(b, 1 if p == 0 else 2))
                    if not (isinstance(b, int) and b == 0 and p == 0):
                        pe.wait_ge(k_sb.sem, k_sb(b, p))
                    turn(TQ, q_parts, p)
                    turn(TK, k_parts, p).then_inc(turned_max.sem, 1)

                def max_step(b, p, t):
                    if t == 0:
                        pe.wait_ge(k_sb.sem, k_sb(b, p + 1))
                    for j in range(2):
                        n = 8 * p + 2 * t + j
                        if not (isinstance(b, int) and b == 0 and n < 2):
                            pe.wait_ge(max_read.sem, max_read(b, n - 1))
                        kt = kT[:, (p // 2) % 2, 2 * (p % 2) + j, 0:keys(t)]
                        ins = pe.matmul(S1[j][:, 0:keys(t)], qT_max[:, p % 2, P * t:P * t + P], kt,
                                        start=True, stop=not causal)
                        if causal:
                            ins = pe.matmul(S1[j][:, P * t:P * t + P], k.identb[:, :], k.mask_qk[:, :],
                                            start=False, stop=True)
                        ins.then_inc(max_ps.sem, 1)

                def turn_q_step(b, p, x_was):
                    pe.wait_ge(max_rows.sem, max_rows(b, p + 1))
                    wait_x_free(pe, x_was)
                    turn(XQ, q_parts, p).then_inc(turned_q.sem, 1)

                def score_step(b, g, r):
                    n = R * g + r
                    if r == 0:
                        pe.wait_ge(q_sb.sem, q_sb(b, 2 * g + 1))
                    elif rounds[r][0][0] == 2 and rounds[r - 1][0][0] < 2:
                        pe.wait_ge(q_sb.sem, q_sb(b, 2 * g + 2))
                    if not (isinstance(b, int) and b == 0 and n < 3):
                        pe.wait_ge(probs_sb.sem, probs_sb(b, n - 2 if n else 0))
                    for j, kt, col in rounds[r]:
                        w = N - q_from(kt)
                        out = S2[n % 3]
                        ins = pe.matmul(out[:, col:col + w], kT[:, g % 2, j, P * kt:P * kt + P],
                                        qT[:, g % 2, j // 2, q_from(kt):N], start=True, stop=not causal)
                        if causal:
                            ins = pe.matmul(out[:, col:col + P], k.identb[:, :], k.mask_kq[:, :],
                                            start=False, stop=True)
                    ins.then_inc(score_ps.sem, 1)

                def av_step(b, g, kt):
                    if kt == 0:
                        pe.wait_ge(probs_sb.sem, probs_sb(b, R * (g + 1)))
                        if g == 0:
                            pe.wait_ge(v_placed.sem, v_placed(b, 1))
                        if not (isinstance(b, int) and b == 0 and g == 0):
                            pe.wait_ge(av_sb.sem, av_sb(b, g))
                    for j in range(4):
                        w = N - q_from(kt)
                        ins = pe.matmul(AV[32 * j:32 * j + 32, q_from(kt):N], v_ones[:, kt, 4 * g + j, :],
                                        probs[:, g % 2, j, at[kt]:at[kt] + w], start=kt == 0, stop=kt == NT - 1)
                    if kt == NT - 1:
                        ins.then_inc(av_ps.sem, 1)

                def o_step(b, g, x_was):
                    pe.wait_ge(av_sb.sem, av_sb(b, g + 1))
                    wait_x_free(pe, x_was)
                    for t in range(NT):
                        ins = pe.transpose(X[:, P * t:P * t + P], oT[:, g % 2, P * t:P * t + P], k.ident[:, :])
                    ins.then_inc(turned_o.sem, 1)

                def turn_o_step(b, x_was):
                    pe.wait_ge(o_sb.sem, o_sb(b, QUADS))
                    wait_x_free(pe, x_was)
                    for t in range(NT):
                        ins = pe.transpose(X[:, P * t:P * t + P], o[:, t, :], k.ident[:, :])
                    ins.then_inc(oT_ps.sem, 1)

                def proj_step(b, x_was):
                    pe.wait_ge(oT_sb.sem, oT_sb(b, 1))
                    wait_x_free(pe, x_was)
                    for t in range(NT):
                        ins = pe.matmul(X[:, P * t:P * t + P], oTn[:, P * t:P * t + P], w_out[:, :],
                                        start=True, stop=True)
                    ins.then_inc(proj_ps.sem, 1)

                PE_DOES.update({"h": h_step, "qkv": qkv_step, "turn_max": turn_max_step, "max": max_step,
                                "turn_q": turn_q_step, "score": score_step, "av": av_step, "o": o_step,
                                "turn_o": turn_o_step, "proj": proj_step})
                run(pe, PE_DOES)


def experts(nc, k, a, name):
    with ExitStack() as ctx:
        take = Semaphores(nc, ctx)

        def sb(n, shape, dt=F32):
            return ctx.enter_context(nc.sbuf_tensor(f"{name}_{n}", shape, dt))

        def sem(n):
            return take(f"{name}_{n}")

        def signal(n, per):
            return Signal(sem(n), per)

        CH = EXP_DIM // P
        FAR = -3.0e38
        TAKEN = 3.0e38
        w1, w2, gate_w, g2 = k.w1, k.w2, k.gate_w, k.g2
        squares = sb("squares", [P, TILES, D])
        ms = sb("ms", [P, TILES])
        rms = sb("rms", [P, TILES])
        h = sb("h", [P, NT, D])
        hT = sb("hT", [P, N])
        logits = sb("logits", [P, NT, 16])
        left = sb("left", [P, NT, 16])
        best = sb("best", [P, NT, 8])
        drop = sb("drop", [P, NT, 8])
        taken = sb("taken", [P, NT, EXPERTS])
        away = sb("away", [P, NT, EXPERTS])
        share = sb("share", [P, NT, EXPERTS])
        total = sb("total", [P, NT])
        gates = sb("gates", [P, NT, EXPERTS])
        hidden = sb("hidden", [P, 2, CH, N])
        bank = k.bank
        T, G = bank[0], bank[1]

        s_weighed, s_go = sem("weighed"), sem("go")
        s_sq0 = sem("squares0_done")
        s_init, s_ms, s_rms, s_sq = sem("init"), sem("rms_step"), sem("rms_done"), sem("squares_done")
        h_ready = signal("h_ready", 1)
        hT_ps = signal("hT_ps", 1)
        hT_sb = signal("hT_sb", 1)
        gate_ps = signal("gate_ps", 1)
        away_sb = signal("away_sb", 1)
        share_sb = signal("share_sb", 1)
        hid_ps = signal("hid_ps", EXPERTS)
        hid_sb = signal("hid_sb", EXPERTS)
        out_ps = signal("out_ps", EXPERTS)

        with nc.Block() as block:
            @block.sync
            def _(sp):
                sp.nop()

            @block.gpsimd
            def _(pool):
                pool.memset(drop[:, :, :], FAR).then_inc(s_init, 1)
                pool.memset(logits[:, :, :], FAR).then_inc(s_init, 1)
                for n, own in enumerate((slice(0, NT), slice(NT, TILES))):
                    pool.wait_ge(s_sq0 if n == 0 else s_sq, 1)
                    pool.tensor_scalar(rms[:, own], ms[:, own], 1.0 / D, 1e-6, ALU.mult, ALU.add).then_inc(s_ms, 1)
                    pool.wait_ge(s_ms, n + 1)
                    pool.tensor_tensor(ms[:, own], rms[:, own], k.half[:, own], ALU.pow).then_inc(s_rms, 1)

            @block.scalar
            def _(act):
                for t in range(NT, TILES):
                    ins = act.activation(squares[:, t, :], k.y[:, t, :], ACT.Square, accum_out=ms[:, t:t + 1])
                ins.then_inc(s_sq, 1)
                act.wait_ge(k.experts_in, 64)

                def copy_h(b):
                    act.wait_ge(hT_ps.sem, hT_ps(b, 1))
                    act.mul(hT[:, :], T[:, :], g2[:, 0:1]).then_inc(hT_sb.sem, 1)

                def batch(b, more):
                    for e in range(EXPERTS):
                        act.wait_ge(hid_ps.sem, hid_ps(b, e + 1))
                        if more and e == EXPERTS - 1:
                            copy_h(b + 1)
                        if e >= 2:
                            act.wait_ge(out_ps.sem, out_ps(b, e - 1))
                        for c in range(CH):
                            ins = act.activation(hidden[:, e % 2, c, :], bank[4 + 2 * (e % 2) + c][:, :], ACT.Silu)
                        ins.then_inc(hid_sb.sem, 1)
                        if e == 0:
                            act.wait_ge(away_sb.sem, away_sb(b, 1))
                            act.activation(share[:, :, :], away[:, :, :], ACT.Exp).then_inc(share_sb.sem, 1)

                copy_h(0)
                with act.Fori(0, B - 1) as b:
                    batch(b, True)
                batch(B - 1, False)

            @block.vector
            def _(dve):
                own = Chain(dve, sem("dve_step"), 9)
                weighed = Chain(dve, s_weighed, EXPERTS)
                for t in range(NT):
                    ins = dve.tensor_tensor_reduce(squares[:, t, :], k.y[:, t, :], k.y[:, t, :], 1.0, 0.0,
                                                   ALU.mult, ALU.add, ms[:, t:t + 1])
                ins.then_inc(s_sq0, 1)
                dve.wait_ge(s_rms, 1)
                dve.wait_ge(s_init, 2)

                def scale_h(b):
                    dve.wait_ge(s_rms, 1 if isinstance(b, int) and b == 0 else 2)
                    for t in range(NT):
                        ins = dve.tensor_scalar(h[:, t, :], k.y[:, b * NT + t, :], ms[:, bass.ds(b * NT + t, 1)],
                                                None, ALU.mult)
                    ins.then_inc(h_ready.sem, 1)

                def batch(b, more):
                    own.start(b)
                    weighed.start(b)
                    dve.wait_ge(gate_ps.sem, gate_ps(b, 1))
                    own(dve.tensor_copy(logits[:, :, 0:EXPERTS],
                                        G[:, 0:NT * EXPERTS].rearrange("p (t e) -> p t e", t=NT)))
                    own.wait_apart(s_go)
                    for t in range(NT):
                        ins = dve.max(best[:, t, :], logits[:, t, 0:EXPERTS])
                    own(ins)
                    own.wait()
                    own(dve.tensor_copy(drop[:, :, 0:2], best[:, :, 0:2]))
                    dve.tensor_tensor(away[:, :, :], logits[:, :, 0:EXPERTS],
                                      best[:, :, 0:1].to_broadcast([P, NT, EXPERTS]), ALU.subtract).then_inc(away_sb.sem, 1)
                    own.wait_apart(s_go)
                    for t in range(NT):
                        ins = dve.match_replace(out=left[:, t, :], in_to_replace=drop[:, t, :],
                                                in_values=logits[:, t, :], imm_value=TAKEN)
                    own(ins)
                    own.wait()
                    own(dve.tensor_scalar(taken[:, :, :], left[:, :, 0:EXPERTS], TAKEN, None, ALU.is_equal))
                    own.wait()
                    dve.wait_ge(share_sb.sem, share_sb(b, 1))
                    own(dve.tensor_tensor(gates[:, :, :], share[:, :, :], taken[:, :, :], ALU.mult))
                    own.wait()
                    own(dve.tensor_reduce(total[:, :], gates[:, :, :], AX.X, ALU.add))
                    own.wait()
                    own(dve.reciprocal(total[:, :], total[:, :]))
                    own.wait()
                    own(dve.tensor_tensor(gates[:, :, :], gates[:, :, :],
                                          total[:, :].unsqueeze(2).to_broadcast([P, NT, EXPERTS]), ALU.mult))
                    own.wait()
                    if more:
                        scale_h(b + 1)
                    for e in range(EXPERTS):
                        dve.wait_ge(out_ps.sem, out_ps(b, e + 1))
                        if e > 0:
                            weighed.wait()
                        O = bank[2 + e % 2]
                        for t in range(NT):
                            tok = k.y[:, b * NT + t, :]
                            ins = dve.scalar_tensor_tensor(out=tok, in0=O[:, P * t:P * t + P], scalar=gates[:, t, e:e + 1],
                                                           in1=tok, op0=ALU.mult, op1=ALU.add)
                        weighed(ins)
                    weighed.wait()
                    for t in range(NT):
                        tok = k.x[:, b * NT + t, :]
                        dve.scalar_tensor_tensor(out=tok, in0=k.y[:, b * NT + t, :], scalar=0.5, in1=tok,
                                                 op0=ALU.mult, op1=ALU.add)
                    own.end()
                    weighed.end()

                scale_h(0)
                with dve.Fori(0, B - 1) as b:
                    batch(b, True)
                batch(B - 1, False)

            @block.tensor
            def _(pe):
                pe.wait_ge(k.experts_in, 64)

                def turn_h(b):
                    pe.wait_ge(h_ready.sem, h_ready(b, 1))
                    for t in range(NT):
                        ins = pe.transpose(T[:, P * t:P * t + P], h[:, t, :], k.ident[:, :])
                    ins.then_inc(hT_ps.sem, 1)

                def batch(b, more):
                    pe.wait_ge(hT_sb.sem, hT_sb(b, 1))
                    for t in range(NT):
                        ins = pe.matmul(G[:, EXPERTS * t:EXPERTS * t + EXPERTS], hT[:, P * t:P * t + P],
                                        gate_w[:, :], start=True, stop=True)
                    ins.then_inc(gate_ps.sem, 1)

                    def up(e):
                        if e >= 2:
                            pe.wait_ge(hid_sb.sem, hid_sb(b, e - 1))
                        for c in range(CH):
                            ins = pe.matmul(bank[4 + 2 * (e % 2) + c][:, :], w1[:, e, P * c:P * c + P], hT[:, :],
                                            start=True, stop=True)
                        ins.then_inc(hid_ps.sem, 1)

                    def down(e):
                        pe.wait_ge(hid_sb.sem, hid_sb(b, e + 1))
                        if not isinstance(b, int) or b > 0 or e >= 2:
                            pe.wait_ge(s_weighed, b * EXPERTS + max(e - 1, 0))
                        for t in range(NT):
                            for c in range(CH):
                                ins = pe.matmul(bank[2 + e % 2][:, P * t:P * t + P], hidden[:, e % 2, c, P * t:P * t + P],
                                                w2[:, e, c, :], start=c == 0, stop=c == CH - 1)
                        ins.then_inc(out_ps.sem, 1)

                    up(0)
                    for e in range(EXPERTS):
                        if e + 1 < EXPERTS:
                            up(e + 1)
                        if more and e == EXPERTS // 2:
                            turn_h(b + 1)
                        down(e)

                turn_h(0)
                with pe.Fori(0, B - 1) as b:
                    batch(b, True)
                batch(B - 1, False)


def rope_table():
    half = ROT // 2
    inv = (np.float32(1.0) / np.power(np.float32(10000.0), np.arange(half, dtype=np.float32)
                                      * np.float32(2.0) / np.float32(ROT))).astype(np.float32)
    ang = (np.arange(N, dtype=np.float32)[:, None] * inv).astype(np.float32)
    c, s = np.cos(ang).astype(np.float32), np.sin(ang).astype(np.float32)
    return np.ascontiguousarray(np.concatenate([c, c, s, s], axis=1))


def mosa(nc, k, name, make_rot):
    with ExitStack() as ctx:
        take = Semaphores(nc, ctx)

        def sb(n, shape, dt=F32):
            return ctx.enter_context(nc.sbuf_tensor(f"{name}_{n}", shape, dt))

        def sem(n):
            return take(f"{name}_{n}")

        def signal(n, per):
            return Signal(sem(n), per)

        E = MEXP
        PAIRS = E // 2
        TAKEN = -1.0
        router_rows, w_qkv, w_rot, w_out, rope = k.router_rows, k.w_qkv, k.w_rot, k.w_out, k.rope
        router = sb("router", [P, 32])
        stats = sb("stats", [P, TILES, 6])
        mv = sb("mv", [P, TILES, 2])
        var = sb("var", [P, TILES])
        rstd = sb("rstd", [P, TILES])
        hT = sb("hT", [P, N])
        grow = sb("grow", [P, N])
        gate = sb("gate", [P, N])
        work = sb("work", [P, 2, N])
        best = sb("best", [P, 8])
        chosen = sb("chosen", [P, N], BF16)
        chosenT = sb("chosenT", [P, NT, P], BF16)
        upto = sb("upto", [P, NT, N], BF16)
        rank = sb("rank", [P, N], BF16)
        rankT = sb("rankT", [P, NT, P])
        gate_part = sb("gate_part", [P, 3, N], BF16)
        gate_rest = sb("gate_rest", [P, 1, N])
        select = sb("select", [P, B * PAIRS, P], BF16)
        count = sb("count", [P, E, MK])
        slot = sb("slot", [P, 1])
        order_mask = sb("order_mask", [P, MK])
        onehot = sb("onehot", [P, NT, E * MK])
        h = sb("h", [P, NT, D])
        xg = sb("xg", [P, E * MK])
        turn = sb("turn", [P, E * MK])
        rot_a = sb("rot_a", [ROT, 2, E * MK])
        rot_b = sb("rot_b", [ROT, 2, E * MK])
        qr = sb("qr", [P, E * MK])
        kr = sb("kr", [P, E * MK])
        v = sb("v", [P, PAIRS, D])
        scores = sb("scores", [P, PAIRS, MK])
        top = sb("top", [P, PAIRS])
        total = sb("total", [P, PAIRS])
        probs = sb("probs", [P, PAIRS, MK])
        diag = sb("diag", [P, PAIRS, P])
        diagT = sb("diagT", [P, PAIRS, P])
        avT = sb("avT", [P, PAIRS, P])
        pre = sb("pre", [P, PAIRS, D])
        gate_sb = sb("gate_sb", [P, PAIRS, N])
        scatter = sb("scatter", [P, PAIRS, N])
        bank = k.bank

        s_made, s_made2, s_var, s_rstd = (sem(n) for n in ("made", "made2", "var_done", "rstd_done"))
        s_gate, s_go, s_parts = sem("gate_done"), sem("go"), sem("gate_parts")
        s_rps, s_rsb = sem("router_ps"), sem("router_sb")
        s_h, s_hps, s_hsb, s_logit = sem("h_ready"), sem("hT_ps"), sem("hT_sb"), sem("logit_ps")
        s_grow, s_chosen, s_cps, s_csb, s_rank, s_rkm, s_rtps, s_ranked = (sem(n) for n in (
            "grown", "chosen_done", "chosenT_ps", "chosenT_sb", "rank_ps", "rank_done", "rankT_ps", "ranked"))
        copied = signal("h_copied", 1)
        hot = signal("onehot_done", 1)
        xg_ps, xg_sb = signal("xg_ps", 1), signal("xg_sb", 1)
        tab_ps, tab_sb = signal("turn_ps", 1), signal("turn_sb", 1)
        proj_ps = signal("qk_ps", 2)
        v_ps, v_sb = signal("v_ps", 1), signal("v_sb", 1)
        rest_sb = signal("unturned_sb", 2)
        qk_sb = signal("qk_sb", 1)
        sc_ps = signal("score_ps", 1)
        away_sb = signal("away_sb", 1)
        exp_sb = signal("exp_sb", 1)
        diag_sb = signal("diag_sb", 1)
        dT_ps, dT_sb = signal("diagT_ps", 1), signal("diagT_sb", 1)
        av_ps, av_sb = signal("av_ps", 1), signal("av_sb", 1)
        pre_ps, pre_sb = signal("pre_ps", 1), signal("pre_sb", 1)
        bc_ps, g_sb, sc_sb = signal("broadcast_ps", PAIRS), signal("gate_sb_done", PAIRS), signal("scatter_sb", PAIRS)
        out_ps = signal("out_ps", 1)

        with nc.Block() as block:
            @block.sync
            def _(sp):
                sp.nop()

            @block.gpsimd
            def _(pool):
                for b in range(B):
                    own = slice(NT * b, NT * b + NT)
                    pool.wait_ge(s_var, b + 1)
                    pool.tensor_tensor(rstd[:, own], var[:, own], k.half[:, own], ALU.pow).then_inc(s_rstd, 1)
                pool.memset(upto[:, :, :], 1.0).then_inc(s_made, 1)
                pool.memset(select[:, :, :], 0.0).then_inc(s_made, 1)
                pool.memset(order_mask[:, :], 0.0).then_inc(s_made, 1)
                pool.memset(diag[:, :, :], 0.0).then_inc(s_made, 1)
                pool.iota(count[:, :, :], pattern=[[0, E], [1, MK]], base=1, channel_multiplier=0,
                          allow_small_or_imprecise_dtypes=True).then_inc(s_made, 1)
                pool.iota(slot[:, :], pattern=[[0, 1]], base=1, channel_multiplier=1,
                          allow_small_or_imprecise_dtypes=True).then_inc(s_made, 1)
                pool.wait_ge(s_made, 6)
                pool.affine_select(out=upto[:, :, :], in_=upto[:, :, :], compare_op=ALU.is_ge, fill=0.0, base=0,
                                   pattern=[[-P, NT], [1, N]], channel_multiplier=-1).then_inc(s_made2, 1)
                for e2 in range(2):
                    for b in range(B):
                        ins = pool.affine_select(out=select[:, PAIRS * b:PAIRS * b + PAIRS, MK * e2:MK * e2 + MK],
                                                 in_=select[:, PAIRS * b:PAIRS * b + PAIRS, MK * e2:MK * e2 + MK],
                                                 compare_op=ALU.not_equal, fill=1.0, base=-32 * b - e2,
                                                 pattern=[[-2, PAIRS], [0, MK]], channel_multiplier=1)
                        ins.then_inc(s_made2, 1)
                pool.affine_select(out=order_mask[:, :], in_=order_mask[:, :],
                                   compare_op=ALU.is_ge, fill=NEG, base=0, pattern=[[-1, MK]],
                                   channel_multiplier=1).then_inc(s_made2, 1)
                pool.wait_ge(s_gate, 1)
                pool.tensor_copy(gate_part[:, 0, :], gate[:, :]).then_inc(s_parts, 1)
                pool.wait_ge(s_parts, 1)
                pool.tensor_tensor(gate_rest[:, 0, :], gate[:, :], gate_part[:, 0, :], ALU.subtract).then_inc(s_parts, 1)
                pool.wait_ge(s_parts, 2)
                pool.tensor_copy(gate_part[:, 1, :], gate_rest[:, 0, :]).then_inc(s_parts, 1)
                pool.wait_ge(s_parts, 3)
                pool.tensor_tensor(gate_part[:, 2, :], gate_rest[:, 0, :], gate_part[:, 1, :],
                                   ALU.subtract).then_inc(s_parts, 1)
                if make_rot:
                    pool.wait_ge(k.mosa_in, 64)
                    for i in range(2):
                        pool.tensor_scalar(w_rot[:, :, i, 0:ROT // 2], w_qkv[:, :, D * i + ROT // 2:D * i + ROT], -1.0, None,
                                           ALU.mult).then_inc(k.rot_made, 1)
                        pool.tensor_copy(w_rot[:, :, i, ROT // 2:ROT], w_qkv[:, :, D * i:D * i + ROT // 2]
                                         ).then_inc(k.rot_made, 1)

            @block.scalar
            def _(act):
                for b in range(B):
                    act.wait_ge(s_hps, b + 1)
                    if b > 0:
                        act.wait_ge(s_logit, b)
                    act.copy(hT[:, :], bank[b % 2][:, :]).then_inc(s_hsb, 1)
                act.wait_ge(s_logit, B)
                act.activation(grow[:, :], bank[2][:, :], ACT.Exp, scale=-1.0).then_inc(s_grow, 1)

                def copy_h(b):
                    act.copy(h[:, :, :], k.y[:, bass.ds(b * NT, NT), :]).then_inc(copied.sem, 1)

                def chosen_tokens(b):
                    act.wait_ge(xg_ps.sem, xg_ps(b, 1))
                    act.copy(xg[:, :], bank[0][:, :]).then_inc(xg_sb.sem, 1)

                def chosen_turns(b):
                    act.wait_ge(tab_ps.sem, tab_ps(b, 1))
                    act.copy(turn[:, :], bank[1][:, :]).then_inc(tab_sb.sem, 1)

                def gate_copy(b, i):
                    act.wait_ge(bc_ps.sem, bc_ps(b, i + 1))
                    act.copy(gate_sb[:, i, :], bank[2 + i % 2][:, :]).then_inc(g_sb.sem, 1)

                def batch(b, more):
                    if more:
                        copy_h(b + 1)
                    for i, dst in enumerate((qr, kr)):
                        act.wait_ge(proj_ps.sem, proj_ps(b, i + 1))
                        act.copy(dst[ROT:P, :], bank[2 + i][ROT:P, :]).then_inc(rest_sb.sem, 1)
                    act.wait_ge(v_ps.sem, v_ps(b, 1))
                    act.copy(v[:, :, :].rearrange("p a d -> p (a d)"), bank[6][:, :]).then_inc(v_sb.sem, 1)
                    gate_copy(b, 0)
                    gate_copy(b, 1)
                    act.wait_ge(away_sb.sem, away_sb(b, 1))
                    act.activation(probs[:, :, :], scores[:, :, :], ACT.Exp).then_inc(exp_sb.sem, 1)
                    act.wait_ge(dT_ps.sem, dT_ps(b, 1))
                    act.copy(diagT[:, :, :].rearrange("p a d -> p (a d)"), bank[6][:, :]).then_inc(dT_sb.sem, 1)
                    gate_copy(b, 2)
                    gate_copy(b, 3)
                    act.wait_ge(av_ps.sem, av_ps(b, 1))
                    act.copy(avT[:, :, :].rearrange("p a d -> p (a d)"), bank[6][:, :]).then_inc(av_sb.sem, 1)
                    if more:
                        chosen_tokens(b + 1)
                    act.wait_ge(pre_ps.sem, pre_ps(b, 1))
                    act.copy(pre[:, :, :].rearrange("p a d -> p (a d)"), bank[3][:, :]).then_inc(pre_sb.sem, 1)
                    if more:
                        chosen_turns(b + 1)

                copy_h(0)
                chosen_tokens(0)
                chosen_turns(0)
                with act.Fori(0, B - 1) as b:
                    batch(b, True)
                batch(B - 1, False)

            @block.vector
            def _(dve):
                first = Chain(dve, sem("dve_first"), 0)
                own = Chain(dve, sem("dve_step"), 6)
                dve.memset(router[:, :], 0.0)

                def variances(b):
                    for t in range(NT * b, NT * b + NT):
                        ins = dve.bn_stats(stats[:, t, :], k.x[:, t, :])
                    first(ins)
                    first.wait()
                    for t in range(NT * b, NT * b + NT):
                        ins = dve.bn_aggr(mv[:, t, :], stats[:, t, :])
                    first(ins)
                    first.wait()
                    own = slice(NT * b, NT * b + NT)
                    dve.tensor_scalar(var[:, own], mv[:, own, 1], 1e-5, None, ALU.add).then_inc(s_var, 1)

                variances(0)
                dve.wait_ge(s_rps, 1)
                dve.tensor_copy(router[:, 0:E], bank[3][:, 0:E]).then_inc(s_rsb, 1)
                for b in range(B):
                    if b + 1 < B:
                        variances(b + 1)
                    dve.wait_ge(s_rstd, b + 1)
                    for t in range(NT * b, NT * b + NT):
                        ins = dve.tensor_scalar(k.y[:, t, :], k.x[:, t, :], mv[:, t, 0:1], rstd[:, t:t + 1],
                                                ALU.subtract, ALU.mult)
                    ins.then_inc(s_h, 1)
                dve.wait_ge(s_grow, 1)
                first(dve.tensor_scalar(grow[:, :], grow[:, :], 1.0, None, ALU.add))
                first.wait()
                dve.reciprocal(gate[:, :], grow[:, :]).then_inc(s_gate, 1)
                dve.wait_ge(s_gate, 1)
                dve.sem_inc(s_go, 1)
                for r in range(MK // 8):
                    src = gate[:, :] if r == 0 else work[:, (r - 1) % 2, :]
                    first(dve.max(best[:, :], src))
                    first.wait()
                    first(dve.match_replace(out=work[:, r % 2, :], in_to_replace=best[:, :], in_values=src,
                                            imm_value=TAKEN))
                    first.wait()
                dve.tensor_scalar(chosen[:, :], work[:, (MK // 8 - 1) % 2, :], TAKEN, None,
                                  ALU.is_equal).then_inc(s_chosen, 1)
                dve.wait_ge(s_made2, 10)
                first(dve.tensor_scalar(slot[MK:P, :], slot[MK:P, :], float(-MK), None, ALU.add))
                first(dve.tensor_copy(order_mask[MK:P, :], order_mask[0:MK, :]))
                first.wait()
                dve.wait_ge(s_cps, 1)
                dve.tensor_copy(chosenT[:, :, :].rearrange("p t r -> p (t r)"),
                                bank[0][:, 0:256].bitcast(BF16)).then_inc(s_csb, 1)
                dve.wait_ge(s_rank, 1)
                dve.wait_ge(s_chosen, 1)
                dve.tensor_tensor(rank[:, :], bank[1][:, :], chosen[:, :], ALU.mult).then_inc(s_rkm, 1)
                dve.wait_ge(s_rtps, 1)
                dve.tensor_copy(rankT[:, :, :].rearrange("p t r -> p (t r)"),
                                bank[0][:, 0:256].bitcast(BF16)).then_inc(s_ranked, 1)
                dve.wait_ge(s_ranked, 1)

                def make_onehot(b):
                    for c in range(NT):
                        ins = dve.tensor_tensor(onehot[:, c, :].rearrange("p (e j) -> p e j", e=E),
                                                rankT[:, c, bass.ds(b * 32, E)].unsqueeze(2).to_broadcast([P, E, MK]),
                                                count[:, :, :], ALU.is_equal)
                    ins.then_inc(hot.sem, 1)

                def make_scatter(b, i):
                    dve.wait_ge(g_sb.sem, g_sb(b, i + 1))
                    dve.scalar_tensor_tensor(out=scatter[:, i, :], in0=bank[4 + i % 2][:, :], scalar=slot[:, 0:1],
                                             in1=gate_sb[:, i, :], op0=ALU.is_equal, op1=ALU.mult).then_inc(sc_sb.sem, 1)

                def batch(b, more):
                    own.start(b)
                    dve.wait_ge(tab_sb.sem, tab_sb(b, 1))
                    if more:
                        make_onehot(b + 1)
                    for i, (src, dst) in enumerate(((bank[2], qr), (bank[3], kr))):
                        dve.wait_ge(rest_sb.sem, rest_sb(b, i + 1))
                        dve.tensor_tensor(rot_a[:, i, :], src[0:ROT, :], turn[0:ROT, :], ALU.mult)
                        own(dve.tensor_tensor(rot_b[:, i, :], bank[4 + i][ROT:P, :], turn[ROT:P, :], ALU.mult))
                        own.wait()
                        ins = dve.tensor_tensor(dst[0:ROT, :], rot_a[:, i, :], rot_b[:, i, :], ALU.add)
                    ins.then_inc(qk_sb.sem, 1)
                    dve.wait_ge(sc_ps.sem, sc_ps(b, 1))
                    own(dve.scalar_tensor_tensor(out=scores[:, :, :],
                                                 in0=bank[7][:, 0:PAIRS * MK].rearrange("p (a m) -> p a m", a=PAIRS),
                                                 scalar=D ** -0.5,
                                                 in1=order_mask[:, :].unsqueeze(1).to_broadcast([P, PAIRS, MK]),
                                                 op0=ALU.mult, op1=ALU.add))
                    own.wait()
                    own(dve.tensor_reduce(top[:, :], scores[:, :, :], AX.X, ALU.max))
                    own.wait()
                    dve.tensor_tensor(scores[:, :, :], scores[:, :, :], top[:, :].unsqueeze(2).to_broadcast([P, PAIRS, MK]),
                                      ALU.subtract).then_inc(away_sb.sem, 1)
                    make_scatter(b, 0)
                    dve.wait_ge(exp_sb.sem, exp_sb(b, 1))
                    own(dve.tensor_reduce(total[:, :], probs[:, :, :], AX.X, ALU.add))
                    own.wait()
                    own(dve.reciprocal(total[:, :], total[:, :]))
                    own.wait()
                    for e2 in range(2):
                        rows = slice(MK * e2, MK * e2 + MK)
                        ins = dve.tensor_tensor(diag[rows, :, MK * e2:MK * e2 + MK], probs[rows, :, :],
                                                total[rows, :].unsqueeze(2).to_broadcast([MK, PAIRS, MK]), ALU.mult)
                    ins.then_inc(diag_sb.sem, 1)
                    for i in range(1, PAIRS):
                        make_scatter(b, i)
                    dve.wait_ge(out_ps.sem, out_ps(b, 1))
                    for t in range(NT):
                        tok = k.x[:, b * NT + t, :]
                        dve.scalar_tensor_tensor(out=tok, in0=bank[7][:, P * t:P * t + P], scalar=0.5, in1=tok,
                                                 op0=ALU.mult, op1=ALU.add)
                    own.end()

                make_onehot(0)
                with dve.Fori(0, B - 1) as b:
                    batch(b, True)
                batch(B - 1, False)

            @block.tensor
            def _(pe):
                pe.wait_ge(k.mosa_in, 64)
                pe.transpose(bank[3][:, 0:E], router_rows[:, :], k.ident[0:E, 0:E]).then_inc(s_rps, 1)
                for b in range(B):
                    pe.wait_ge(s_h, b + 1)
                    if b >= 2:
                        pe.wait_ge(s_hsb, b - 1)
                    for t in range(NT):
                        ins = pe.transpose(bank[b % 2][:, P * t:P * t + P], k.y[:, NT * b + t, :], k.ident[:, :])
                    ins.then_inc(s_hps, 1)
                    if b == 0:
                        pe.wait_ge(s_rsb, 1)
                    pe.wait_ge(s_hsb, b + 1)
                    pe.matmul(bank[2][32 * b:32 * b + 32, :], router[:, :], hT[:, :], start=True,
                              stop=True).then_inc(s_logit, 1)
                pe.wait_ge(s_chosen, 1)
                for c in range(NT):
                    ins = pe.transpose(bank[0][:, 64 * c:64 * c + 64].bitcast(BF16), chosen[:, P * c:P * c + P],
                                       k.identb[:, :])
                ins.then_inc(s_cps, 1)
                pe.wait_ge(s_csb, 1)
                pe.wait_ge(s_made2, 10)
                for c in range(NT):
                    ins = pe.matmul(bank[1][:, :], chosenT[:, c, :], upto[:, c, :], start=c == 0, stop=c == NT - 1)
                ins.then_inc(s_rank, 1)
                pe.wait_ge(s_rkm, 1)
                for c in range(NT):
                    ins = pe.transpose(bank[0][:, 64 * c:64 * c + 64].bitcast(BF16), rank[:, P * c:P * c + P],
                                       k.identb[:, :])
                ins.then_inc(s_rtps, 1)
                pe.wait_ge(k.rot_made, 4)
                pe.wait_ge(s_parts, 4)

                def gather_tokens(b, chunks):
                    if 0 in chunks:
                        pe.wait_ge(copied.sem, copied(b, 1))
                        pe.wait_ge(hot.sem, hot(b, 1))
                    for c in chunks:
                        ins = pe.matmul(bank[0][:, :], h[:, c, :], onehot[:, c, :], start=c == 0, stop=c == NT - 1)
                    if c == NT - 1:
                        ins.then_inc(xg_ps.sem, 1)

                def gather_turns(b, chunks):
                    for c in chunks:
                        ins = pe.matmul(bank[1][:, :], rope[:, c, :], onehot[:, c, :], start=c == 0, stop=c == NT - 1)
                    if c == NT - 1:
                        ins.then_inc(tab_ps.sem, 1)

                def spread(b, i):
                    if i >= 2:
                        pe.wait_ge(sc_sb.sem, sc_sb(b, i - 1))
                    sel = select[:, b * PAIRS + i, :]
                    pe.matmul(bank[4 + i % 2][:, :], sel, rank[:, :], start=True, stop=True)
                    for part in range(3):
                        ins = pe.matmul(bank[2 + i % 2][:, :], sel, gate_part[:, part, :], start=part == 0, stop=part == 2)
                    ins.then_inc(bc_ps.sem, 1)

                def batch(b, more):
                    pe.wait_ge(xg_sb.sem, xg_sb(b, 1))
                    for i in range(2):
                        for e in range(E):
                            cols = slice(MK * e, MK * e + MK)
                            pe.matmul(bank[2 + i][:, cols], w_qkv[:, e, D * i:D * i + D], xg[:, cols], start=True, stop=True)
                            ins = pe.matmul(bank[4 + i][ROT:P, cols], w_rot[:, e, i, :], xg[:, cols], start=True, stop=True)
                        ins.then_inc(proj_ps.sem, 1)
                    for e in range(E):
                        half = slice(MK * (e % 2), MK * (e % 2) + MK)
                        ins = pe.matmul(bank[6][half, D * (e // 2):D * (e // 2) + D], xg[:, MK * e:MK * e + MK],
                                        w_qkv[:, e, 2 * D:3 * D], start=True, stop=True)
                    ins.then_inc(v_ps.sem, 1)
                    if more:
                        gather_tokens(b + 1, (0,))
                    pe.wait_ge(qk_sb.sem, qk_sb(b, 1))
                    for e in range(E):
                        half = slice(MK * (e % 2), MK * (e % 2) + MK)
                        cols = slice(MK * e, MK * e + MK)
                        ins = pe.matmul(bank[7][half, MK * (e // 2):MK * (e // 2) + MK], qr[:, cols], kr[:, cols],
                                        start=True, stop=True)
                    ins.then_inc(sc_ps.sem, 1)
                    spread(b, 0)
                    spread(b, 1)
                    if more:
                        gather_tokens(b + 1, (1,))
                        gather_turns(b + 1, (0, 1))
                    pe.wait_ge(diag_sb.sem, diag_sb(b, 1))
                    pe.wait_ge(v_sb.sem, v_sb(b, 1))
                    for i in range(PAIRS):
                        ins = pe.transpose(bank[6][:, P * i:P * i + P], diag[:, i, :], k.ident[:, :])
                    ins.then_inc(dT_ps.sem, 1)
                    spread(b, 2)
                    spread(b, 3)
                    pe.wait_ge(dT_sb.sem, dT_sb(b, 1))
                    for i in range(PAIRS):
                        ins = pe.matmul(bank[6][:, P * i:P * i + P], v[:, i, :], diagT[:, i, :], start=True, stop=True)
                    ins.then_inc(av_ps.sem, 1)
                    if more:
                        gather_tokens(b + 1, (2, 3))
                    pe.wait_ge(av_sb.sem, av_sb(b, 1))
                    pe.wait_ge(sc_sb.sem, sc_sb(b, PAIRS))
                    for e in range(E):
                        half = slice(MK * (e % 2), MK * (e % 2) + MK)
                        ins = pe.matmul(bank[3][half, D * (e // 2):D * (e // 2) + D],
                                        avT[:, e // 2, MK * (e % 2):MK * (e % 2) + MK], w_out[:, e, :],
                                        start=True, stop=True)
                    ins.then_inc(pre_ps.sem, 1)
                    if more:
                        gather_turns(b + 1, (2, 3))
                    pe.wait_ge(pre_sb.sem, pre_sb(b, 1))
                    for t in range(NT):
                        for i in range(PAIRS):
                            ins = pe.matmul(bank[7][:, P * t:P * t + P], scatter[:, i, P * t:P * t + P], pre[:, i, :],
                                            start=i == 0, stop=i == PAIRS - 1)
                    ins.then_inc(out_ps.sem, 1)

                pe.wait_ge(s_ranked, 1)
                gather_tokens(0, range(NT))
                gather_turns(0, range(NT))
                with pe.Fori(0, B - 1) as b:
                    batch(b, True)
                batch(B - 1, False)


def additive(nc, k, a, name="add"):
    with ExitStack() as ctx:
        take = Semaphores(nc, ctx)

        def sb(n, shape, dt=F32):
            return ctx.enter_context(nc.sbuf_tensor(f"{name}_{n}", shape, dt))

        def sem(n):
            return take(f"{name}_{n}")

        def signal(n, per):
            return Signal(sem(n), per)

        C2 = ADIM // P
        CH = HID // P
        TOKEN_SCALE = 16 ** -0.5
        W = D + 1
        SLOTS = B + 2
        z = k.y
        wqk = sb("wqk", [P, 2, ADIM])
        wp = sb("wp", [P, C2, ADIM])
        wfg = sb("wfg", [P, C2, W])
        bqkp = sb("bqkp", [P, 3, C2])
        wqk_next = sb("wqk_next", [P, 2, ADIM])
        bqkp_next = sb("bqkp_next", [P, 3, C2])
        ln_next = sb("ln_next", [P, 4])
        w1_next = sb("w1_next", [P, HID])
        w2_next = sb("w2_next", [P, CH, D])
        b1_next = sb("b1_next", [P, CH])
        b2_next = sb("b2_next", [P, D])
        bqk_rows = sb("bqk_rows", [P, 2, ADIM])
        bf_rows = sb("bf_rows", [P, D])
        w1 = sb("w1", [P, HID])
        w2 = sb("w2", [P, CH, D])
        b1 = sb("b1", [P, CH])
        b2_rows = sb("b2_rows", [P, D])
        ln = sb("ln", [P, 4])
        wpT = sb("wpT", [P, C2, ADIM])
        wqkT = sb("wqkT", [P, 2, C2, D])
        wpf = sb("wpf", [P, C2, D])
        wqfg = sb("wqfg", [P, W])
        fold_rows = sb("fold_rows", [P, W + D])
        bpf_rows = sb("bpf_rows", [P, D])
        b_hi = sb("b_hi", [P, 2 * ADIM], BF16)
        b_mid = sb("b_mid", [P, 2 * ADIM], BF16)
        b_rest = sb("b_rest", [P, 2 * ADIM])
        b_lo = sb("b_lo", [P, 2 * ADIM], BF16)
        b_sum = sb("b_sum", [P, 2 * ADIM])
        b_parts = sb("b_parts", [P, 2 * ADIM], BF16)
        row_is = sb("row_is", [P, 3])
        three = sb("three", [P, P], BF16)
        ones = sb("ones", [P, P])
        half2 = sb("half2", [P, 2, TILES])
        stats = sb("stats", [P, 2, TILES, 6])
        mv = sb("mv", [P, 2, TILES, 2])
        var = sb("var", [P, 2, TILES])
        rstd = sb("rstd", [P, 2, TILES])
        zn1 = sb("zn1", [P, TILES, D])
        zn2 = sb("zn2", [P, NT, D])
        hT1 = sb("hT1", [P, B, N])
        hT2 = sb("hT2", [P, N])
        squares = sb("squares", [P, ADIM])
        kstats = sb("kstats", [P, TILES, 6])
        kmv = sb("kmv", [P, TILES, 2])
        ss = sb("ss", [P, 2, TILES])
        inv = sb("inv", [P, 2, TILES])
        qf = sb("qf", [P, TILES, W])
        alpha = sb("alpha", [P, TILES])
        token_sums = sb("token_sums", [P, B, 2, NT])
        over = sb("over", [P, 2, B])
        inv_a = sb("inv_a", [P, B])
        u = sb("u", [P, B])
        coef = sb("coef", [P, B])
        G = sb("G", [P, C2, B])
        bkG = sb("bkG", [P, C2, B])
        wG = sb("wG", [P, C2, D])
        M_bk = sb("M_bk", [P, 2, D])
        kp4 = sb("kp4", [P, NT, D])
        hidden = sb("hidden", [P, CH, N])
        bank = k.bank
        Q, K, F, T, OUT, S = bank[0], bank[1], bank[2], bank[3], bank[6], bank[7]
        UP = [bank[4], bank[5]]

        s_w, s_rows, s_mlp = signal("w_attn", 16 * 7), signal("rows_in", 16 * 3), signal("w_mlp", 16 * 6)
        s_raw = signal("w_raw", 16 * 3)
        s_made, s_first, s_go, s_go_sp = sem("made"), sem("first"), sem("go"), sem("go_sp")
        zn1_ok, zn2_ok = signal("zn1_ready", B), signal("zn2_ready", B)
        var_ok = [signal(f"var{j}", B) for j in (1, 2)]
        rstd_ok = [signal(f"rstd{j}", B) for j in (1, 2)]
        BEFORE, TURNS = 6, 12
        t_ps, t_sb = signal("turned_ps", TURNS), signal("turned_sb", TURNS)
        in_use, mlp_in_use, w2_in_use = (signal(n, 1) for n in ("attn_in_use", "mlp_in_use", "w2_in_use"))
        bias_ok, bpf_made = signal("bias_parts", 1), signal("bpf_rows_made", 1)
        q_ps, q_sq = signal("q_ps", TILES), signal("q_sq", TILES)
        k_ps, k_sq = signal("k_ps", TILES), signal("k_sq", TILES)
        f_ps, f_sb = signal("f_ps", TILES), signal("f_sb", TILES)
        ss_ok, inv_ok = signal("ss_ready", 2 * B), signal("inv_ready", 2 * B)
        sums_ok, sums_ps = signal("sums_ready", B), signal("sums_ps", B)
        over_ok, inva_ok = signal("over_ready", B), signal("inva_ready", B)
        u_ok, g_ps, g_ok = signal("u_ready", B), signal("g_ps", B), signal("g_ready", B)
        wg_ok, m_ps, m_sb = signal("wg_ready", B), signal("m_ps", B), signal("m_sb", B)
        kp_ps, kp_read = signal("kp_ps", B), signal("kp_read", B)
        bpf_ok, b2_ok = signal("bpf_added", B), signal("b2_added", B)
        hid_ps, hid_sb = signal("hid_ps", B * CH), signal("hid_sb", B * CH)
        out_ps, out_read = signal("out_ps", B), signal("out_read", B)

        def cols(x):
            return x.rearrange("o (c p) -> p (o c)", p=P)

        def tiles(b):
            return slice(NT * b, NT * b + NT)

        normals = [("x", 0), ("x", 1), ("z", 0), ("x", 2), ("z", 1), ("x", 3), ("z", 2), ("z", 3)]
        MADE = 6

        at_first = {1: 1, 2: 2, 3: 3, 4: 4, (1, 0): 5, (1, 1): BEFORE}

        def at_next(i):
            return {what: (i + 1) * TURNS + n for what, n in
                    {1: 0, 2: 1, 3: 2, 4: 3, (1, 0): 4, (1, 1): BEFORE}.items()}

        def at_own(i, more):
            n = {(1, 1): 0, (1, 2): 1, (2, 0): 2, (1, 3): 3, (2, 1): 4, (2, 2): 5, (2, 3): 11 if more else 6}
            return {what: i * TURNS + BEFORE + m for what, m in n.items()}

        def slots(i, first, more):
            queries = {1: (i, 1), 2: (i, 2), 3: (i, 3)}
            if more:
                queries.update({5: (i + 1, 0)})
            own, later = at_own(i, more), at_next(i)
            for s in range(1, SLOTS if more else SLOTS - 1):
                after = {1: (i, 2), 2: (i, 3), 4: (i + 1, 0), 5: (i + 1, 1)}.get(s) if more or s < 3 else None
                at = None if after is None else (own if s < 3 else later)[1, after[1]]
                mlp = {1: None if first else (i - 1, 3), 2: (i, 0), 3: (i, 1), 4: (i, 2)}.get(s)
                ended = {2: None if first else (i - 1, 3), 3: (i, 0), 4: (i, 1), 5: (i, 2)}.get(s)
                if ended and not more and s > 2:
                    ended = None
                yield s, queries.get(s), after, at, mlp, ended

        def run(eng, layer, before):
            before()
            layer(0, True, True)
            with eng.Fori(0, DEPTH - 2) as n:
                layer(n + 1, False, True)
            layer(DEPTH - 1, False, False)

        with nc.Block() as block:
            @block.sync
            def _(sp):
                def raw(i):
                    one = bass.ds(i, 1)
                    for dst, src in (
                            (wp[:, :, :], a["L1_attn_Wp"][one].rearrange("o (c p) n -> p (o c) n", p=P)),
                            (wfg[:, :, 0:D], a["L1_attn_Wf"][one].rearrange("o (c p) n -> p (o c) n", p=P)),
                            (wfg[:, :, D:W], a["L1_attn_w_g"][one].rearrange("o (c p) n -> p (o c) n", p=P))):
                        sp.dma_start(dst, src, allow_slow_non_contiguous=True).then_inc(s_raw.sem, 16)

                def attn(i):
                    one = bass.ds(i, 1)
                    for dst, src in (
                            (wqk_next[:, 0, :], a["L1_attn_Wq"][one].rearrange("o p n -> p (o n)")),
                            (wqk_next[:, 1, :], a["L1_attn_Wk"][one].rearrange("o p n -> p (o n)")),
                            (bqkp_next[:, 0, :], cols(a["L1_attn_bq"][one])),
                            (bqkp_next[:, 1, :], cols(a["L1_attn_bk"][one])),
                            (bqkp_next[:, 2, :], cols(a["L1_attn_bp"][one])),
                            (ln_next[:, 0:1], cols(a["L1_attn_ln1_g"][one])),
                            (ln_next[:, 1:2], cols(a["L1_attn_ln1_b"][one]))):
                        sp.dma_start(dst, src, allow_slow_non_contiguous=True).then_inc(s_w.sem, 16)

                def mlp(i):
                    one = bass.ds(i, 1)
                    for dst, src in (
                            (ln_next[:, 2:3], cols(a["L1_attn_ln2_g"][one])),
                            (ln_next[:, 3:4], cols(a["L1_attn_ln2_b"][one])),
                            (w1_next[:, :], a["L1_attn_W1"][one].rearrange("o p n -> p (o n)")),
                            (b1_next[:, :], cols(a["L1_attn_b1"][one])),
                            (w2_next[:, :, :], a["L1_attn_W2"][one].rearrange("o (c p) n -> p (o c) n", p=P)),
                            (b2_next[:, :], a["L1_attn_b2"][one].to_broadcast([P, D]))):
                        sp.dma_start(dst, src, allow_slow_non_contiguous=True).then_inc(s_mlp.sem, 16)

                def rows(i):
                    one = bass.ds(i, 1)
                    for dst, src in (
                            (bqk_rows[:, 0, :], a["L1_attn_bq"][one].to_broadcast([P, ADIM])),
                            (bqk_rows[:, 1, :], a["L1_attn_bk"][one].to_broadcast([P, ADIM])),
                            (bf_rows[:, :], a["L1_attn_bf"][one].to_broadcast([P, D]))):
                        sp.dma_start(dst, src, allow_slow_non_contiguous=True).then_inc(s_rows.sem, 16)

                attn(0)
                raw(0)
                rows(0)
                mlp(0)
                with sp.Fori(0, DEPTH - 1) as i:
                    sp.wait_ge(t_sb.sem, t_sb(i, BEFORE))
                    sp.sem_inc(s_go_sp, 1)
                    sp.wait_ge(in_use.sem, in_use(i, 1))
                    sp.sem_inc(s_go_sp, 1)
                    sp.wait_ge(bias_ok.sem, bias_ok(i, 1))
                    sp.sem_inc(s_go_sp, 1)
                    sp.wait_ge(bpf_made.sem, bpf_made(i, 1))
                    sp.sem_inc(s_go_sp, 1)
                    attn(i + 1)
                    raw(i + 1)
                    rows(i + 1)
                    sp.wait_ge(mlp_in_use.sem, mlp_in_use(i, 1))
                    sp.sem_inc(s_go_sp, 1)
                    sp.wait_ge(w2_in_use.sem, w2_in_use(i, 1))
                    sp.sem_inc(s_go_sp, 1)
                    mlp(i + 1)
                sp.wait_ge(s_mlp.sem, s_mlp(DEPTH, 0))

            @block.gpsimd
            def _(pool):
                pool.memset(ones[:, :], 1.0).then_inc(s_made, 1)
                pool.memset(half2[:, :, :], -0.5).then_inc(s_made, 1)
                pool.memset(three[:, :], 1.0).then_inc(s_made, 1)
                pool.memset(row_is[:, :], 0.0).then_inc(s_made, 1)
                pool.wait_ge(s_made, 4)
                pool.affine_select(out=three[:, :], in_=three[:, :], compare_op=ALU.is_ge, fill=0.0, base=2,
                                   pattern=[[0, P]], channel_multiplier=-1).then_inc(s_made, 1)
                pool.affine_select(out=row_is[:, :], in_=row_is[:, :], compare_op=ALU.not_equal, fill=1.0, base=0,
                                   pattern=[[-1, 3]], channel_multiplier=1).then_inc(s_made, 1)
                for n, (_, b) in enumerate(normals):
                    pool.wait_ge(s_first, n + 1)
                    pool.tensor_tensor(rstd[:, 0, tiles(b)], var[:, 0, tiles(b)], half2[:, 0, tiles(b)],
                                       ALU.pow).then_inc(s_made, 1)

                def make_bpf(i, at):
                    pool.wait_ge(t_sb.sem, at)
                    pool.wait_ge(s_rows.sem, s_rows(i, 48))
                    pool.tensor_tensor(bpf_rows[:, :], fold_rows[:, W:W + D], bf_rows[:, :],
                                       ALU.add).then_inc(bpf_made.sem, 1)

                def rsqrt_var(i, j, b):
                    pool.wait_ge(var_ok[j].sem, var_ok[j](i, b + 1))
                    pool.tensor_tensor(rstd[:, j, tiles(b)], var[:, j, tiles(b)], half2[:, 0, tiles(b)],
                                       ALU.pow).then_inc(rstd_ok[j].sem, 1)

                def add_rows(b, rows, done):
                    tok = z[:, tiles(b), :]
                    pool.tensor_tensor(tok, tok, rows[:, :].unsqueeze(1).to_broadcast([P, NT, D]),
                                       ALU.add).then_inc(done.sem, 1)

                def with_bpf(i, b):
                    pool.wait_ge(zn1_ok.sem, zn1_ok(i, b + 1))
                    if b == 0:
                        pool.wait_ge(bpf_made.sem, bpf_made(i, 1))
                    add_rows(b, bpf_rows, bpf_ok)

                def norms(i, b):
                    for j in range(2):
                        pool.wait_ge(ss_ok.sem, ss_ok(i, 2 * b + j + 1))
                        pool.tensor_tensor(inv[:, j, tiles(b)], ss[:, j, tiles(b)], half2[:, j, tiles(b)],
                                           ALU.pow).then_inc(inv_ok.sem, 1)

                def before():
                    make_bpf(0, at_first[4])
                    with_bpf(0, 0)
                    norms(0, 0)

                def layer(i, first, more):
                    for s, now, after, at, mlp, ended in slots(i, first, more):
                        c = s - 1
                        if s == 5:
                            make_bpf(i + 1, at_next(i)[4])
                        if now:
                            with_bpf(*now)
                        if c < B:
                            pool.wait_ge(over_ok.sem, over_ok(i, c + 1))
                            pool.tensor_tensor(inv_a[:, c:c + 1], over[:, 0, c:c + 1], half2[:, 0, 0:1],
                                               ALU.pow).then_inc(inva_ok.sem, 1)
                        if ended:
                            rsqrt_var(ended[0], 0, ended[1])
                        if c < B:
                            rsqrt_var(i, 1, c)
                        if now:
                            norms(*now)
                        if c < B:
                            pool.wait_ge(zn2_ok.sem, zn2_ok(i, c + 1))
                            if c == 0:
                                pool.wait_ge(mlp_in_use.sem, mlp_in_use(i, 1))
                            add_rows(c, b2_rows, b2_ok)

                run(pool, layer, before)

            @block.scalar
            def _(act):
                def turn_out(dst, at, col):
                    act.wait_ge(t_ps.sem, at)
                    act.activation(dst, T[:, :], ACT.Identity, bias=ln[:, col + 1:col + 2],
                                   scale=ln[:, col:col + 1]).then_inc(t_sb.sem, 1)

                def fold(n, at):
                    act.wait_ge(t_ps.sem, at)
                    if n == 1:
                        act.copy(wpT[:, :, :].rearrange("p c n -> p (c n)"), T[:, :]).then_inc(t_sb.sem, 1)
                    elif n == 2:
                        act.copy(wqkT[:, :, :, :].rearrange("p s c n -> p (s c n)"), T[:, :]).then_inc(t_sb.sem, 1)
                    elif n == 3:
                        act.copy(wpf[:, :, :].rearrange("p c n -> p (c n)"), T[:, 0:C2 * D])
                        act.copy(wqfg[:, :], T[:, C2 * D:C2 * D + W]).then_inc(t_sb.sem, 1)
                    else:
                        act.copy(fold_rows[:, :], T[:, 0:W + D]).then_inc(t_sb.sem, 1)

                def use_weights(i):
                    act.wait_ge(s_w.sem, s_w(i, 112))
                    act.copy(wqk[:, :, :], wqk_next[:, :, :])
                    act.copy(bqkp[:, :, :], bqkp_next[:, :, :])
                    act.copy(ln[:, 0:2], ln_next[:, 0:2]).then_inc(in_use.sem, 1)
                    act.wait_ge(in_use.sem, in_use(i, 1))

                def use_mlp_weights(i):
                    act.wait_ge(s_mlp.sem, s_mlp(i, 96))
                    if not isinstance(i, int) or i > 0:
                        act.wait_ge(b2_ok.sem, b2_ok(i, 0))
                        act.wait_ge(hid_sb.sem, hid_sb(i, 0))
                    act.copy(w1[:, :], w1_next[:, :])
                    act.copy(b1[:, :], b1_next[:, :])
                    act.copy(b2_rows[:, :], b2_next[:, :])
                    act.copy(ln[:, 2:4], ln_next[:, 2:4]).then_inc(mlp_in_use.sem, 1)

                def use_w2(i):
                    if not isinstance(i, int) or i > 0:
                        act.wait_ge(out_ps.sem, out_ps(i, 0))
                    act.copy(w2[:, :, :], w2_next[:, :, :]).then_inc(w2_in_use.sem, 1)

                def gelu(i, m, c):
                    n = CH * m + c
                    act.wait_ge(hid_ps.sem, hid_ps(i, n + 1))
                    act.activation(hidden[:, c, :], UP[c % 2][:, :], ACT.Gelu,
                                   bias=b1[:, c:c + 1]).then_inc(hid_sb.sem, 1)

                def square(i, b, t):
                    n = NT * b + t
                    act.wait_ge(q_ps.sem, q_ps(i, n + 1))
                    if not (isinstance(i, int) and i == 0 and n == 0):
                        act.wait_ge(q_sq.sem, q_sq(i, n))
                    act.activation(squares[:, :], Q[:, 0:ADIM], ACT.Square,
                                   accum_out=ss[:, 0, n:n + 1]).then_inc(q_sq.sem, 1)

                def before():
                    for n in range(1, 5):
                        fold(n, at_first[n])
                    use_weights(0)
                    turn_out(hT1[:, 0, :], at_first[1, 0], 0)
                    for t in range(NT):
                        square(0, 0, t)
                    turn_out(hT1[:, 1, :], at_first[1, 1], 0)
                    square(0, 1, 0)

                def layer(i, first, more):
                    for s, now, after, at, mlp, ended in slots(i, first, more):
                        c = s - 1
                        has_c, folding = c < B, more and s == 4
                        if folding:
                            fold(1, at_next(i)[1])
                        if mlp:
                            gelu(*mlp, 0)
                            gelu(*mlp, 1)
                        if now:
                            square(*now, 1)
                        if mlp:
                            gelu(*mlp, 2)
                            gelu(*mlp, 3)
                        if has_c:
                            act.wait_ge(m_ps.sem, m_ps(i, c + 1))
                            act.copy(M_bk[:, :, :].rearrange("p s d -> p (s d)"), S[:, 0:2 * D]).then_inc(m_sb.sem, 1)
                        if s == 1:
                            use_mlp_weights(i)
                        if folding:
                            use_weights(i + 1)
                            fold(2, at_next(i)[2])
                        if now:
                            square(*now, 2)
                        if folding:
                            fold(3, at_next(i)[3])
                            fold(4, at_next(i)[4])
                        if after:
                            turn_out(hT1[:, after[1], :], at, 0)
                        if now:
                            square(*now, 3)
                        if after:
                            square(*after, 0)
                        if has_c:
                            if s == 1:
                                act.wait_ge(mlp_in_use.sem, mlp_in_use(i, 1))
                            turn_out(hT2[:, :], at_own(i, more)[2, c], 2)
                        if s == 1:
                            use_w2(i)
                    if not more:
                        for c in range(CH):
                            gelu(i, B - 1, c)

                run(act, layer, before)

            @block.vector
            def _(dve):
                own = Chain(dve, sem("dve_step"), 15 * B)
                LATER = 2
                first = Chain(dve, sem("dve_first"), 0)

                def normal_stats(step, j, src, which, eps, done):
                    for t in which:
                        ins = dve.bn_stats(stats[:, j, t, :], src[:, t, :])
                    step(ins)
                    step.wait_apart(s_go)
                    for t in which:
                        ins = dve.bn_aggr(mv[:, j, t, :], stats[:, j, t, :])
                    step(ins)
                    step.wait()
                    span = slice(which[0], which[-1] + 1)
                    dve.tensor_scalar(var[:, j, span], mv[:, j, span, 1], eps, None, ALU.add).then_inc(done, 1)

                def normal(j, src, dst, which, shift=0):
                    for t in which:
                        ins = dve.tensor_scalar(dst[:, t - shift, :], src[:, t, :], mv[:, j, t, 0:1],
                                                rstd[:, j, t:t + 1], ALU.subtract, ALU.mult)
                    return ins

                def statistics(kind, b):
                    own = range(NT * b, NT * b + NT)
                    if kind == "x":
                        normal_stats(first, 0, k.x, own, 1e-5, s_first)
                    else:
                        dve.wait_ge(s_made, MADE + normals.index(("x", b)) + 1)
                        first(normal(0, k.x, z, own))
                        first.wait_apart(s_go)
                        normal_stats(first, 0, z, own, 1e-6, s_first)

                for n, (kind, b) in enumerate(normals):
                    statistics(kind, b)
                    if n > 0 and normals[n - 1][0] == "z":
                        b = normals[n - 1][1]
                        dve.wait_ge(s_made, MADE + n)
                        normal(0, z, zn1, range(NT * b, NT * b + NT)).then_inc(zn1_ok.sem, 1)
                dve.wait_ge(s_made, MADE + len(normals))
                normal(0, z, zn1, range(NT * (B - 1), TILES)).then_inc(zn1_ok.sem, 1)

                split = Chain(dve, sem("split_step"), 6)

                def bias_parts(i):
                    split.start(i)
                    dve.wait_ge(s_rows.sem, s_rows(i, 48))
                    rows = bqk_rows[:, :, :].rearrange("p s n -> p (s n)")
                    split(dve.tensor_copy(b_hi[:, :], rows))
                    split.wait()
                    split(dve.tensor_tensor(b_rest[:, :], rows, b_hi[:, :], ALU.subtract))
                    split.wait()
                    split(dve.tensor_copy(b_mid[:, :], b_rest[:, :]))
                    split.wait()
                    split(dve.tensor_tensor(b_lo[:, :], b_rest[:, :], b_mid[:, :], ALU.subtract))
                    split(dve.tensor_scalar(b_sum[:, :], b_hi[:, :], row_is[:, 0:1], None, ALU.mult))
                    split.wait()
                    split(dve.scalar_tensor_tensor(out=b_rest[:, :], in0=b_mid[:, :], scalar=row_is[:, 1:2],
                                                   in1=b_sum[:, :], op0=ALU.mult, op1=ALU.add))
                    split.wait()
                    dve.scalar_tensor_tensor(out=b_parts[:, :], in0=b_lo[:, :], scalar=row_is[:, 2:3],
                                             in1=b_rest[:, :], op0=ALU.mult, op1=ALU.add).then_inc(bias_ok.sem, 1)
                    split.end()

                def tile_out(i, b, t, at=None):
                    n = NT * b + t
                    if n == 0:
                        dve.wait_ge(t_sb.sem, at)
                        dve.wait_ge(in_use.sem, in_use(i, 1))
                    dve.wait_ge(k_ps.sem, k_ps(i, n + 1))
                    dve.bn_stats(kstats[:, n, :], K[:, 0:ADIM]).then_inc(k_sq.sem, 1)
                    dve.wait_ge(f_ps.sem, f_ps(i, n + 1))
                    dve.tensor_tensor(qf[:, n, :], F[:, 0:W], fold_rows[:, 0:W], ALU.add).then_inc(f_sb.sem, 1)

                def norms(own, i, b):
                    ts = tiles(b)
                    dve.wait_ge(q_sq.sem, q_sq(i, NT * (b + 1)))
                    dve.tensor_scalar(ss[:, 0, ts], ss[:, 0, ts], 1e-24, None, ALU.max).then_inc(ss_ok.sem, 1)
                    dve.wait_ge(k_sq.sem, k_sq(i, NT * (b + 1)))
                    dve.sem_inc(s_go, 1)
                    for t in range(NT * b, NT * b + NT):
                        ins = dve.bn_aggr(kmv[:, t, :], kstats[:, t, :])
                    own(ins)
                    own.wait()
                    own(dve.tensor_tensor(ss[:, 1, ts], kmv[:, ts, 0], kmv[:, ts, 0], ALU.mult))
                    own.wait()
                    own(dve.tensor_tensor(ss[:, 1, ts], ss[:, 1, ts], kmv[:, ts, 1], ALU.add))
                    own.wait()
                    own(dve.tensor_scalar(ss[:, 1, ts], ss[:, 1, ts], float(ADIM), None, ALU.mult))
                    own.wait()
                    dve.tensor_scalar(ss[:, 1, ts], ss[:, 1, ts], 1e-24, None, ALU.max).then_inc(ss_ok.sem, 1)

                def alphas(own, i, b):
                    ts = tiles(b)
                    dve.wait_ge(inv_ok.sem, inv_ok(i, 2 * b + 1))
                    dve.wait_ge(f_sb.sem, f_sb(i, NT * (b + 1)))
                    own(dve.scalar_tensor_tensor(out=alpha[:, ts], in0=qf[:, ts, D], scalar=TOKEN_SCALE,
                                                 in1=inv[:, 0, ts], op0=ALU.mult, op1=ALU.mult))
                    own.wait()
                    dve.tensor_tensor(token_sums[:, b, 0, :], alpha[:, ts], alpha[:, ts], ALU.mult)
                    dve.tensor_tensor(token_sums[:, b, 1, :], alpha[:, ts], inv[:, 0, ts], ALU.mult).then_inc(sums_ok.sem, 1)

                def summed(i, b):
                    one = slice(b, b + 1)
                    dve.wait_ge(sums_ps.sem, sums_ps(i, b + 1))
                    own(dve.tensor_reduce(over[:, :, one], S[:, 0:2 * NT].rearrange("p (s t) -> p s t", s=2).unsqueeze(2),
                                          AX.X, ALU.add))
                    own.wait()
                    dve.tensor_scalar(over[:, 0, one], over[:, 0, one], 1e-24, None, ALU.max).then_inc(over_ok.sem, 1)
                    own(dve.tensor_scalar(u[:, one], S[:, 64:65], ln[:, 0:1], None, ALU.mult))
                    own.wait()
                    own(dve.scalar_tensor_tensor(out=coef[:, one], in0=over[:, 1, one], scalar=ln[:, 1:2], in1=u[:, one],
                                                 op0=ALU.mult, op1=ALU.add))
                    own.wait()
                    dve.wait_ge(inva_ok.sem, inva_ok(i, b + 1))
                    own(dve.tensor_tensor(u[:, one], coef[:, one], inv_a[:, one], ALU.mult))
                    own.wait()
                    dve.tensor_tensor(coef[:, one], over[:, 1, one], inv_a[:, one], ALU.mult).then_inc(u_ok.sem, 1)

                def global_vector(i, b):
                    one = slice(b, b + 1)
                    dve.wait_ge(g_ps.sem, g_ps(i, b + 1))
                    dve.wait_ge(u_ok.sem, u_ok(i, b + 1))
                    for c in range(C2):
                        ins = dve.scalar_tensor_tensor(out=G[:, c, one], in0=coef[:, one], scalar=bqkp[:, 0, c:c + 1],
                                                       in1=S[:, c:c + 1], op0=ALU.mult, op1=ALU.add)
                    ins.then_inc(g_ok.sem, 1)
                    dve.wait_ge(g_ok.sem, g_ok(i, b + 1))
                    for c in range(C2):
                        dve.tensor_scalar(wG[:, c, :], wpf[:, c, :], G[:, c, one], None, ALU.mult)
                        ins = dve.tensor_scalar(bkG[:, c, one], G[:, c, one], bqkp[:, 1, c:c + 1], None, ALU.mult)
                    ins.then_inc(wg_ok.sem, 1)

                def add_q(i, b):
                    dve.wait_ge(bpf_ok.sem, bpf_ok(i, b + 1))
                    for t in range(NT * b, NT * b + NT):
                        ins = dve.scalar_tensor_tensor(out=z[:, t, :], in0=qf[:, t, 0:D], scalar=inv[:, 0, t:t + 1],
                                                       in1=z[:, t, :], op0=ALU.mult, op1=ALU.add)
                    own(ins)

                def add_k(i, b):
                    dve.wait_ge(inv_ok.sem, inv_ok(i, 2 * b + 2))
                    dve.wait_ge(kp_ps.sem, kp_ps(i, b + 1))
                    dve.tensor_tensor(kp4[:, :, :], S[:, :].rearrange("p (t d) -> p t d", t=NT),
                                      M_bk[:, 1, :].unsqueeze(1).to_broadcast([P, NT, D]), ALU.add
                                      ).then_inc(kp_read.sem, 1)
                    dve.wait_ge(kp_read.sem, kp_read(i, b + 1))
                    own.wait()
                    for t in range(NT):
                        tok = z[:, NT * b + t, :]
                        ins = dve.scalar_tensor_tensor(out=tok, in0=kp4[:, t, :], scalar=inv[:, 1, NT * b + t:NT * b + t + 1],
                                                       in1=tok, op0=ALU.mult, op1=ALU.add)
                    own(ins)
                    own.wait_apart(s_go)
                    normal_stats(own, 1, z, range(NT * b, NT * b + NT), 1e-6, var_ok[1].sem)

                def ln1_stats(i, b):
                    dve.wait_ge(out_read.sem, out_read(i, b + 1))
                    dve.sem_inc(s_go, 1)
                    normal_stats(own, 0, z, range(NT * b, NT * b + NT), 1e-6, var_ok[0].sem)

                def ln1(i, b):
                    dve.wait_ge(rstd_ok[0].sem, rstd_ok[0](i, b + 1))
                    normal(0, z, zn1, range(NT * b, NT * b + NT)).then_inc(zn1_ok.sem, 1)

                def before():
                    bias_parts(0)
                    for t in range(NT):
                        tile_out(0, 0, t, at_first[4])
                    norms(first, 0, 0)
                    tile_out(0, 1, 0)
                    alphas(first, 0, 0)

                def end_mlp(i, m):
                    dve.wait_ge(out_ps.sem, out_ps(i, m + 1))
                    dve.wait_ge(b2_ok.sem, b2_ok(i, m + 1))
                    tok = z[:, tiles(m), :]
                    dve.tensor_tensor(tok, OUT[:, :].rearrange("p (t d) -> p t d", t=NT), tok,
                                      ALU.add).then_inc(out_read.sem, 1)

                def layer(i, first, more):
                    own.start(i)
                    own.n = 0 if first else -LATER
                    for s, now, after, at, mlp, ended in slots(i, first, more):
                        c = s - 1
                        has_c = c < B
                        if has_c:
                            summed(i, c)
                            global_vector(i, c)
                        if s == 4 and more:
                            bias_parts(i + 1)
                        if now:
                            tile_out(*now, 1)
                        if ended:
                            ln1_stats(*ended)
                        if has_c:
                            add_q(i, c)
                        if ended:
                            ln1(*ended)
                        if now:
                            tile_out(*now, 2)
                        if has_c:
                            add_k(i, c)
                        if now:
                            tile_out(*now, 3)
                            norms(own, *now)
                        if has_c:
                            dve.wait_ge(rstd_ok[1].sem, rstd_ok[1](i, c + 1))
                            normal(1, z, zn2, range(NT * c, NT * c + NT), NT * c).then_inc(zn2_ok.sem, 1)
                        if after:
                            tile_out(*after, 0, at_next(i)[4])
                        if now:
                            alphas(own, *now)
                        if mlp:
                            end_mlp(*mlp)
                    if more:
                        assert own.n == own.per - LATER
                    else:
                        end_mlp(i, B - 1)
                        dve.wait_ge(out_read.sem, out_read(i, B))
                        dve.tensor_tensor(k.x[:, :, :], k.x[:, :, :], z[:, :, :], ALU.add)

                run(dve, layer, before)

            @block.tensor
            def _(pe):
                def wait_t_free(at):
                    if not isinstance(at, int) or at > 1:
                        pe.wait_ge(t_sb.sem, at - 1)

                def fold(i, n, at):
                    if n == 1:
                        pe.wait_ge(s_w.sem, s_w(i, 112))
                        pe.wait_ge(s_raw.sem, s_raw(i, 48))
                    wait_t_free(at)
                    if n == 1:
                        for m in range(C2):
                            for c in range(C2):
                                ins = pe.transpose(T[:, ADIM * m + P * c:ADIM * m + P * c + P],
                                                   wp[:, c, P * m:P * m + P], k.ident[:, :])
                    elif n == 2:
                        for s in range(2):
                            for c in range(C2):
                                ins = pe.transpose(T[:, ADIM * s + P * c:ADIM * s + P * c + P],
                                                   wqk_next[:, s, P * c:P * c + P], k.ident[:, :])
                    elif n == 3:
                        for c in range(C2):
                            for m in range(C2):
                                pe.matmul(T[:, D * c:D * c + D], wpT[:, m, P * c:P * c + P], wfg[:, m, 0:D],
                                          start=m == 0, stop=m == C2 - 1)
                        for c in range(C2):
                            ins = pe.matmul(T[:, C2 * D:C2 * D + W], wqkT[:, 0, c, :], wfg[:, c, :],
                                            start=c == 0, stop=c == C2 - 1)
                    else:
                        for c in range(C2):
                            pe.matmul(T[:, 0:W], bqkp_next[:, 0, c:c + 1].to_broadcast([P, P]), wfg[:, c, :],
                                      start=c == 0, stop=c == C2 - 1)
                        for c in range(C2):
                            ins = pe.matmul(T[:, W:W + D], bqkp_next[:, 2, c:c + 1].to_broadcast([P, P]), wfg[:, c, 0:D],
                                            start=c == 0, stop=c == C2 - 1)
                    ins.then_inc(t_ps.sem, 1)

                def turn(i, kind, b, at):
                    if kind == 1:
                        pe.wait_ge(zn1_ok.sem, zn1_ok(i, b + 1))
                    else:
                        pe.wait_ge(zn2_ok.sem, zn2_ok(i, b + 1))
                    wait_t_free(at)
                    for t in range(NT):
                        src = zn1[:, NT * b + t, :] if kind == 1 else zn2[:, t, :]
                        ins = pe.transpose(T[:, P * t:P * t + P], src, k.ident[:, :])
                    ins.then_inc(t_ps.sem, 1)

                def tile(i, b, t, at=None):
                    n = NT * b + t
                    if n == 0:
                        pe.wait_ge(bias_ok.sem, bias_ok(i, 1))
                        pe.wait_ge(in_use.sem, in_use(i, 1))
                    if t == 0:
                        pe.wait_ge(t_sb.sem, at)
                    lhs = hT1[:, b, P * t:P * t + P]
                    no_wait = isinstance(i, int) and i == 0 and n == 0
                    for s, out, ps, read in ((0, Q, q_ps, q_sq), (1, K, k_ps, k_sq)):
                        if not no_wait:
                            pe.wait_ge(read.sem, read(i, n))
                        pe.matmul(out[:, 0:ADIM], lhs, wqk[:, s, :], start=True, stop=False)
                        pe.matmul(out[:, 0:ADIM], three[:, :], b_parts[:, ADIM * s:ADIM * s + ADIM], start=False,
                                  stop=True).then_inc(ps.sem, 1)
                    if not no_wait:
                        pe.wait_ge(f_sb.sem, f_sb(i, n))
                    pe.matmul(F[:, 0:W], lhs, wqfg[:, :], start=True, stop=True).then_inc(f_ps.sem, 1)

                def sums(i, b):
                    pe.wait_ge(sums_ok.sem, sums_ok(i, b + 1))
                    if not (isinstance(i, int) and i == 0 and b == 0):
                        pe.wait_ge(kp_read.sem, kp_read(i, b))
                    pe.matmul(S[:, 0:2 * NT], ones[:, :], token_sums[:, b, :, :].rearrange("p s t -> p (s t)"),
                              start=True, stop=True)
                    for t in range(NT):
                        ins = pe.matmul(S[:, 64:65], zn1[:, NT * b + t, :], token_sums[:, b, 1, t:t + 1],
                                        start=t == 0, stop=t == NT - 1)
                    ins.then_inc(sums_ps.sem, 1)

                def g_product(i, b):
                    pe.wait_ge(u_ok.sem, u_ok(i, b + 1))
                    for c in range(C2):
                        ins = pe.matmul(S[:, c:c + 1], wqk[:, 0, P * c:P * c + P], u[:, b:b + 1],
                                        start=True, stop=True)
                    ins.then_inc(g_ps.sem, 1)

                def m_product(i, b):
                    pe.wait_ge(wg_ok.sem, wg_ok(i, b + 1))
                    for c in range(C2):
                        pe.matmul(S[:, 0:D], wqkT[:, 1, c, :], wG[:, c, :], start=c == 0, stop=c == C2 - 1)
                    for c in range(C2):
                        ins = pe.matmul(S[:, D:2 * D], bkG[:, c, b:b + 1].to_broadcast([P, P]), wpf[:, c, :],
                                        start=c == 0, stop=c == C2 - 1)
                    ins.then_inc(m_ps.sem, 1)

                def k_product(i, b):
                    pe.wait_ge(m_sb.sem, m_sb(i, b + 1))
                    for t in range(NT):
                        ins = pe.matmul(S[:, P * t:P * t + P], hT1[:, b, P * t:P * t + P], M_bk[:, 0, :],
                                        start=True, stop=True)
                    ins.then_inc(kp_ps.sem, 1)

                def up(i, m, c, at):
                    if m == 0 and c == 0:
                        pe.wait_ge(mlp_in_use.sem, mlp_in_use(i, 1))
                    if c == 0:
                        pe.wait_ge(t_sb.sem, at)
                    n = CH * m + c
                    if not (isinstance(i, int) and i == 0 and n < 2):
                        pe.wait_ge(hid_sb.sem, hid_sb(i, max(n - 1, 0)))
                    pe.matmul(UP[c % 2][:, :], w1[:, P * c:P * c + P], hT2[:, :], start=True,
                              stop=True).then_inc(hid_ps.sem, 1)

                def down(i, m, t):
                    if t == 0:
                        if m == 0:
                            pe.wait_ge(w2_in_use.sem, w2_in_use(i, 1))
                        pe.wait_ge(hid_sb.sem, hid_sb(i, CH * (m + 1)))
                        if not (isinstance(i, int) and i == 0 and m == 0):
                            pe.wait_ge(out_read.sem, out_read(i, m))
                    for c in range(CH):
                        ins = pe.matmul(OUT[:, P * t:P * t + P], hidden[:, c, P * t:P * t + P], w2[:, c, :],
                                        start=c == 0, stop=c == CH - 1)
                    if t == NT - 1:
                        ins.then_inc(out_ps.sem, 1)

                def before():
                    for n in range(1, 5):
                        fold(0, n, at_first[n])
                    turn(0, 1, 0, at_first[1, 0])
                    for t in range(NT):
                        tile(0, 0, t, at_first[1, 0])
                    turn(0, 1, 1, at_first[1, 1])
                    tile(0, 1, 0, at_first[1, 1])

                def layer(i, first, more):
                    own, later = at_own(i, more), at_next(i)
                    for s, now, after, at, mlp, ended in slots(i, first, more):
                        c = s - 1
                        has_c, folding = c < B, more and s == 4
                        h2 = None if mlp is None else at_own(mlp[0], True)[2, 3] if s == 1 else own[2, mlp[1]]
                        if has_c:
                            sums(i, c)
                        if folding:
                            fold(i + 1, 1, later[1])
                        if mlp:
                            up(*mlp, 0, h2)
                            up(*mlp, 1, h2)
                        if has_c:
                            g_product(i, c)
                        if now:
                            tile(*now, 1)
                        if mlp:
                            up(*mlp, 2, h2)
                            up(*mlp, 3, h2)
                        if has_c:
                            m_product(i, c)
                        if folding:
                            fold(i + 1, 2, later[2])
                        if now:
                            tile(*now, 2)
                        if mlp:
                            down(*mlp, 0)
                        if has_c:
                            k_product(i, c)
                        if folding:
                            fold(i + 1, 3, later[3])
                        if mlp:
                            down(*mlp, 1)
                        if folding:
                            fold(i + 1, 4, later[4])
                        if after:
                            turn(after[0], 1, after[1], at)
                        if now:
                            tile(*now, 3)
                        if mlp:
                            down(*mlp, 2)
                            down(*mlp, 3)
                        if after:
                            tile(*after, 0, at)
                        if has_c:
                            turn(i, 2, c, own[2, c])
                    if not more:
                        for c in range(CH):
                            up(i, B - 1, c, own[2, B - 1])
                        for t in range(NT):
                            down(i, B - 1, t)

                pe.wait_ge(s_made, 6)
                run(pe, layer, before)


def whole(nc, k, a):
    attention(nc, k, "mla1", True)
    experts(nc, k, a, "moe1")
    attention(nc, k, "att", False)
    attention(nc, k, "mla2", True)
    experts(nc, k, a, "moe2")
    mosa(nc, k, "mosa1", True)
    additive(nc, k, a)
    mosa(nc, k, "mosa2", False)


def macaron_kernel(nc, out, **a):
    with ExitStack() as ctx:
        k = Kernel()
        open_buffers(nc, ctx, k)
        setup(nc, k, a)
        whole(nc, k, a)
        stored = ctx.enter_context(nc.semaphore("stored"))
        with nc.Block() as block:
            @block.sync
            def _(sp):
                sp.dma_start(out.rearrange("b (t p) d -> p (b t) d", p=P), k.x[:, :, :]).then_inc(stored, 16)
                sp.wait_ge(stored, 16)


_INS = ["L0_attn_x", "L0_attn_w_qkv", "L0_attn_w_proj", "L0_attn_b_proj", "L0_ffn_g1", "L0_ffn_Wq", "L0_ffn_Wdkv",
        "L0_ffn_Wuk", "L0_ffn_Wuv", "L0_ffn_Wo", "L0_ffn_g2", "L0_ffn_gate_w", "L0_ffn_w1", "L0_ffn_w2",
        "L1_attn_ln1_g", "L1_attn_ln1_b", "L1_attn_Wq", "L1_attn_bq", "L1_attn_Wk", "L1_attn_bk", "L1_attn_w_g",
        "L1_attn_Wp", "L1_attn_bp", "L1_attn_Wf", "L1_attn_bf", "L1_attn_ln2_g", "L1_attn_ln2_b", "L1_attn_W1",
        "L1_attn_b1", "L1_attn_W2", "L1_attn_b2", "L1_ffn_Wr", "L1_ffn_Wqkv", "L1_ffn_Wo"]


def kernel(**inputs):
    import concourse.bacc as _bacc
    from concourse.bass_utils import run_bass_kernel_spmd as _run

    nc = _bacc.Bacc("TRN2", target_bir_lowering=False, num_devices=1)
    arrays, args = {}, {}
    for name in _INS + ["rope"]:
        arr = np.ascontiguousarray(rope_table() if name == "rope" else inputs[name])
        arrays[f"in_{name}"] = arr
        args[name] = nc.dram_tensor(f"in_{name}", arr.shape, mybir.dt.from_np(arr.dtype), kind="ExternalInput").ap()
    out = nc.dram_tensor("out_0", (B, N, D), F32, kind="ExternalOutput").ap()
    macaron_kernel(nc, out, **args)
    r = _run(nc, [arrays], core_ids=[0])
    return r.results[0]["out_0"]
```
